# Optimizing a Trainium2 kernel written in Bass

```python
import numpy as np
import jax
import jax.numpy as jnp

def _softmax(x, axis=-1):
    return jax.nn.softmax(x, axis=axis)

def _gelu(x):
    return jax.nn.gelu(x, approximate=True)

def _silu(x):
    return jax.nn.silu(x)

def _sigmoid(x):
    return jax.nn.sigmoid(x)

def _layernorm(x, axis=-1, eps=1e-05):
    m = jnp.mean(x, axis=axis, keepdims=True)
    v = jnp.var(x, axis=axis, keepdims=True)
    return (x - m) / jnp.sqrt(v + eps)

def _scatter_add(tgt, idx, src, axis=0):
    return tgt.at[idx].add(src)

def _segment_sum(src, seg, n):
    return jax.ops.segment_sum(src, seg, n)
kernel_name = 'mk_adaln_d1_jaxref_r4_0abbfa'

def setup_inputs(seed: int=0):
    np.random.seed(seed)
    _w = jnp.asarray

    def _L0_attn_setup():
        import math
        import jax, jax.numpy as jnp
        import numpy as np
        EMB = 256
        HEADS = 16
        HEAD_DIM = EMB // HEADS

        def _srms_norm(x, eps=1e-12):
            dtype = x.dtype
            xf = x.astype(jnp.float32)
            scale = 1.0 / math.sqrt(x.shape[-1])
            n = jnp.linalg.norm(xf * scale, axis=-1, keepdims=True)
            return (xf / jnp.maximum(n, eps)).astype(dtype)
        key = jax.random.key(seed)
        ks = jax.random.split(key, 6)
        b, l = (4, 1024)
        x = jax.random.normal(ks[0], (b, l, EMB), dtype=jnp.float32)
        std = math.sqrt(2.0 / (EMB + EMB))
        Wq = jax.random.normal(ks[1], (EMB, EMB), dtype=jnp.float32) * std
        Wk = jax.random.normal(ks[2], (EMB, EMB), dtype=jnp.float32) * std
        Wv = jax.random.normal(ks[3], (EMB, EMB), dtype=jnp.float32) * std
        Wu = jax.random.normal(ks[4], (EMB, EMB), dtype=jnp.float32) * std
        Wo = jax.random.normal(ks[5], (EMB, EMB), dtype=jnp.float32) * std
        return {'x': x, 'Wq': Wq, 'Wk': Wk, 'Wv': Wv, 'Wu': Wu, 'Wo': Wo}
    _L0_attn_in = _L0_attn_setup()

    def _L0_ffn_setup():
        import jax, jax.numpy as jnp
        import numpy as np
        key = jax.random.key(seed)
        k1, k2, k3, k4 = jax.random.split(key, 4)
        B, T, M = (4, 512, 256)
        E, F = (16, 1024)
        x = jax.random.normal(k1, (B, T, M), dtype=jnp.float32) * 0.02
        Wg = jax.random.normal(k2, (M, E), dtype=jnp.float32) * 0.02
        w1 = jax.random.normal(k3, (E, M, F), dtype=jnp.float32) * 0.02
        w2 = jax.random.normal(k4, (E, F, M), dtype=jnp.float32) * 0.02
        return {'x': x, 'Wg': Wg, 'w1': w1, 'w2': w2}
    _L0_ffn_in = _L0_ffn_setup()
    _L0_c = _w((lambda *s: np.random.randn(*s).astype(np.float32) * 0.05)(4, 256))
    _L0_wmod = _w((lambda *s: np.random.randn(*s).astype(np.float32) * 0.05)(256, 6 * 256) * 256 ** (-0.5))
    _d = {'L0_attn_x': _L0_attn_in['x'], 'L0_attn_Wq': _L0_attn_in['Wq'], 'L0_attn_Wk': _L0_attn_in['Wk'], 'L0_attn_Wv': _L0_attn_in['Wv'], 'L0_attn_Wu': _L0_attn_in['Wu'], 'L0_attn_Wo': _L0_attn_in['Wo'], 'L0_ffn_Wg': _L0_ffn_in['Wg'], 'L0_ffn_w1': _L0_ffn_in['w1'], 'L0_ffn_w2': _L0_ffn_in['w2'], 'L0_c': _L0_c, 'L0_wmod': _L0_wmod}
    _x0 = _d['L0_attn_x']
    _d['L0_attn_x'] = jax.random.normal(jax.random.fold_in(jax.random.key(seed), 1), (4, 2048, 256), dtype=_x0.dtype)
    del _x0
    return _d

def reference(L0_attn_x, L0_attn_Wq, L0_attn_Wk, L0_attn_Wv, L0_attn_Wu, L0_attn_Wo, L0_ffn_Wg, L0_ffn_w1, L0_ffn_w2, L0_c, L0_wmod):

    def _L0_attn_ref(x, Wq, Wk, Wv, Wu, Wo):
        import math
        import jax, jax.numpy as jnp
        import numpy as np
        EMB = 256
        HEADS = 16
        HEAD_DIM = EMB // HEADS

        def _srms_norm(x, eps=1e-12):
            dtype = x.dtype
            xf = x.astype(jnp.float32)
            scale = 1.0 / math.sqrt(x.shape[-1])
            n = jnp.linalg.norm(xf * scale, axis=-1, keepdims=True)
            return (xf / jnp.maximum(n, eps)).astype(dtype)
        b, l, d = x.shape
        h, hd = (HEADS, HEAD_DIM)
        scale = math.sqrt(hd)

        def proj(W):
            return jnp.einsum('bld,ed->ble', x, W).reshape(b, l, h, hd).transpose(0, 2, 1, 3)
        q = jax.nn.relu(proj(Wq)) / scale
        k = jax.nn.relu(proj(Wk)) / scale
        v = proj(Wv)
        u = jax.nn.silu(proj(Wu))
        kv = jnp.einsum('bhlk,bhlv->bhkv', k, v)
        out = jnp.einsum('bhlk,bhkv->bhlv', q, kv)
        out = _srms_norm(out) * u
        out = out.transpose(0, 2, 1, 3).reshape(b, l, d)
        return jnp.einsum('bld,ed->ble', out, Wo)

    def _L0_ffn_ref(x, Wg, w1, w2):
        import jax, jax.numpy as jnp
        import numpy as np
        d = x.shape[-1]
        xr = x.reshape(-1, d)
        S = xr.shape[0]
        E = Wg.shape[1]
        C = (S + E - 1) // E
        gate = jax.nn.softmax(xr @ Wg, axis=-1)
        idx = jnp.argmax(gate, axis=1)
        gates_s = jnp.take_along_axis(gate, idx[:, None], axis=1)[:, 0]
        onehot = jax.nn.one_hot(idx, E, dtype=jnp.int32)
        loc = jnp.sum((jnp.cumsum(onehot, axis=0) - 1) * onehot, axis=1)
        valid = loc < C
        loc_pad = jnp.minimum(loc, C)
        dispatched = jnp.zeros((E, C + 1, d), dtype=x.dtype).at[idx, loc_pad].set(xr)
        dispatched = dispatched[:, :C]
        h = jax.nn.relu(jnp.einsum('ecm,emf->ecf', dispatched, w1))
        expert_out = jnp.einsum('ecf,efm->ecm', h, w2)
        gathered = expert_out[idx, jnp.minimum(loc, C - 1)]
        combined = gathered * (gates_s * valid.astype(x.dtype))[:, None]
        return combined.reshape(x.shape)
    x = L0_attn_x
    mod = (_silu(L0_c) @ L0_wmod).reshape(L0_c.shape[0], 6, 1, -1)
    sa, ca, ga, sb, cb, gb = (mod[:, 0], mod[:, 1], mod[:, 2], mod[:, 3], mod[:, 4], mod[:, 5])
    ga = (2 * (ga >= 0) - 1) * jnp.maximum(jnp.abs(ga), 0.25)
    gb = (2 * (gb >= 0) - 1) * jnp.maximum(jnp.abs(gb), 0.25)
    h = _layernorm(x, axis=-1) * (1 + ca) + sa
    x = x + ga * _L0_attn_ref(h, L0_attn_Wq, L0_attn_Wk, L0_attn_Wv, L0_attn_Wu, L0_attn_Wo)
    h = _layernorm(x, axis=-1) * (1 + cb) + sb
    x = x + gb * _L0_ffn_ref(h, L0_ffn_Wg, L0_ffn_w1, L0_ffn_w2)
    return x

_drawn_inputs = setup_inputs


def setup_inputs(seed=0):
    import zlib

    import numpy as np

    out = dict(_drawn_inputs(seed))
    spreads = {}
    factors = {'L0_ffn_Wg': 8.0, 'L0_ffn_w1': 8.0, 'L0_ffn_w2': 8.0}
    for name, (base, spread) in spreads.items():
        noise = np.random.default_rng([zlib.crc32(name.encode()), seed]).standard_normal(out[name].shape)
        drawn = base * np.exp(spread * noise) if base else spread * noise
        out[name] = jnp.asarray(drawn.astype(out[name].dtype))
    for name, factor in factors.items():
        out[name] = (out[name] * factor).astype(out[name].dtype)
    return out
```

```python
from contextlib import ExitStack

import concourse.bass as bass
from concourse import mybir

ALU = mybir.AluOpType
ACT = mybir.ActivationFunctionType
AX = mybir.AxisListType
F32 = mybir.dt.float32
F32R = mybir.dt.float32r
BF16 = mybir.dt.bfloat16
U32 = mybir.dt.uint32

P = 128
START = 2


def n(count):
    return count + START


def adaln_block_kernel(nc, x, w_kvuq, w_o, w_gate, w_experts, c_t, w_mod, out):
    NBLK, _, XW = x.shape
    D = w_o.shape[2]
    H = D // P
    T = XW // D
    BLK = T * P
    NB = c_t.shape[2]
    PER = NBLK // NB
    E = w_gate.shape[2]
    EW = w_experts.shape[2]
    F = EW // (2 * H)
    NF = F // P
    CAP = (NBLK * BLK + E - 1) // E
    HEAD = 16
    NH = D // HEAD
    ROW = 2 * D + 8
    GATE0, TOKEN = 2 * D, 2 * D + NB
    FAR = 65536.0
    LN_EPS, RMS_FLOOR = 1e-5, 1e-12
    assert CAP == BLK and H == 2 and T == 4 and PER == 4 and D % HEAD == 0

    dispatched = nc.dram_tensor("dispatched_dram", [E * CAP, ROW], F32, kind="Internal").ap()
    slots = dispatched.rearrange("(e p t) w -> e p (t w)", p=P, t=T)
    out_blocks = out.rearrange("(i p t) d -> i p (t d)", p=P, t=T)

    with ExitStack() as ctx:
        def sem(name):
            return ctx.enter_context(nc.semaphore(name))

        bank = [ctx.enter_context(nc.psum_tensor(f"bank{i}", [P, 512], F32)) for i in range(8)]
        X = bank[0:2]
        KV = bank[2:4]
        UB, KVSUM = bank[4], bank[5]
        O = bank[6:8]
        Y = [[UB, KVSUM], O]

        def sb(name, shape, dt=F32, stack=ctx):
            return stack.enter_context(nc.sbuf_tensor(name, shape, dt))

        ident = sb("ident", [P, P])
        gb_all = sb("gb_all", [P, NB, D])
        w_raw = sb("w_raw", [P, EW])
        w_hi = [sb("w_hi0", [P, EW], F32R), None]
        w_lo = [sb("w_lo0", [P, EW], F32R), None]

        attention = ExitStack()

        def asb(name, shape, dt=F32):
            return sb(name, shape, dt, attention)

        before = asb("before", [P, P], BF16)
        up_to = asb("up_to", [P, P], BF16)
        ones = asb("ones", [P, P], BF16)
        tri = asb("tri", [P, P])
        head_mask = asb("head_mask", [P, P])
        rank = asb("rank", [P, E])
        row_onehot = asb("row_onehot", [P, NB, NB])
        token_no = asb("token_no", [P, T])
        exponent = asb("exponent", [P, T])
        wg = asb("wg", [P, H, E])
        w4_hi = asb("w4_hi", [P, H, 4 * D], F32R)
        w4_lo = asb("w4_lo", [P, H, 4 * D], F32R)
        wo = asb("wo", [P, H, D])
        wog_hi = asb("wog_hi", [P, H, D], F32R)
        wog_lo = asb("wog_lo", [P, H, D], F32R)
        c_raw = asb("c_raw", [P, H, NB])
        c_silu = asb("c_silu", [P, H, NB])
        shift1 = asb("shift1", [P, H, NBLK])
        scale1 = asb("scale1", [P, H, NBLK])
        GA, SB, CB = range(3)
        mods = asb("mods", [P, NB, 3, D])

        xa = asb("xa", [P, T, D])
        stats1 = asb("stats1", [P, T, 6])
        mv1 = asb("mv1", [P, T, 2])
        var1 = asb("var1", [P, T])
        neg_mean1 = asb("neg_mean1", [P, T])
        rstd1 = asb("rstd1", [P, T])
        bias1 = asb("bias1", [P, T])
        xn = asb("xn", [P, T, D])
        h32 = asb("h32", [P, H, BLK])
        h_hi = asb("h_hi", [P, H, BLK], F32R)
        h_lo = asb("h_lo", [P, H, BLK], F32R)
        k_hi = [asb(f"k_hi{i}", [P, D], F32R) for i in range(2)]
        k_lo = [asb(f"k_lo{i}", [P, D], F32R) for i in range(2)]
        v2 = [asb(f"v2{i}", [P, H, 2 * P], F32R) for i in range(2)]
        q_ring = asb("q_ring", [P, PER, H, BLK])
        u_ring = asb("u_ring", [P, PER, T, D])
        kv_a = asb("kv_a", [P, H, P])
        kv_b = asb("kv_b", [P, H, P])
        kv_hi = asb("kv_hi", [P, H, P], F32R)
        kv_lo = asb("kv_lo", [P, H, P], F32R)
        q_hi = asb("q_hi", [P, H, BLK], F32R)
        q_lo = asb("q_lo", [P, H, BLK], F32R)
        sq = asb("sq", [P, T, D])
        c_wide = sq[:, :, :].rearrange("p t d -> p (t d)").rearrange("p (h b w) -> p h b w", h=H, b=NB)
        ssq = asb("ssq", [P, T * NH])
        rms = asb("rms", [P, T * NH])
        rrms = asb("rrms", [P, T * NH])
        g = asb("g", [P, T, D])
        g_size, g_sign = g[:, 0, :], g[:, 1, :]
        gt_hi = asb("gt_hi", [P, H, BLK], F32R)
        gt_lo = asb("gt_lo", [P, H, BLK], F32R)
        xr = asb("xr", [P, T, D])
        x1 = asb("x1", [P, T, D])
        stats2 = asb("stats2", [P, T, 6])
        mv2 = asb("mv2", [P, T, 2])
        var2 = asb("var2", [P, T])
        rstd2 = asb("rstd2", [P, T])
        xc = asb("xc", [P, T, D])
        wog = xc[:, 0:H, :]
        rows = asb("rows", [P, T, ROW])
        h2t = asb("h2t", [P, H, BLK])
        top = asb("top", [P, T])
        below_top = asb("below_top", [P, T, E])
        prob = asb("prob", [P, T, E])
        psum_ = asb("psum_", [P, T])
        ptop = asb("ptop", [P, T])
        is_top = asb("is_top", [P, T, E])
        ranked = asb("ranked", [P, T, E])
        best = asb("best", [P, T])
        chosen = asb("chosen", [P, T, E], BF16)
        seen = asb("seen", [P, E], BF16)
        newly = asb("newly", [P, E])
        rsum = asb("rsum", [P, T])
        gate = asb("gate", [P, T])
        picked = asb("picked", [P, T, E])
        place = asb("place", [P, T])
        over = asb("over", [P, T])
        first_slot = asb("first_slot", [P, T])
        slot = asb("slot", [P, T])
        slot_no = asb("slot_no", [P, T], U32)
        attention.close()

        w_hi[1] = sb("w_hi1", [P, EW], F32R)
        w_lo[1] = sb("w_lo1", [P, EW], F32R)
        got = [sb(f"got{i}", [P, T, ROW]) for i in range(2)]
        e_hi = [sb(f"e_hi{i}", [P, H, BLK], F32R) for i in range(2)]
        e_lo = [sb(f"e_lo{i}", [P, H, BLK], F32R) for i in range(2)]
        f_hi = [sb(f"f_hi{i}", [P, BLK], F32R) for i in range(2)]
        f_lo = [sb(f"f_lo{i}", [P, BLK], F32R) for i in range(2)]
        factor = sb("factor", [P, T, D])
        res = [sb(f"res{i}", [P, T, D]) for i in range(2)]
        token_at = [sb(f"token_at{i}", [P, T], U32) for i in range(2)]

        weights_in = sem("weights_in")
        x_in, xr_in = sem("x_in"), sem("xr_in")
        zeros_out = sem("zeros_out")
        x1_out = sem("x1_out")
        rows_out = sem("rows_out")
        w_in = sem("w_in")
        got_in = [sem("got_in0"), sem("got_in1")]
        res_out = sem("res_out")
        rows_zero, consts_pool, consts_dve = sem("rows_zero"), sem("consts_pool"), sem("consts_dve")
        tri_made = sem("tri_made")
        c_ready, mod_t_done, mod_t_read, w4_hi_done, w4_lo_done = (
            sem(s) for s in ("c_ready", "mod_t_done", "mod_t_read", "w4_hi_done", "w4_lo_done"))
        c_spread, mod_done, mod_read, g_guard = (
            sem(s) for s in ("c_spread", "mod_done", "mod_read", "g_guard"))
        h_turned, kv_done, u_done, q_done, kv_summed = (
            sem(s) for s in ("h_turned", "kv_done", "u_done", "q_done", "kv_summed"))
        att_done, g_turned, wo_done, h2_turned, logits_done, places_done = (
            sem(s) for s in ("att_done", "g_turned", "wo_done", "h2_turned", "logits_done", "places_done"))
        e_turned, hid_done, y_part = sem("e_turned"), sem("hid_done"), sem("y_part")
        xn_done, h_scaled, kv_hi_out, u_out, q_out, sq_out, rms_out = (
            sem(s) for s in ("xn_done", "h_scaled", "kv_hi_out", "u_out", "q_out", "sq_out", "rms_out"))
        gt_hi_out, x1_copied, h2t_out, prob_out = (
            sem(s) for s in ("gt_hi_out", "x1_copied", "h2t_out", "prob_out"))
        e_hi_out, f_hi_out, w_hi_out, factor0_out = (
            sem(s) for s in ("e_hi_out", "f_hi_out", "w_hi_out", "factor0_out"))
        stats1_done, mv1_done, var1_done = (
            sem(s) for s in ("stats1_done", "mv1_done", "var1_done"))
        kv_lo_done, q_hi_done, att_kv, att_kv_step, wog_step, wog_done = (
            sem(s) for s in ("kv_lo_done", "q_hi_done", "att_kv", "att_kv_step", "wog_step", "wog_done"))
        gated, ssq_sum, ssq_done, rrms_done, g_done, gt_lo_done, x1_done = (
            sem(s) for s in ("gated", "ssq_sum", "ssq_done", "rrms_done", "g_done", "gt_lo_done", "x1_done"))
        stats2_done, mv2_done, var2_done, xc_done, h2_done = (
            sem(s) for s in ("stats2_done", "mv2_done", "var2_done", "xc_done", "h2_done"))
        route_step, shifted_done, chosen_done, places_read, slot_step, slots_done = (
            sem(s) for s in ("route_step", "shifted_done", "chosen_done", "places_read", "slot_step", "slots_done"))
        e_lo_done, f_lo_done, w_lo_done, factor_step, scaled_done, token_done = (
            sem(s) for s in ("e_lo_done", "f_lo_done", "w_lo_done", "factor_step", "scaled_done", "token_done"))
        stats1_seen, stats2_seen, scatter_turn = (
            sem(s) for s in ("stats1_seen", "stats2_seen", "scatter_turn"))
        rstd1_step, rstd1_done, h_lo_done, q_lo_done, rstd2_done, res_done = (
            sem(s) for s in ("rstd1_step", "rstd1_done", "h_lo_done", "q_lo_done", "rstd2_done", "res_done"))

        block = ctx.enter_context(nc.Block())

        def run_steps(eng, step, batch_end, last):
            step(0, 0, 0, p1=True, p2=False, p3=False, ahead=True)
            with eng.Fori(1, PER) as r:
                step(r, 0, r, p1=True, p2=False, p3=False, ahead=True)
            batch_end(0)
            step(PER, 1, 0, p1=True, p2=True, p3=False, ahead=True)
            with eng.Fori(1, NB - 1) as b:
                with eng.Fori(1, PER) as r:
                    step(b * PER + r, b, r, p1=True, p2=True, p3=True, ahead=True)
                batch_end(b)
                step(b * PER + PER, b + 1, 0, p1=True, p2=True, p3=True, ahead=True)
            with eng.Fori(1, PER - 1) as r:
                step(r + (NB - 1) * PER, NB - 1, r, p1=True, p2=True, p3=True, ahead=True)
            step(NBLK - 1, NB - 1, PER - 1, p1=True, p2=True, p3=True, ahead=False)
            batch_end(NB - 1)
            with eng.Fori(0, PER - 1) as r:
                step(r + NBLK, NB, r, p1=False, p2=True, p3=True, ahead=False)
            step(NBLK + PER - 1, NB, PER - 1, p1=False, p2=True, p3=True, ahead=False)
            last(NBLK - 1)

        def has_next(j):
            return not (isinstance(j, int) and j == NBLK - 1)

        def run_experts(eng, body, last):
            body(0, 0, 0, False, True)
            body(1, 0, 1, True, True)
            with eng.Fori(1, E // 2 - 1) as pair:
                body(2 * pair, pair, 0, True, True)
                body(2 * pair + 1, pair, 1, True, True)
            body(E - 2, E // 2 - 1, 0, True, True)
            body(E - 1, E // 2 - 1, 1, True, False)
            last(E - 1, E // 2 - 1, 1)

        def start_counts(eng, *sems):
            for s in sems:
                eng.sem_inc(s, START)

        @block.sync
        def _(sp):
            sp.dma_start(xa[:, :, :], x[0]).then_inc(x_in, 16)
            sp.dma_start(q_ring[:, 0:2, :, :], w_kvuq).then_inc(weights_in, 16)
            sp.dma_start(w_raw[:, 0:H * 6 * D], w_mod).then_inc(weights_in, 16)
            sp.dma_start(wo[:, :, :], w_o).then_inc(weights_in, 16)

            sp.wait_ge(rows_zero, 1)

            def zero_slots(s):
                for e in range(PER):
                    sp.dma_start(slots[s * PER + e], rows[:, :, :]).then_inc(zeros_out, 16)

            def load_x(i):
                sp.wait_ge(xn_done, n(i))
                sp.dma_start(xa[:, :, :], x[i]).then_inc(x_in, 16)

            def swap_x1(j, more):
                sp.wait_ge(x1_done, n(2 * j + 2))
                sp.dma_start(out_blocks[j], x1[:, :, :]).then_inc(x1_out, 16)
                if more:
                    sp.dma_start(xr[:, :, :], x[j + 1]).then_inc(xr_in, 16)

            with sp.Fori(0, PER) as s:
                load_x(s + 1)
                zero_slots(s)
            sp.dma_start(xr[:, :, :], x[0]).then_inc(xr_in, 16)
            with sp.Fori(PER, NBLK - 1) as s:
                load_x(s + 1)
                swap_x1(s - PER, True)
            sp.wait_ge(mod_done, n(2 * NB))
            sp.dma_start(w_raw[:, :], w_experts[0]).then_inc(w_in, 16)
            with sp.Fori(NBLK - 1 - PER, NBLK - 1) as j:
                swap_x1(j, True)
            swap_x1(NBLK - 1, False)

            sp.wait_ge(x1_out, 16 * NBLK)
            sp.wait_ge(rows_out, 16 * (NBLK * T + 1))
            sp.dma_start(got[0][:, :, :], slots[0]).then_inc(got_in[0], 16)
            sp.dma_start(got[1][:, :, :], slots[1]).then_inc(got_in[1], 16)

            def load_w(e):
                sp.wait_ge(w_hi_out, n(4 * e))
                sp.wait_ge(w_lo_done, n(4 * e))
                sp.dma_start(w_raw[:, :], w_experts[e]).then_inc(w_in, 16)

            def load_rows(e, y):
                sp.wait_ge(res_done, n(e - 1))
                sp.dma_start(got[y][:, :, :], slots[e]).then_inc(got_in[y], 16)

            load_w(1)
            with sp.Fori(1, E // 2) as pair:
                load_w(2 * pair)
                load_rows(2 * pair, 0)
                load_w(2 * pair + 1)
                load_rows(2 * pair + 1, 1)
            sp.wait_ge(res_out, 16 * (E * T + 1))

        @block.gpsimd
        def _(pool):
            start_counts(pool, rstd1_step, rstd1_done, h_lo_done, q_lo_done, rstd2_done, res_done)
            pool.dma_start(c_raw[:, :, :], c_t).then_inc(res_out, 16)
            pool.dma_start(wg[:, :, :], w_gate).then_inc(rows_out, 16)
            nc.gpsimd.memset(rows[:, :, :], 0.0).then_inc(rows_zero, 1)
            nc.gpsimd.memset(ident[:, :], 0.0).then_inc(tri_made, 1)
            nc.gpsimd.memset(tri[:, :], 1.0).then_inc(tri_made, 1)
            nc.gpsimd.memset(head_mask[:, :], 1.0 / HEAD).then_inc(tri_made, 1)
            nc.gpsimd.memset(row_onehot[:, :, :], 0.0).then_inc(tri_made, 1)
            pool.wait_ge(tri_made, 4)
            nc.gpsimd.affine_select(out=ident[:, :], in_=ident[:, :], compare_op=ALU.not_equal, fill=1.0,
                                    base=0, pattern=[[-1, P]], channel_multiplier=1).then_inc(consts_pool, 1)
            per_half = [[-HEAD, P // HEAD], [0, HEAD]]
            nc.gpsimd.affine_select(out=head_mask[:, :], in_=head_mask[:, :], compare_op=ALU.is_ge, fill=0.0,
                                    base=0, pattern=per_half, channel_multiplier=1).then_inc(tri_made, 1)
            pool.wait_ge(tri_made, 5)
            nc.gpsimd.affine_select(out=head_mask[:, :], in_=head_mask[:, :], compare_op=ALU.is_ge, fill=0.0,
                                    base=HEAD - 1, pattern=[[HEAD, P // HEAD], [0, HEAD]],
                                    channel_multiplier=-1).then_inc(consts_pool, 1)
            nc.gpsimd.affine_select(out=row_onehot[:, :, :], in_=row_onehot[:, :, :], compare_op=ALU.not_equal,
                                    fill=1.0, base=0, pattern=[[1, NB], [-1, NB]],
                                    channel_multiplier=0).then_inc(consts_pool, 1)
            nc.gpsimd.iota(rank[:, :], pattern=[[-1, E]], base=E, channel_multiplier=0,
                           allow_small_or_imprecise_dtypes=True).then_inc(consts_pool, 1)
            nc.gpsimd.iota(token_no[:, :], pattern=[[1, T]], base=-int(FAR), channel_multiplier=T,
                           allow_small_or_imprecise_dtypes=True).then_inc(consts_pool, 1)
            nc.gpsimd.affine_select(out=before[:, :], in_=tri[:, :], compare_op=ALU.is_gt, fill=0.0,
                                    base=0, pattern=[[1, P]], channel_multiplier=-1).then_inc(consts_pool, 1)
            nc.gpsimd.affine_select(out=up_to[:, :], in_=tri[:, :], compare_op=ALU.is_ge, fill=0.0,
                                    base=0, pattern=[[1, P]], channel_multiplier=-1).then_inc(consts_pool, 1)

            def rstd_first(i):
                pool.wait_ge(var1_done, n(i + 1))
                nc.gpsimd.tensor_tensor(rstd1[:, :], var1[:, :], exponent[:, :], ALU.pow).then_inc(rstd1_step, 1)
                pool.wait_ge(rstd1_step, n(i + 1))
                nc.gpsimd.tensor_tensor(bias1[:, :], neg_mean1[:, :], rstd1[:, :], ALU.mult).then_inc(rstd1_done, 1)

            def low_part(i):
                for c in range(H):
                    pool.wait_ge(h_scaled, n(2 * i + c + 1))
                    nc.gpsimd.tensor_tensor(h_lo[:, c, :], h32[:, c, :], h_hi[:, c, :],
                                            ALU.subtract).then_inc(h_lo_done, 1)

            pool.wait_ge(consts_dve, 1)
            rstd_first(0)
            low_part(0)

            def step(i, b, r, p1, p2, p3, ahead):
                j, k = i - PER, i - PER - 1
                if p3:
                    rstd_second(k)
                if ahead:
                    rstd_first(i + 1)
                if p2 and has_next(j):
                    split_q(j + 1, (r + 1) % PER)
                if ahead:
                    low_part(i + 1)
                if p3:
                    scatter_rows(k)

            def split_q(j, r):
                for c in range(H):
                    pool.wait_ge(q_hi_done, n(2 * j + c + 1))
                    nc.gpsimd.tensor_tensor(q_lo[:, c, :], q_ring[:, r, c, :], q_hi[:, c, :],
                                            ALU.subtract).then_inc(q_lo_done, 1)

            def batch_end(b):
                if isinstance(b, int) and b == 0:
                    split_q(0, 0)

            def rstd_second(k):
                pool.wait_ge(var2_done, n(k + 1))
                nc.gpsimd.tensor_tensor(rstd2[:, :], var2[:, :], exponent[:, :], ALU.pow).then_inc(rstd2_done, 1)

            def scatter_rows(k):
                pool.wait_ge(slots_done, n(k + 1))
                pool.wait_ge(x1_copied, n(k + 1))
                pool.wait_ge(zeros_out, 16 * E)
                pool.wait_ge(rows_out, 16 * (T * k + 1))
                pool.sem_inc(scatter_turn, 1)
                for t in range(T):
                    nc.gpsimd.indirect_dma_start(
                        dispatched, bass.IndirectOffsetOnAxis(ap=slot_no[:, t:t + 1], axis=0),
                        rows[:, t, :], None, bounds_check=E * CAP - 1, oob_is_err=False).then_inc(rows_out, 16)

            def last(k):
                rstd_second(k)
                scatter_rows(k)

            run_steps(pool, step, batch_end, last)

            def finish(e, pair, y):
                pool.wait_ge(scaled_done, n(e + 1))
                pool.wait_ge(got_in[y], 16 * (pair + 1))
                nc.gpsimd.tensor_tensor(res[y][:, :, :], res[y][:, :, :], got[y][:, :, D:2 * D],
                                        ALU.add).then_inc(res_done, 1)
                pool.wait_ge(token_done, n(e + 1))
                pool.wait_ge(res_done, n(e + 1))
                pool.wait_ge(x1_out, 16 * NBLK)
                pool.wait_ge(res_out, 16 * (T * e + 1))
                pool.sem_inc(scatter_turn, 1)
                for t in range(T):
                    nc.gpsimd.indirect_dma_start(
                        out, bass.IndirectOffsetOnAxis(ap=token_at[y][:, t:t + 1], axis=0),
                        res[y][:, t, :], None, bounds_check=NBLK * BLK - 1, oob_is_err=False).then_inc(res_out, 16)

            def body(e, pair, y, prev, nxt):
                if prev:
                    finish(e - 1, pair if y else pair - 1, 1 - y)

            run_experts(pool, body, finish)

        @block.scalar
        def _(act):
            start_counts(act, xn_done, q_hi_done, h_scaled, kv_hi_out, u_out, q_out, sq_out, rms_out, gt_hi_out, x1_copied,
                         h2t_out, prob_out, e_hi_out, f_hi_out, w_hi_out, factor0_out)
            act.wait_ge(weights_in, 16 * 3)
            act.wait_ge(res_out, 16)
            nc.scalar.activation(c_silu[:, :, :], c_raw[:, :, :], ACT.Silu).then_inc(c_ready, 1)
            for c in range(H):
                nc.scalar.activation(w4_hi[:, c, :], q_ring[:, c, :, :].rearrange("p h w -> p (h w)"),
                                     ACT.Copy).then_inc(w4_hi_done, 1)

            def normalise_first(i):
                act.wait_ge(rstd1_done, n(i + 1))
                act.wait_ge(h_turned, n(2 * i))
                for t in range(T):
                    ins = nc.scalar.activation(xn[:, t, :], xa[:, t, :], ACT.Identity, bias=bias1[:, t:t + 1],
                                               scale=rstd1[:, t:t + 1])
                ins.then_inc(xn_done, 1)

            def scale_h(i):
                act.wait_ge(q_done, n(2 * i))
                act.wait_ge(h_lo_done, n(2 * i))
                act.wait_ge(mod_t_read, 2)
                for c in range(H):
                    act.wait_ge(h_turned, n(2 * i + c + 1))
                    for h in (h32, h_hi):
                        ins = nc.scalar.activation(h[:, c, :], X[c][:, :], ACT.Identity,
                                                   bias=shift1[:, c, bass.ds(i, 1)], scale=scale1[:, c, bass.ds(i, 1)])
                    ins.then_inc(h_scaled, 1)

            def q_high(j, r):
                act.wait_ge(att_done, n(2 * j))
                act.wait_ge(q_out, n(2 * j + 2))
                for c in range(H):
                    nc.scalar.activation(q_hi[:, c, :], q_ring[:, r, c, :], ACT.Copy).then_inc(q_hi_done, 1)

            def kv_high(i, t):
                act.wait_ge(kv_done, n(4 * i + t + 1))
                act.wait_ge(kv_summed, n(4 * i + t - 1))
                nc.scalar.activation(k_hi[t % 2][:, :], KV[t % 2][:, 0:D], ACT.Relu)
                nc.scalar.activation(v2[t % 2][:, :, 0:P], KV[t % 2][:, D:2 * D].rearrange("p (c w) -> p c w", c=H),
                                     ACT.Copy).then_inc(kv_hi_out, 1)

            def silu_u(i, r, pr):
                act.wait_ge(u_done, n(2 * i + pr + 1))
                nc.scalar.activation(u_ring[:, r, 2 * pr:2 * pr + 2, :].rearrange("p t d -> p (t d)"),
                                     UB[:, :], ACT.Silu).then_inc(u_out, 1)

            def copy_x1(k):
                act.wait_ge(x1_done, n(2 * k + 2))
                act.wait_ge(rows_out, 16 * (T * k + 1))
                act.wait_ge(zeros_out, 16 * E)
                nc.scalar.activation(rows[:, :, D:2 * D], x1[:, :, :], ACT.Copy).then_inc(x1_copied, 1)

            def keep_h2t(k):
                for c in range(H):
                    act.wait_ge(h2_turned, n(2 * k + c + 1))
                    act.wait_ge(logits_done, n(k))
                    nc.scalar.activation(h2t[:, c, :], X[c][:, :], ACT.Copy).then_inc(h2t_out, 1)

            def exp_logits(k):
                act.wait_ge(shifted_done, n(k + 1))
                act.wait_ge(slots_done, n(k))
                nc.scalar.activation(prob[:, :, :], below_top[:, :, :], ACT.Exp).then_inc(prob_out, 1)

            normalise_first(0)
            scale_h(0)

            def step(i, b, r, p1, p2, p3, ahead):
                j, k = i - PER, i - PER - 1
                if p1:
                    kv_high(i, 0)
                    kv_high(i, 1)
                if p2:
                    for pr in range(2):
                        act.wait_ge(att_done, n(2 * j + pr + 1))
                        act.wait_ge(ssq_sum, n(j))
                        nc.scalar.activation(sq[:, 2 * pr:2 * pr + 2, :].rearrange("p t d -> p (t d)"),
                                             O[pr][:, :], ACT.Square).then_inc(sq_out, 1)
                if p1:
                    if p2:
                        act.wait_ge(gated, n(2 * j + 2))
                    silu_u(i, r, 0)
                    kv_high(i, 2)
                if p3:
                    copy_x1(k)
                if p2:
                    act.wait_ge(ssq_done, n(j + 1))
                    nc.scalar.activation(rms[:, :], ssq[:, :], ACT.Sqrt, scale=1.0 / HEAD).then_inc(rms_out, 1)
                if p1:
                    kv_high(i, 3)
                if p2 and has_next(j):
                    q_high(j + 1, (r + 1) % PER)
                if ahead:
                    normalise_first(i + 1)
                if p3:
                    keep_h2t(k)
                if p1:
                    keep_q(i, j, r, 0, p2)
                if p2:
                    for c in range(H):
                        act.wait_ge(g_turned, n(2 * j + c + 1))
                        act.wait_ge(wo_done, n(2 * j))
                        nc.scalar.activation(gt_hi[:, c, :], X[c][:, :], ACT.Copy).then_inc(gt_hi_out, 1)
                if p3:
                    exp_logits(k)
                if p1:
                    silu_u(i, r, 1)
                    keep_q(i, j, r, 1, p2)
                if ahead:
                    scale_h(i + 1)

            def keep_q(i, j, r, c, p2):
                act.wait_ge(q_done, n(2 * i + c + 1))
                if p2:
                    act.wait_ge(q_lo_done, n(2 * j + 2))
                else:
                    act.wait_ge(w4_lo_done, 2)
                nc.scalar.activation(q_ring[:, r, c, :], KV[c][:, :], ACT.Relu).then_inc(q_out, 1)

            def batch_end(b):
                if isinstance(b, int) and b == 0:
                    q_high(0, 0)

            def last(k):
                copy_x1(k)
                keep_h2t(k)
                exp_logits(k)

            run_steps(act, step, batch_end, last)

            def split_w(e, y, piece):
                act.wait_ge(w_in, 16 * (e + 1))
                act.wait_ge(y_part, n(NF * (e - 1)))
                part = slice(piece * EW // 4, (piece + 1) * EW // 4)
                nc.scalar.activation(w_hi[y][:, part], w_raw[:, part], ACT.Copy).then_inc(w_hi_out, 1)

            def rows_high(e, y):
                for c in range(H):
                    act.wait_ge(e_turned, n(2 * e + c + 1))
                    act.wait_ge(hid_done, n(NF * (e - 1)))
                    nc.scalar.activation(e_hi[y][:, c, :], X[c][:, :], ACT.Copy).then_inc(e_hi_out, 1)

            act.wait_ge(w_in, 16)
            for piece in range(4):
                part = slice(piece * EW // 4, (piece + 1) * EW // 4)
                nc.scalar.activation(w_hi[0][:, part], w_raw[:, part], ACT.Copy).then_inc(w_hi_out, 1)
            act.wait_ge(e_turned, n(1))
            nc.scalar.activation(e_hi[0][:, 0, :], X[0][:, :], ACT.Copy).then_inc(e_hi_out, 1)
            act.wait_ge(e_turned, n(2))
            nc.scalar.activation(e_hi[0][:, 1, :], X[1][:, :], ACT.Copy).then_inc(e_hi_out, 1)

            def body(e, pair, y, prev, nxt):
                for f in range(NF):
                    act.wait_ge(hid_done, n(NF * e + f + 1))
                    act.wait_ge(y_part, n(NF * e + f - 1))
                    nc.scalar.activation(f_hi[f % 2][:, :], KV[f % 2][:, :], ACT.Relu).then_inc(f_hi_out, 1)
                    if nxt and f % 2 == 1:
                        split_w(e + 1, 1 - y, f // 2)
                    if f == 2:
                        act.wait_ge(scaled_done, n(e))
                        act.wait_ge(got_in[y], 16 * (pair + 1))
                        for t in range(T):
                            ins = nc.scalar.activation(factor[:, t, :], gb_all[:, 0, :], ACT.Copy,
                                                       scale=got[y][:, t, GATE0:GATE0 + 1])
                        ins.then_inc(factor0_out, 1)
                    if nxt and f == NF - 1:
                        rows_high(e + 1, 1 - y)

            run_experts(act, body, lambda e, pair, y: None)

        @block.vector
        def _(dve):
            start_counts(dve, stats1_done, mv1_done, var1_done, kv_lo_done, places_read,
                         att_kv, att_kv_step, wog_step, wog_done, gated, ssq_sum, ssq_done, rrms_done, g_done,
                         gt_lo_done, x1_done, stats2_done, mv2_done, var2_done, xc_done, h2_done,
                         route_step, shifted_done, chosen_done, slot_step, slots_done,
                         e_lo_done, f_lo_done, w_lo_done, factor_step, scaled_done, token_done, mod_read)
            nc.vector.memset(exponent[:, :], -0.5).then_inc(consts_dve, 1)
            nc.vector.memset(ones[:, :], 1.0).then_inc(consts_dve, 1)
            nc.vector.memset(seen[:, :], 0.0).then_inc(consts_dve, 1)

            def norm_stats_first(i):
                dve.wait_ge(x_in, 16 * (i + 1))
                for t in range(T):
                    ins = nc.vector.bn_stats(stats1[:, t, :], xa[:, t, :])
                ins.then_inc(stats1_done, 1)
                dve.wait_ge(stats1_done, n(i + 1))
                dve.sem_inc(stats1_seen, 1)
                for t in range(T):
                    ins = nc.vector.bn_aggr(mv1[:, t, :], stats1[:, t, :])
                ins.then_inc(mv1_done, 1)
                dve.wait_ge(mv1_done, n(i + 1))
                nc.vector.tensor_scalar(neg_mean1[:, :], mv1[:, :, 0], -1.0, None, ALU.mult)
                nc.vector.tensor_scalar(var1[:, :], mv1[:, :, 1], LN_EPS, None, ALU.add).then_inc(var1_done, 1)

            norm_stats_first(0)
            dve.wait_ge(c_ready, 1)
            nc.vector.tensor_copy(c_wide,
                                  c_silu[:, :, :].unsqueeze(3).to_broadcast([P, H, NB, P])).then_inc(c_spread, 1)
            for c in range(H):
                dve.wait_ge(w4_hi_done, c + 1)
                nc.vector.tensor_tensor(w4_lo[:, c, :], q_ring[:, c, :, :].rearrange("p h w -> p (h w)"),
                                        w4_hi[:, c, :], ALU.subtract).then_inc(w4_lo_done, 1)
            dve.wait_ge(mod_t_done, 1)
            by_row = UB[:, 0:2 * H * NB].rearrange("p (a c b) -> p a c b", a=2, c=H)
            nc.vector.tensor_copy(shift1[:, :, :].rearrange("p c (b r) -> p c b r", r=PER),
                                  by_row[:, 0, :, :].unsqueeze(3).to_broadcast([P, H, NB, PER])).then_inc(mod_t_read, 1)
            nc.vector.tensor_scalar(scale1[:, :, :].rearrange("p c (b r) -> p c b r", r=PER),
                                    by_row[:, 1, :, :].unsqueeze(3).to_broadcast([P, H, NB, PER]),
                                    1.0, None, ALU.add).then_inc(mod_t_read, 1)
            def kv_low(i, t):
                dve.wait_ge(kv_hi_out, n(4 * i + t + 1))
                nc.vector.scalar_tensor_tensor(out=k_lo[t % 2][:, :], in0=KV[t % 2][:, 0:D], scalar=0.0,
                                               in1=k_hi[t % 2][:, :], op0=ALU.max, op1=ALU.subtract)
                nc.vector.tensor_tensor(v2[t % 2][:, :, P:2 * P],
                                        KV[t % 2][:, D:2 * D].rearrange("p (c w) -> p c w", c=H),
                                        v2[t % 2][:, :, 0:P], ALU.subtract).then_inc(kv_lo_done, 1)

            def batch_end(b):
                dve.wait_ge(kv_summed, n(4 * PER * (b + 1)))
                dve.wait_ge(consts_pool, 7)
                both = KVSUM[:, :].rearrange("p (c a w) -> p c a w", c=H, a=2)
                mask = head_mask[:, :].unsqueeze(1).to_broadcast([P, H, P])
                dve.wait_ge(att_done, n(2 * PER * b))
                nc.vector.tensor_tensor(kv_a[:, :, :], both[:, :, 0, :], mask, ALU.mult)
                nc.vector.tensor_tensor(kv_b[:, :, :], both[:, :, 1, :], mask, ALU.mult).then_inc(att_kv_step, 1)
                dve.wait_ge(att_kv_step, n(3 * b + 1))
                nc.vector.tensor_tensor(kv_a[:, :, :], kv_a[:, :, :], kv_b[:, :, :], ALU.add).then_inc(att_kv_step, 1)
                dve.wait_ge(att_kv_step, n(3 * b + 2))
                nc.vector.tensor_copy(kv_hi[:, :, :], kv_a[:, :, :]).then_inc(att_kv_step, 1)
                dve.wait_ge(att_kv_step, n(3 * b + 3))
                nc.vector.tensor_tensor(kv_lo[:, :, :], kv_a[:, :, :], kv_hi[:, :, :],
                                        ALU.subtract).then_inc(att_kv, 1)
                dve.wait_ge(wo_done, n(2 * PER * b))
                dve.wait_ge(g_guard, 6 * NB)
                ga = mods[:, b, GA, :].unsqueeze(1).to_broadcast([P, H, D])
                nc.vector.tensor_tensor(wog, wo[:, :, :], ga, ALU.mult).then_inc(wog_step, 1)
                dve.wait_ge(wog_step, n(2 * b + 1))
                nc.vector.tensor_copy(wog_hi[:, :, :], wog).then_inc(wog_step, 1)
                dve.wait_ge(wog_step, n(2 * b + 2))
                nc.vector.tensor_tensor(wog_lo[:, :, :], wog, wog_hi[:, :, :],
                                        ALU.subtract).then_inc(wog_done, 1)

            def make_mods():
                guards = 0
                for b in range(NB):
                    for half in range(2):
                        dve.wait_ge(mod_done, n(2 * b + half + 1))
                        g_psum, s_psum = (O[half][:, 0:D], O[half][:, D:2 * D]) if half == 0 else (
                            O[half][:, D:2 * D], O[half][:, 0:D])
                        g_out = gb_all[:, b, :] if half else mods[:, b, GA, :]
                        if guards:
                            dve.wait_ge(g_guard, guards)
                        nc.vector.tensor_scalar(g_size, g_psum, 0.25, None, ALU.max)
                        nc.vector.tensor_scalar(g_sign, g_psum, 0.0, 2.0, ALU.is_ge,
                                                ALU.mult).then_inc(g_guard, 1)
                        nc.vector.tensor_scalar(mods[:, b, CB if half else SB, :], s_psum,
                                                1.0 if half else 0.0, None, ALU.add).then_inc(mod_read, 1)
                        dve.wait_ge(g_guard, guards + 1)
                        nc.vector.scalar_tensor_tensor(out=g_size, in0=g_psum, scalar=-1.0, in1=g_size,
                                                       op0=ALU.mult, op1=ALU.max).then_inc(g_guard, 1)
                        dve.wait_ge(g_guard, guards + 2)
                        nc.vector.scalar_tensor_tensor(out=g_out, in0=g_sign, scalar=-1.0, in1=g_size,
                                                       op0=ALU.add, op1=ALU.mult).then_inc(g_guard, 1)
                        guards += 3

            def stats_second(k):
                dve.wait_ge(x1_done, n(2 * k + 2))
                for t in range(T):
                    ins = nc.vector.bn_stats(stats2[:, t, :], x1[:, t, :])
                ins.then_inc(stats2_done, 1)
                dve.wait_ge(stats2_done, n(k + 1))
                dve.sem_inc(stats2_seen, 1)
                for t in range(T):
                    ins = nc.vector.bn_aggr(mv2[:, t, :], stats2[:, t, :])
                ins.then_inc(mv2_done, 1)
                dve.wait_ge(mv2_done, n(k + 1))
                nc.vector.tensor_scalar(var2[:, :], mv2[:, :, 1], LN_EPS, None, ALU.add).then_inc(var2_done, 1)

            def centre(k):
                for t in range(T):
                    ins = nc.vector.scalar_tensor_tensor(out=xc[:, t, :], in0=x1[:, t, :], scalar=mv2[:, t, 0:1],
                                                         in1=mods[:, row_of(k), CB, :], op0=ALU.subtract, op1=ALU.mult)
                ins.then_inc(xc_done, 1)

            def row_of(k):
                return k // PER

            def modulate(k):
                dve.wait_ge(rstd2_done, n(k + 1))
                dve.wait_ge(xc_done, n(k + 1))
                dve.wait_ge(rows_out, 16 * (T * k + 1))
                dve.wait_ge(zeros_out, 16 * E)
                for t in range(T):
                    ins = nc.vector.scalar_tensor_tensor(out=rows[:, t, 0:D], in0=xc[:, t, :], scalar=rstd2[:, t:t + 1],
                                                         in1=mods[:, row_of(k), SB, :], op0=ALU.mult, op1=ALU.add)
                ins.then_inc(h2_done, 1)

            ROUTE = 9

            def wide(ap):
                return ap.unsqueeze(2).to_broadcast([P, T, E])

            def shift_logits(k):
                dve.wait_ge(logits_done, n(k + 1))
                logits = O[0][:, 0:T * E].rearrange("p (t e) -> p t e", t=T)
                nc.vector.tensor_reduce(top[:, :], logits, AX.X, ALU.max).then_inc(route_step, 1)
                dve.wait_ge(route_step, n(ROUTE * k + 1))
                nc.vector.tensor_tensor(below_top[:, :, :], logits, wide(top[:, :]), ALU.subtract).then_inc(shifted_done, 1)

            def choose(k):
                dve.wait_ge(prob_out, n(k + 1))
                nc.vector.tensor_reduce(ptop[:, :], prob[:, :, :], AX.X, ALU.max).then_inc(route_step, 1)
                nc.vector.tensor_reduce(psum_[:, :], prob[:, :, :], AX.X, ALU.add).then_inc(route_step, 1)
                dve.wait_ge(route_step, n(ROUTE * k + 2))
                nc.vector.tensor_tensor(is_top[:, :, :], prob[:, :, :], wide(ptop[:, :]),
                                        ALU.is_equal).then_inc(route_step, 1)
                dve.wait_ge(route_step, n(ROUTE * k + 4))
                nc.vector.tensor_tensor(ranked[:, :, :], is_top[:, :, :],
                                        rank[:, :].unsqueeze(1).to_broadcast([P, T, E]), ALU.mult).then_inc(route_step, 1)
                dve.wait_ge(route_step, n(ROUTE * k + 5))
                nc.vector.tensor_reduce(best[:, :], ranked[:, :, :], AX.X, ALU.max).then_inc(route_step, 1)
                nc.vector.reciprocal(rsum[:, :], psum_[:, :])
                dve.wait_ge(route_step, n(ROUTE * k + 6))
                nc.vector.tensor_tensor(chosen[:, :, :], ranked[:, :, :], wide(best[:, :]),
                                        ALU.is_equal).then_inc(chosen_done, 1)
                dve.wait_ge(chosen_done, n(k + 1))
                nc.vector.tensor_tensor(gate[:, :], ptop[:, :], rsum[:, :], ALU.mult).then_inc(route_step, 1)
                nc.vector.tensor_copy(rows[:, :, TOKEN], token_no[:, :])
                dve.wait_ge(route_step, n(ROUTE * k + 7))
                nc.vector.tensor_tensor(rows[:, :, GATE0:GATE0 + NB],
                                        row_onehot[:, row_of(k), :].unsqueeze(1).to_broadcast([P, T, NB]),
                                        gate[:, :].unsqueeze(2).to_broadcast([P, T, NB]), ALU.mult)
                nc.vector.tensor_scalar(first_slot[:, :], best[:, :], -float(CAP), float(E * CAP), ALU.mult, ALU.add)
                nc.vector.tensor_reduce(newly[:, :], chosen[:, :, :].rearrange("p t e -> p e t"),
                                        AX.X, ALU.add).then_inc(route_step, 1)
                nc.vector.tensor_scalar(token_no[:, :], token_no[:, :], float(BLK), None, ALU.add)

            def number_slots(k):
                dve.wait_ge(places_done, n(k + 1))
                places = O[1][:, 0:T * E].rearrange("p (t e) -> p t e", t=T)
                nc.vector.tensor_tensor(picked[:, :, :], places, chosen[:, :, :], ALU.mult).then_inc(places_read, 1)
                dve.wait_ge(route_step, n(ROUTE * k + 8))
                nc.vector.tensor_tensor(seen[:, :], seen[:, :], newly[:, :], ALU.add)
                dve.wait_ge(places_read, n(k + 1))
                nc.vector.tensor_reduce(place[:, :], picked[:, :, :], AX.X, ALU.add).then_inc(route_step, 1)
                dve.wait_ge(route_step, n(ROUTE * k + 9))
                nc.vector.tensor_scalar(over[:, :], place[:, :], float(CAP), FAR, ALU.is_ge, ALU.mult)
                nc.vector.tensor_tensor(slot[:, :], place[:, :], first_slot[:, :], ALU.add).then_inc(slot_step, 1)
                dve.wait_ge(slot_step, n(k + 1))
                nc.vector.tensor_tensor(slot_no[:, :], slot[:, :], over[:, :], ALU.add).then_inc(slots_done, 1)

            def step(i, b, r, p1, p2, p3, ahead):
                j, k = i - PER, i - PER - 1
                if p3:
                    stats_second(k)
                if p1:
                    kv_low(i, 0)
                if p3:
                    centre(k)
                if p1:
                    kv_low(i, 1)
                if ahead:
                    norm_stats_first(i + 1)
                if p2:
                    for pr in range(2):
                        dve.wait_ge(att_done, n(2 * j + pr + 1))
                        dve.wait_ge(g_turned, n(2 * j))
                        dve.wait_ge(u_out, n(2 * j + pr + 1))
                        dve.wait_ge(sq_out, n(2 * j + pr + 1))
                        nc.vector.tensor_tensor(g[:, 2 * pr:2 * pr + 2, :].rearrange("p t d -> p (t d)"), O[pr][:, :],
                                                u_ring[:, r, 2 * pr:2 * pr + 2, :].rearrange("p t d -> p (t d)"),
                                                ALU.mult).then_inc(gated, 1)
                    nc.vector.tensor_reduce(ssq[:, :], sq[:, :, :].rearrange("p t (h w) -> p (t h) w", w=HEAD),
                                            AX.X, ALU.add).then_inc(ssq_sum, 1)
                    dve.wait_ge(ssq_sum, n(j + 1))
                    nc.vector.tensor_scalar(ssq[:, :], ssq[:, :], HEAD * RMS_FLOOR ** 2, None,
                                            ALU.max).then_inc(ssq_done, 1)
                if p1:
                    kv_low(i, 2)
                if p3:
                    modulate(k)
                if p2:
                    dve.wait_ge(rms_out, n(j + 1))
                    nc.vector.reciprocal(rrms[:, :], rms[:, :]).then_inc(rrms_done, 1)
                    dve.wait_ge(rrms_done, n(j + 1))
                    heads = g[:, :, :].rearrange("p t (h w) -> p (t h) w", w=HEAD)
                    nc.vector.tensor_tensor(heads, heads, rrms[:, :].unsqueeze(2).to_broadcast([P, T * NH, HEAD]),
                                            ALU.mult).then_inc(g_done, 1)
                if p1:
                    kv_low(i, 3)
                if p2:
                    for c in range(H):
                        dve.wait_ge(gt_hi_out, n(2 * j + c + 1))
                        nc.vector.tensor_tensor(gt_lo[:, c, :], X[c][:, :], gt_hi[:, c, :],
                                                ALU.subtract).then_inc(gt_lo_done, 1)
                if p3:
                    shift_logits(k)
                    choose(k)
                    number_slots(k)
                if p2:
                    for pr in range(2):
                        dve.wait_ge(wo_done, n(2 * j + pr + 1))
                        dve.wait_ge(xr_in, 16 * (j + 1))
                        if p3:
                            dve.wait_ge(x1_out, 16 * j)
                            dve.wait_ge(x1_copied, n(j))
                            dve.wait_ge(xc_done, n(j))
                        nc.vector.tensor_tensor(x1[:, 2 * pr:2 * pr + 2, :].rearrange("p t d -> p (t d)"), O[pr][:, :],
                                                xr[:, 2 * pr:2 * pr + 2, :].rearrange("p t d -> p (t d)"),
                                                ALU.add).then_inc(x1_done, 1)

            def batch_end_all(b):
                if isinstance(b, int) and b == 0:
                    make_mods()
                batch_end(b)

            def last(k):
                stats_second(k)
                centre(k)
                modulate(k)
                shift_logits(k)
                choose(k)
                number_slots(k)

            run_steps(dve, step, batch_end_all, last)

            def split_w(e, y, piece):
                dve.wait_ge(w_hi_out, n(4 * e + piece + 1))
                part = slice(piece * EW // 4, (piece + 1) * EW // 4)
                nc.vector.tensor_tensor(w_lo[y][:, part], w_raw[:, part], w_hi[y][:, part],
                                        ALU.subtract).then_inc(w_lo_done, 1)

            def rows_low(e, y):
                for c in range(H):
                    dve.wait_ge(e_hi_out, n(2 * e + c + 1))
                    nc.vector.tensor_tensor(e_lo[y][:, c, :], X[c][:, :], e_hi[y][:, c, :],
                                            ALU.subtract).then_inc(e_lo_done, 1)

            def results_landed(e):
                if not (isinstance(e, int) and e < 2):
                    dve.wait_ge(res_out, 16 * (T * (e - 1) + 1))

            def scale_y(e, y):
                dve.wait_ge(y_part, n(NF * (e + 1)))
                dve.wait_ge(factor_step, n((NB - 1) * (e + 1)))
                results_landed(e)
                for pr in range(2):
                    ins = nc.vector.tensor_tensor(res[y][:, 2 * pr:2 * pr + 2, :].rearrange("p t d -> p (t d)"),
                                                  Y[y][pr][:, :],
                                                  factor[:, 2 * pr:2 * pr + 2, :].rearrange("p t d -> p (t d)"), ALU.mult)
                ins.then_inc(scaled_done, 1)

            for piece in range(4):
                split_w(0, 0, piece)
            rows_low(0, 0)

            def body(e, pair, y, prev, nxt):
                for f in range(NF):
                    dve.wait_ge(f_hi_out, n(NF * e + f + 1))
                    nc.vector.scalar_tensor_tensor(out=f_lo[f % 2][:, :], in0=KV[f % 2][:, :], scalar=0.0,
                                                   in1=f_hi[f % 2][:, :], op0=ALU.max,
                                                   op1=ALU.subtract).then_inc(f_lo_done, 1)
                    if nxt and f % 2 == 1:
                        split_w(e + 1, 1 - y, f // 2)
                    if prev and f == 0:
                        scale_y(e - 1, 1 - y)
                    if f == 2:
                        dve.wait_ge(got_in[y], 16 * (pair + 1))
                        results_landed(e)
                        nc.vector.tensor_scalar(token_at[y][:, :], got[y][:, :, TOKEN], FAR, None,
                                                ALU.add).then_inc(token_done, 1)
                    if 3 <= f < 3 + NB - 1:
                        row = f - 2
                        dve.wait_ge(factor0_out, n(e + 1))
                        dve.wait_ge(factor_step, n((NB - 1) * e + row - 1))
                        for t in range(T):
                            ins = nc.vector.scalar_tensor_tensor(
                                out=factor[:, t, :], in0=gb_all[:, row, :],
                                scalar=got[y][:, t, GATE0 + row:GATE0 + row + 1],
                                in1=factor[:, t, :], op0=ALU.mult, op1=ALU.add)
                        ins.then_inc(factor_step, 1)
                    if nxt and f == NF - 1:
                        rows_low(e + 1, 1 - y)

            run_experts(dve, body, lambda e, pair, y: scale_y(e, y))

        @block.tensor
        def _(pe):
            start_counts(pe, h_turned, kv_done, u_done, q_done, kv_summed, att_done, g_turned, wo_done,
                         h2_turned, logits_done, places_done, e_turned, hid_done, y_part, mod_done)

            def tile(t):
                return slice(t * P, (t + 1) * P)

            def turn(src, done):
                for c in range(H):
                    for t in range(T):
                        ins = nc.tensor.transpose(X[c][:, tile(t)], src[:, t, c * P:(c + 1) * P], ident[:, :])
                    ins.then_inc(done, 1)

            pe.wait_ge(c_ready, 1)
            wm = w_raw[:, 0:H * 6 * D].rearrange("p (k w) -> p k w", k=H)
            for a in range(2):
                for c in range(H):
                    at = (a * H + c) * NB
                    for kk in range(H):
                        ins = nc.tensor.matmul(UB[:, at:at + NB], wm[:, kk, a * D + c * P:a * D + (c + 1) * P],
                                               c_silu[:, kk, :], start=(kk == 0), stop=(kk == H - 1))
            ins.then_inc(mod_t_done, 1)

            def turn_xn(i, j):
                pe.wait_ge(xn_done, n(i + 1))
                if j is None:
                    pe.wait_ge(h_scaled, n(2 * i))
                else:
                    pe.wait_ge(gt_lo_done, n(2 * j + 2))
                turn(xn, h_turned)

            pe.wait_ge(consts_pool, 1)
            turn_xn(0, None)

            def project_tile(i, t):
                if t == 0:
                    pe.wait_ge(h_scaled, n(2 * i + 2))
                    pe.wait_ge(q_out, n(2 * i))
                elif t >= 2:
                    pe.wait_ge(kv_lo_done, n(4 * i + t - 1))
                us = UB[:, (t % 2) * D:(t % 2 + 1) * D]
                parts = [(h_hi, w4_hi), (h_hi, w4_lo), (h_lo, w4_hi)]
                for m, (a, w) in enumerate(parts):
                    if m == 2 and t == 0:
                        pe.wait_ge(h_lo_done, n(2 * i + 2))
                    for c in range(H):
                        first, final = m == 0 and c == 0, m == 2 and c == H - 1
                        ins = nc.tensor.matmul(KV[t % 2][:, :], a[:, c, tile(t)], w[:, c, 0:2 * D],
                                               start=first, stop=final)
                        if final:
                            ins.then_inc(kv_done, 1)
                if t % 2 == 0:
                    pe.wait_ge(u_out, n(2 * i + t // 2))
                for m, (a, w) in enumerate(parts):
                    for c in range(H):
                        first, final = m == 0 and c == 0, m == 2 and c == H - 1
                        ins = nc.tensor.matmul(us, a[:, c, tile(t)], w[:, c, 2 * D:3 * D], start=first, stop=final)
                if t % 2:
                    ins.then_inc(u_done, 1)

            def sum_kv(i, b, r, t):
                pe.wait_ge(kv_lo_done, n(4 * i + t + 1))
                opens = isinstance(r, int) and r == 0 and t == 0
                if opens:
                    pe.wait_ge(att_kv, n(b))
                ends = False
                for c in range(H):
                    nc.tensor.matmul(KVSUM[:, c * 2 * P:(c + 1) * 2 * P], k_hi[t % 2][:, c * P:(c + 1) * P],
                                     v2[t % 2][:, c, :], start=opens and c == 0, stop=ends, skip_group_check=True)
                    ins = nc.tensor.matmul(KVSUM[:, c * 2 * P:c * 2 * P + P], k_lo[t % 2][:, c * P:(c + 1) * P],
                                           v2[t % 2][:, c, 0:P], start=False, stop=ends, skip_group_check=True)
                ins.then_inc(kv_summed, 1)

            def project_q(i, c):
                pe.wait_ge(kv_lo_done, n(4 * i + 3 + c))
                out_ch = slice(3 * D + c * P, 3 * D + (c + 1) * P)
                m = 0
                for a, w in ((h_hi, w4_hi), (h_hi, w4_lo), (h_lo, w4_hi)):
                    for kk in range(H):
                        ins = nc.tensor.matmul(KV[c][:, :], w[:, kk, out_ch], a[:, kk, :],
                                               start=(m == 0), stop=(m == 3 * H - 1))
                        m += 1
                ins.then_inc(q_done, 1)

            def attend(j, bj):
                pe.wait_ge(att_kv, n(bj + 1))
                pe.wait_ge(q_lo_done, n(2 * j + 2))
                for pr in range(2):
                    pe.wait_ge(x1_done, n(2 * j - 1 + pr))
                    for t in (2 * pr, 2 * pr + 1):
                        for c in range(H):
                            dst = O[pr][:, (t % 2) * D + c * P:(t % 2) * D + (c + 1) * P]
                            nc.tensor.matmul(dst, q_hi[:, c, tile(t)], kv_hi[:, c, :], start=True, stop=False)
                            nc.tensor.matmul(dst, q_hi[:, c, tile(t)], kv_lo[:, c, :], start=False, stop=False)
                            ins = nc.tensor.matmul(dst, q_lo[:, c, tile(t)], kv_hi[:, c, :], start=False, stop=True)
                    ins.then_inc(att_done, 1)

            def project_out(j, bj, k):
                pe.wait_ge(wog_done, n(bj + 1))
                pe.wait_ge(gt_lo_done, n(2 * j + 2))
                for pr in range(2):
                    if k is not None:
                        pe.wait_ge(places_read if pr else shifted_done, n(k + 1))
                    for t in (2 * pr, 2 * pr + 1):
                        m = 0
                        for a, w in ((gt_hi, wog_hi), (gt_hi, wog_lo), (gt_lo, wog_hi)):
                            for c in range(H):
                                ins = nc.tensor.matmul(O[pr][:, (t % 2) * D:(t % 2 + 1) * D], a[:, c, tile(t)],
                                                       w[:, c, :], start=(m == 0), stop=(m == 3 * H - 1))
                                m += 1
                    ins.then_inc(wo_done, 1)

            def turn_h2(k, i):
                pe.wait_ge(h2_done, n(k + 1))
                if i is not None:
                    pe.wait_ge(h_scaled, n(2 * i + 2))
                turn(rows, h2_turned)

            def logits(k, j):
                pe.wait_ge(rows_out, 16)
                pe.wait_ge(h2t_out, n(2 * k + 2))
                if j is not None:
                    pe.wait_ge(gated, n(2 * j + 1))
                for t in range(T):
                    for c in range(H):
                        ins = nc.tensor.matmul(O[0][:, t * E:(t + 1) * E], h2t[:, c, tile(t)], wg[:, c, :],
                                               start=(c == 0), stop=(c == H - 1))
                ins.then_inc(logits_done, 1)

            def count_places(k):
                pe.wait_ge(chosen_done, n(k + 1))
                places = O[1][:, 0:T * E].rearrange("p (t e) -> p t e", t=T)
                nc.tensor.matmul(places, ones[:, :], seen[:, :].unsqueeze(1).to_broadcast([P, T, E]),
                                 start=True, stop=False, skip_group_check=True)
                for s in range(T):
                    ins = nc.tensor.matmul(places[:, 0:s + 1, :], before[:, :],
                                           chosen[:, s, :].unsqueeze(1).to_broadcast([P, s + 1, E]),
                                           start=False, stop=s == T - 1, skip_group_check=True)
                    if s < T - 1:
                        nc.tensor.matmul(places[:, s + 1:T, :], up_to[:, :],
                                         chosen[:, s, :].unsqueeze(1).to_broadcast([P, T - 1 - s, E]),
                                         start=False, stop=False, skip_group_check=True)
                ins.then_inc(places_done, 1)

            def step(i, b, r, p1, p2, p3, ahead):
                j, k = i - PER, i - PER - 1
                if p1:
                    project_tile(i, 0)
                    project_tile(i, 1)
                    sum_kv(i, b, r, 0)
                if p2:
                    attend(j, b - 1)
                if p1:
                    sum_kv(i, b, r, 1)
                    project_tile(i, 2)
                    project_tile(i, 3)
                    sum_kv(i, b, r, 2)
                if p3:
                    turn_h2(k, i if p1 else None)
                if p1:
                    project_q(i, 0)
                if p2:
                    pe.wait_ge(g_done, n(j + 1))
                    if p3:
                        pe.wait_ge(h2t_out, n(2 * k + 2))
                    else:
                        pe.wait_ge(h_scaled, n(2 * i + 2))
                    turn(g, g_turned)
                if p3:
                    logits(k, j)
                if p1:
                    sum_kv(i, b, r, 3)
                    project_q(i, 1)
                if ahead:
                    turn_xn(i + 1, j if p2 else None)
                if p3:
                    count_places(k)
                if p2:
                    project_out(j, b - 1, k if p3 else None)

            def batch_end(b):
                if isinstance(b, int) and b == 0:
                    spread_mods()

            def spread_mods():
                pe.wait_ge(c_spread, 1)
                for b in range(NB):
                    for half in range(2):
                        if b:
                            pe.wait_ge(mod_read, n(2 * b - 1 + half))
                            pe.wait_ge(g_guard, 6 * b - 4 + 3 * half)
                        for kk in range(H):
                            ins = nc.tensor.matmul(O[half][:, :], c_wide[:, kk, b, :],
                                                   wm[:, kk, 2 * D * (half + 1):2 * D * (half + 2)],
                                                   start=(kk == 0), stop=(kk == H - 1))
                        ins.then_inc(mod_done, 1)
                pe.wait_ge(g_guard, 6 * NB)
                pe.wait_ge(mod_read, n(2 * NB))

            def last(k):
                turn_h2(k, None)
                logits(k, None)
                count_places(k)

            run_steps(pe, step, batch_end, last)

            def turn_rows(e, pair, y):
                pe.wait_ge(got_in[y], 16 * (pair + 1))
                pe.wait_ge(e_lo_done, n(2 * e))
                turn(got[y], e_turned)

            def hidden(e, y, f):
                pe.wait_ge(f_lo_done, n(NF * e + f - 1))
                m = 0
                for w, a in ((w_hi, e_hi), (w_lo, e_hi), (w_hi, e_lo)):
                    w1 = w[y][:, 0:H * F].rearrange("p (c f) -> p c f", c=H)
                    for c in range(H):
                        ins = nc.tensor.matmul(KV[f % 2][:, :], w1[:, c, f * P:(f + 1) * P], a[y][:, c, :],
                                               start=(m == 0), stop=(m == 3 * H - 1))
                        m += 1
                ins.then_inc(hid_done, 1)

            def partial_y(e, y, f):
                pe.wait_ge(f_lo_done, n(NF * e + f + 1))
                for t in range(T):
                    dst = Y[y][t // 2][:, (t % 2) * D:(t % 2 + 1) * D]
                    m = 0
                    for a, w in ((f_hi, w_hi), (f_hi, w_lo), (f_lo, w_hi)):
                        w2 = w[y][:, H * F:2 * H * F].rearrange("p (f d) -> p f d", f=NF)
                        ins = nc.tensor.matmul(dst, a[f % 2][:, tile(t)], w2[:, f, :],
                                               start=(f == 0 and m == 0 and t % 2 == 0),
                                               stop=(f == NF - 1 and m == 2), skip_group_check=True)
                        m += 1
                ins.then_inc(y_part, 1)

            turn_rows(0, 0, 0)

            def body(e, pair, y, prev, nxt):
                pe.wait_ge(e_lo_done, n(2 * e + 2))
                pe.wait_ge(w_lo_done, n(4 * e + 4))
                for f in range(NF):
                    hidden(e, y, f)
                    if f == 1 and prev:
                        pe.wait_ge(scaled_done, n(e - 1))
                    if f:
                        partial_y(e, y, f - 1)
                    if f == NF - 2 and nxt:
                        turn_rows(e + 1, pair + 1 if y else pair, 1 - y)
                partial_y(e, y, NF - 1)

            run_experts(pe, body, lambda e, pair, y: None)


def kernel(L0_attn_x, L0_attn_Wq, L0_attn_Wk, L0_attn_Wv, L0_attn_Wu, L0_attn_Wo, L0_ffn_Wg, L0_ffn_w1,
           L0_ffn_w2, L0_c, L0_wmod):
    import numpy as np
    import concourse.bacc as bacc
    from concourse.bass_utils import run_bass_kernel_spmd

    def halves(w):
        w = np.asarray(w)
        return np.ascontiguousarray(w.reshape(-1, P, w.shape[1]).transpose(1, 0, 2))

    x = np.ascontiguousarray(L0_attn_x)
    b, l, d = x.shape
    experts, _, hidden = L0_ffn_w1.shape
    w4 = np.concatenate([np.asarray(w).T for w in (L0_attn_Wk, L0_attn_Wv, L0_attn_Wu, L0_attn_Wq)], axis=1)
    w1 = np.asarray(L0_ffn_w1).reshape(experts, -1, P, hidden).transpose(0, 2, 1, 3).reshape(experts, P, -1)
    w2 = np.asarray(L0_ffn_w2).reshape(experts, -1, P, d).transpose(0, 2, 1, 3).reshape(experts, P, -1)
    arrays = {
        "x_dram": x.reshape(-1, P, 4 * d),
        "w_kvuq_dram": halves(w4),
        "w_o_dram": halves(np.asarray(L0_attn_Wo).T),
        "w_gate_dram": halves(L0_ffn_Wg),
        "w_experts_dram": np.ascontiguousarray(np.concatenate([w1, w2], axis=2)),
        "c_t_dram": halves(np.asarray(L0_c).T),
        "w_mod_dram": halves(L0_wmod),
    }
    nc = bacc.Bacc("TRN2", target_bir_lowering=False, num_devices=1)
    args = [nc.dram_tensor(name, a.shape, mybir.dt.from_np(a.dtype), kind="ExternalInput").ap()
            for name, a in arrays.items()]
    out = nc.dram_tensor("out_dram", (b * l, d), F32, kind="ExternalOutput").ap()
    adaln_block_kernel(nc, *args, out)
    result = run_bass_kernel_spmd(nc, [arrays], core_ids=[0]).results[0]["out_dram"]
    return result.reshape(b, l, d)
```

```python
from contextlib import ExitStack

import concourse.bass as bass
from concourse import mybir

ALU = mybir.AluOpType
ACT = mybir.ActivationFunctionType
AX = mybir.AxisListType
F32 = mybir.dt.float32
F32R = mybir.dt.float32r
BF16 = mybir.dt.bfloat16
U32 = mybir.dt.uint32

P = 128
START = 2


def n(count):
    return count + START


def adaln_block_kernel(nc, x, w_kvuq, w_o, w_gate, w_experts, c_t, w_mod, out):
    NBLK, _, XW = x.shape
    D = w_o.shape[2]
    H = D // P
    T = XW // D
    BLK = T * P
    NB = c_t.shape[2]
    PER = NBLK // NB
    E = w_gate.shape[2]
    EW = w_experts.shape[2]
    F = EW // (2 * H)
    NF = F // P
    CAP = (NBLK * BLK + E - 1) // E
    HEAD = 16
    NH = D // HEAD
    ROW = 2 * D + 8
    GATE0, TOKEN = 2 * D, 2 * D + NB
    FAR = 65536.0
    LN_EPS, RMS_FLOOR = 1e-5, 1e-12
    assert CAP == BLK and H == 2 and T == 4 and PER == 4 and D % HEAD == 0

    dispatched = nc.dram_tensor("dispatched_dram", [E * CAP, ROW], F32, kind="Internal").ap()
    slots = dispatched.rearrange("(e p t) w -> e p (t w)", p=P, t=T)
    mod_dram = nc.dram_tensor("mod_rows_dram", [NB, 4, D], F32, kind="Internal").ap()
    slots_rows = dispatched.rearrange("(e p t) w -> e p t w", p=P, t=T)
    slots_h, slots_x1 = slots_rows[:, :, :, 0:D], slots_rows[:, :, :, D:ROW]
    out_blocks = out.rearrange("(i p t) d -> i p (t d)", p=P, t=T)

    with ExitStack() as ctx:
        def sem(name):
            return ctx.enter_context(nc.semaphore(name))

        bank = [ctx.enter_context(nc.psum_tensor(f"bank{i}", [P, 512], F32)) for i in range(8)]
        X = bank[0:2]
        KV = bank[2:4]
        UB, KVSUM = bank[4], bank[5]
        O = bank[6:8]
        HID = KV + X[0:1]
        Y = [[UB, KVSUM], O]

        def sb(name, shape, dt=F32, stack=ctx):
            return stack.enter_context(nc.sbuf_tensor(name, shape, dt))

        ident = sb("ident", [P, P])
        gb_all = sb("gb_all", [P, NB, D])
        w_raw = [sb("w_raw0", [P, EW]), None]
        w_hi = [sb("w_hi0", [P, EW], F32R), None]
        w_lo = [sb("w_lo0", [P, EW], F32R), None]

        attention = ExitStack()

        def asb(name, shape, dt=F32):
            return sb(name, shape, dt, attention)

        before = asb("before", [P, P], BF16)
        up_to = asb("up_to", [P, P], BF16)
        ones = asb("ones", [P, P], BF16)
        tri = asb("tri", [P, P])
        head_mask = asb("head_mask", [P, P])
        rank = asb("rank", [P, E])
        row_onehot = asb("row_onehot", [P, NB, NB])
        token_no = asb("token_no", [P, T])
        exponent = asb("exponent", [P, T])
        wg = asb("wg", [P, H, E])
        w4_hi = asb("w4_hi", [P, H, 4 * D], F32R)
        w4_lo = asb("w4_lo", [P, H, 4 * D], F32R)
        wo = asb("wo", [P, H, D])
        wog_hi = asb("wog_hi", [P, H, D], F32R)
        wog_lo = asb("wog_lo", [P, H, D], F32R)
        c_raw = asb("c_raw", [P, H, NB])
        c_silu = asb("c_silu", [P, H, NB])
        shift1 = asb("shift1", [P, H, NBLK])
        scale1 = asb("scale1", [P, H, NBLK])
        GA, SB, CB = range(3)
        mods = asb("mods", [P, NB, 3, D])

        xa = asb("xa", [P, T, D])
        stats1 = asb("stats1", [P, T, 6])
        mv1 = asb("mv1", [P, T, 2])
        var1 = asb("var1", [P, T])
        neg_mean1 = asb("neg_mean1", [P, T])
        rstd1 = asb("rstd1", [P, T])
        bias1 = asb("bias1", [P, T])
        xn = asb("xn", [P, T, D])
        h32 = asb("h32", [P, H, BLK])
        h_hi = asb("h_hi", [P, H, BLK], F32R)
        h_lo = asb("h_lo", [P, H, BLK], F32R)
        k_hi = [asb(f"k_hi{i}", [P, D], F32R) for i in range(2)]
        k_lo = [asb(f"k_lo{i}", [P, D], F32R) for i in range(2)]
        v2 = [asb(f"v2{i}", [P, H, 2 * P], F32R) for i in range(2)]
        q_ring = asb("q_ring", [P, PER, H, BLK])
        u_ring = asb("u_ring", [P, PER, T, D])
        kv_a = asb("kv_a", [P, H, P])
        kv_b = asb("kv_b", [P, H, P])
        kv_hi = asb("kv_hi", [P, H, P], F32R)
        kv_lo = asb("kv_lo", [P, H, P], F32R)
        q_hi = asb("q_hi", [P, H, BLK], F32R)
        q_lo = asb("q_lo", [P, H, BLK], F32R)
        sq = asb("sq", [P, T, D])
        ssq = asb("ssq", [P, T * NH])
        rms = asb("rms", [P, T * NH])
        rrms = asb("rrms", [P, T * NH])
        g = asb("g", [P, T, D])
        mod_rows = g[0:NB, :, :]
        g_size, g_sign = sq[0:NB, 0, :], sq[0:NB, 1, :]
        gt_hi = asb("gt_hi", [P, H, BLK], F32R)
        gt_lo = asb("gt_lo", [P, H, BLK], F32R)
        xr = asb("xr", [P, T, D])
        x1 = asb("x1", [P, T, D])
        stats2 = asb("stats2", [P, T, 6])
        mv2 = asb("mv2", [P, T, 2])
        var2 = asb("var2", [P, T])
        rstd2 = asb("rstd2", [P, T])
        xc = asb("xc", [P, T, D])
        wog = xc[:, 0:H, :]
        rows = asb("rows", [P, T, ROW])
        h2t = asb("h2t", [P, H, BLK])
        top = asb("top", [P, T])
        below_top = asb("below_top", [P, T, E])
        prob = asb("prob", [P, T, E])
        psum_ = asb("psum_", [P, T])
        ptop = asb("ptop", [P, T])
        is_top = asb("is_top", [P, T, E])
        ranked = asb("ranked", [P, T, E])
        best = asb("best", [P, T])
        chosen = asb("chosen", [P, T, E], BF16)
        seen = asb("seen", [P, E], BF16)
        newly = asb("newly", [P, E])
        rsum = asb("rsum", [P, T])
        gate = asb("gate", [P, T])
        picked = asb("picked", [P, T, E])
        place = asb("place", [P, T])
        over = asb("over", [P, T])
        first_slot = asb("first_slot", [P, T])
        slot = asb("slot", [P, T])
        slot_no = asb("slot_no", [P, T], U32)
        attention.close()

        w_raw[1] = sb("w_raw1", [P, EW])
        w_hi[1] = sb("w_hi1", [P, EW], F32R)
        w_lo[1] = sb("w_lo1", [P, EW], F32R)
        got_h = [sb(f"got_h{i}", [P, T, D]) for i in range(2)]
        got_x1 = [sb(f"got_x1{i}", [P, T, ROW - D]) for i in range(2)]
        GATE1, TOKEN1 = GATE0 - D, TOKEN - D
        e_hi = [sb(f"e_hi{i}", [P, H, BLK], F32R) for i in range(2)]
        e_lo = [sb(f"e_lo{i}", [P, H, BLK], F32R) for i in range(2)]
        f_hi = [sb(f"f_hi{i}", [P, BLK], F32R) for i in range(3)]
        f_lo = [sb(f"f_lo{i}", [P, BLK], F32R) for i in range(3)]
        factor = sb("factor", [P, T, D])
        res = [sb(f"res{i}", [P, T, D]) for i in range(2)]
        token_at = [sb(f"token_at{i}", [P, T], U32) for i in range(2)]

        mod1_in, w4_in, weights_in = sem("mod1_in"), sem("w4_in"), sem("weights_in")
        x_in, xr_in = sem("x_in"), sem("xr_in")
        zeros_out = sem("zeros_out")
        x1_out = sem("x1_out")
        rows_out = sem("rows_out")
        w_in = [sem("w_in0"), sem("w_in1")]
        h_in = [sem("h_in0"), sem("h_in1")]
        x1_in = [sem("x1_in0"), sem("x1_in1")]
        res_out = sem("res_out")
        rows_zero, consts_pool, consts_dve = sem("rows_zero"), sem("consts_pool"), sem("consts_dve")
        tri_made = sem("tri_made")
        c_ready, mod_t_done, mod_t_read, w4_hi_done, w4_lo_done = (
            sem(s) for s in ("c_ready", "mod_t_done", "mod_t_read", "w4_hi_done", "w4_lo_done"))
        mod_done, g_guard, mod_rows_out, mods_in = (
            sem(s) for s in ("mod_done", "g_guard", "mod_rows_out", "mods_in"))
        h_turned, kv_done, u_done, q_done, kv_summed = (
            sem(s) for s in ("h_turned", "kv_done", "u_done", "q_done", "kv_summed"))
        att_done, g_turned, wo_done, h2_turned, logits_done, places_done = (
            sem(s) for s in ("att_done", "g_turned", "wo_done", "h2_turned", "logits_done", "places_done"))
        e_turned, hid_done, y_part = sem("e_turned"), sem("hid_done"), sem("y_part")
        xn_done, h_scaled, kv_hi_out, u_out, q_out, sq_out, rms_out = (
            sem(s) for s in ("xn_done", "h_scaled", "kv_hi_out", "u_out", "q_out", "sq_out", "rms_out"))
        gt_hi_out, x1_copied, h2t_out, prob_out = (
            sem(s) for s in ("gt_hi_out", "x1_copied", "h2t_out", "prob_out"))
        e_hi_out, f_hi_out, w_hi_out, factor0_out = (
            sem(s) for s in ("e_hi_out", "f_hi_out", "w_hi_out", "factor0_out"))
        stats1_done, mv1_done, var1_done = (
            sem(s) for s in ("stats1_done", "mv1_done", "var1_done"))
        kv_lo_done, q_hi_done, att_kv, att_kv_step, wog_step, wog_done = (
            sem(s) for s in ("kv_lo_done", "q_hi_done", "att_kv", "att_kv_step", "wog_step", "wog_done"))
        gated, ssq_sum, ssq_done, rrms_done, g_done, gt_lo_done, x1_done = (
            sem(s) for s in ("gated", "ssq_sum", "ssq_done", "rrms_done", "g_done", "gt_lo_done", "x1_done"))
        stats2_done, mv2_done, var2_done, xc_done, h2_done = (
            sem(s) for s in ("stats2_done", "mv2_done", "var2_done", "xc_done", "h2_done"))
        route_step, shifted_done, chosen_done, places_read, slot_step, slots_done = (
            sem(s) for s in ("route_step", "shifted_done", "chosen_done", "places_read", "slot_step", "slots_done"))
        e_lo_done, f_lo_done, w_lo_done, factor_step, scaled_done, token_done = (
            sem(s) for s in ("e_lo_done", "f_lo_done", "w_lo_done", "factor_step", "scaled_done", "token_done"))
        stats1_seen, stats2_seen, scatter_turn = (
            sem(s) for s in ("stats1_seen", "stats2_seen", "scatter_turn"))
        rstd1_step, rstd1_done, h_lo_done, q_lo_done, rstd2_done, res_done = (
            sem(s) for s in ("rstd1_step", "rstd1_done", "h_lo_done", "q_lo_done", "rstd2_done", "res_done"))

        block = ctx.enter_context(nc.Block())

        def run_steps(eng, step, batch_end, last):
            step(0, 0, 0, p1=True, p2=False, p3=False, ahead=2)
            with eng.Fori(1, PER) as r:
                step(r, 0, r, p1=True, p2=False, p3=False, ahead=2)
            batch_end(0)
            step(PER, 1, 0, p1=True, p2=True, p3=False, ahead=2)
            with eng.Fori(1, NB - 1) as b:
                with eng.Fori(1, PER) as r:
                    step(b * PER + r, b, r, p1=True, p2=True, p3=True, ahead=2)
                batch_end(b)
                step(b * PER + PER, b + 1, 0, p1=True, p2=True, p3=True, ahead=2)
            with eng.Fori(1, PER - 2) as r:
                step(r + (NB - 1) * PER, NB - 1, r, p1=True, p2=True, p3=True, ahead=2)
            step(NBLK - 2, NB - 1, PER - 2, p1=True, p2=True, p3=True, ahead=1)
            step(NBLK - 1, NB - 1, PER - 1, p1=True, p2=True, p3=True, ahead=0)
            batch_end(NB - 1)
            with eng.Fori(0, PER - 1) as r:
                step(r + NBLK, NB, r, p1=False, p2=True, p3=True, ahead=0)
            step(NBLK + PER - 1, NB, PER - 1, p1=False, p2=True, p3=True, ahead=0)
            last(NBLK - 1)

        def first_step(i):
            return isinstance(i, int) and i == 0

        def has_next(j):
            return not (isinstance(j, int) and j == NBLK - 1)

        def run_experts(eng, body, last):
            body(0, 0, 0, False, True)
            body(1, 0, 1, True, True)
            with eng.Fori(1, E // 2 - 1) as pair:
                body(2 * pair, pair, 0, True, True)
                body(2 * pair + 1, pair, 1, True, True)
            body(E - 2, E // 2 - 1, 0, True, True)
            body(E - 1, E // 2 - 1, 1, True, False)
            last(E - 1, E // 2 - 1, 1)

        def chunk_freed(e, f):
            return NF * e + (f - 2 if f >= 3 else (-1, 0, 0)[f])

        def start_counts(eng, *sems):
            for s in sems:
                eng.sem_inc(s, START)

        @block.sync
        def _(sp):
            sp.dma_start(xa[:, :, :], x[0]).then_inc(x_in, 16)
            wm = w_raw[0][:, 0:H * 6 * D].rearrange("p (k w) -> p k w", k=H)
            sp.dma_start(wm[:, :, 0:2 * D], w_mod[:, :, 0:2 * D]).then_inc(mod1_in, 16)
            sp.dma_start(q_ring[:, 0:2, :, :], w_kvuq).then_inc(w4_in, 16)
            sp.dma_start(wm[:, :, 2 * D:6 * D], w_mod[:, :, 2 * D:6 * D]).then_inc(weights_in, 16)
            sp.dma_start(wo[:, :, :], w_o).then_inc(weights_in, 16)

            sp.wait_ge(rows_zero, 1)

            def zero_slots(s):
                for e in range(E // NB):
                    sp.dma_start(slots[s * (E // NB) + e], rows[:, :, :]).then_inc(zeros_out, 16)

            def load_x(i):
                sp.wait_ge(xn_done, n(i))
                sp.dma_start(xa[:, :, :], x[i]).then_inc(x_in, 16)

            def swap_x1(j, more):
                sp.wait_ge(x1_done, n(2 * j + 2))
                sp.dma_start(out_blocks[j], x1[:, :, :]).then_inc(x1_out, 16)
                if more:
                    sp.dma_start(xr[:, :, :], x[j + 1]).then_inc(xr_in, 16)

            load_x(1)
            load_x(2)
            sp.wait_ge(g_guard, 6)
            sp.dma_start(mod_dram, mod_rows).then_inc(mod_rows_out, 16)
            sp.wait_ge(mod_rows_out, 16)

            def spread_mods(b):
                row = mod_dram[bass.ds(b, 1)]
                sp.dma_start(mods[:, bass.ds(b, 1), :, :],
                             row[:, 0:3, :].unsqueeze(0).to_broadcast([P, 1, 3, D])).then_inc(mods_in, 16)
                sp.dma_start(gb_all[:, bass.ds(b, 1), :],
                             row[:, 3, :].unsqueeze(0).to_broadcast([P, 1, D])).then_inc(mods_in, 16)

            with sp.Fori(0, NB) as s:
                spread_mods(s)
                zero_slots(s)
                load_x(s + 3)
            sp.dma_start(xr[:, :, :], x[0]).then_inc(xr_in, 16)
            sp.wait_ge(mod_done, 2)
            sp.dma_start(w_raw[0][:, :], w_experts[0]).then_inc(w_in[0], 16)
            swap_x1(0, True)
            with sp.Fori(PER + 1, NBLK - 2) as s:
                load_x(s + 2)
                swap_x1(s - PER, True)
            with sp.Fori(NBLK - 2 - PER, NBLK - 1) as j:
                swap_x1(j, True)
            swap_x1(NBLK - 1, False)

            sp.wait_ge(x1_out, 16 * NBLK)
            sp.wait_ge(rows_out, 16 * (NBLK * T + 1))

            def load_h(e, y):
                if not (isinstance(e, int) and e < 2):
                    sp.wait_ge(e_turned, n(2 * (e - 1)))
                sp.dma_start(got_h[y][:, :, :], slots_h[e]).then_inc(h_in[y], 16)

            def load_x1(e, y):
                if not (isinstance(e, int) and e < 2):
                    sp.wait_ge(res_done, n(e - 1))
                sp.dma_start(got_x1[y][:, :, :], slots_x1[e]).then_inc(x1_in[y], 16)

            def load_w(e, y):
                if not (isinstance(e, int) and e < 2):
                    sp.wait_ge(w_hi_out, n(4 * (e - 1)))
                    sp.wait_ge(w_lo_done, n(4 * (e - 1)))
                sp.dma_start(w_raw[y][:, :], w_experts[e]).then_inc(w_in[y], 16)

            load_h(0, 0)
            load_w(1, 1)
            load_h(1, 1)
            load_x1(0, 0)
            load_x1(1, 1)
            load_h(2, 0)
            load_w(2, 0)
            with sp.Fori(1, E // 2 - 1) as pair:
                load_x1(2 * pair, 0)
                load_h(2 * pair + 1, 1)
                load_w(2 * pair + 1, 1)
                load_x1(2 * pair + 1, 1)
                load_h(2 * pair + 2, 0)
                load_w(2 * pair + 2, 0)
            load_x1(E - 2, 0)
            load_h(E - 1, 1)
            load_w(E - 1, 1)
            load_x1(E - 1, 1)
            sp.wait_ge(res_out, 16 * (E * T + 1))

        @block.gpsimd
        def _(pool):
            start_counts(pool, rstd1_step, rstd1_done, h_lo_done, q_lo_done, rstd2_done, res_done)
            def rstd_first(i):
                pool.wait_ge(var1_done, n(i + 1))
                nc.gpsimd.tensor_tensor(rstd1[:, :], var1[:, :], exponent[:, :], ALU.pow).then_inc(rstd1_step, 1)
                pool.wait_ge(rstd1_step, n(i + 1))
                nc.gpsimd.tensor_tensor(bias1[:, :], neg_mean1[:, :], rstd1[:, :], ALU.mult).then_inc(rstd1_done, 1)

            pool.dma_start(c_raw[:, :, :], c_t).then_inc(res_out, 16)
            pool.dma_start(wg[:, :, :], w_gate).then_inc(rows_out, 16)
            nc.gpsimd.memset(ident[:, :], 0.0).then_inc(tri_made, 1)
            nc.gpsimd.memset(tri[:, :], 1.0).then_inc(tri_made, 1)
            nc.gpsimd.memset(head_mask[:, :], 1.0 / HEAD).then_inc(tri_made, 1)
            nc.gpsimd.memset(row_onehot[:, :, :], 0.0).then_inc(tri_made, 1)
            pool.wait_ge(tri_made, 4)
            nc.gpsimd.affine_select(out=ident[:, :], in_=ident[:, :], compare_op=ALU.not_equal, fill=1.0,
                                    base=0, pattern=[[-1, P]], channel_multiplier=1).then_inc(consts_pool, 1)
            pool.wait_ge(consts_dve, 1)
            rstd_first(0)
            nc.gpsimd.memset(rows[:, :, :], 0.0).then_inc(rows_zero, 1)
            per_half = [[-HEAD, P // HEAD], [0, HEAD]]
            nc.gpsimd.affine_select(out=head_mask[:, :], in_=head_mask[:, :], compare_op=ALU.is_ge, fill=0.0,
                                    base=0, pattern=per_half, channel_multiplier=1).then_inc(tri_made, 1)
            pool.wait_ge(tri_made, 5)
            nc.gpsimd.affine_select(out=head_mask[:, :], in_=head_mask[:, :], compare_op=ALU.is_ge, fill=0.0,
                                    base=HEAD - 1, pattern=[[HEAD, P // HEAD], [0, HEAD]],
                                    channel_multiplier=-1).then_inc(consts_pool, 1)
            nc.gpsimd.affine_select(out=row_onehot[:, :, :], in_=row_onehot[:, :, :], compare_op=ALU.not_equal,
                                    fill=1.0, base=0, pattern=[[1, NB], [-1, NB]],
                                    channel_multiplier=0).then_inc(consts_pool, 1)
            nc.gpsimd.iota(rank[:, :], pattern=[[-1, E]], base=E, channel_multiplier=0,
                           allow_small_or_imprecise_dtypes=True).then_inc(consts_pool, 1)
            nc.gpsimd.iota(token_no[:, :], pattern=[[1, T]], base=-int(FAR), channel_multiplier=T,
                           allow_small_or_imprecise_dtypes=True).then_inc(consts_pool, 1)
            nc.gpsimd.affine_select(out=before[:, :], in_=tri[:, :], compare_op=ALU.is_gt, fill=0.0,
                                    base=0, pattern=[[1, P]], channel_multiplier=-1).then_inc(consts_pool, 1)
            nc.gpsimd.affine_select(out=up_to[:, :], in_=tri[:, :], compare_op=ALU.is_ge, fill=0.0,
                                    base=0, pattern=[[1, P]], channel_multiplier=-1).then_inc(consts_pool, 1)

            def low_part(i):
                for c in range(H):
                    pool.wait_ge(h_scaled, n(2 * i + c + 1))
                    nc.gpsimd.tensor_tensor(h_lo[:, c, :], h32[:, c, :], h_hi[:, c, :],
                                            ALU.subtract).then_inc(h_lo_done, 1)

            low_part(0)
            rstd_first(1)

            def step(i, b, r, p1, p2, p3, ahead):
                j, k = i - PER, i - PER - 1
                if p3:
                    rstd_second(k)
                if p2 and has_next(j):
                    split_q(j + 1, (r + 1) % PER)
                if ahead == 2:
                    rstd_first(i + 2)
                if ahead:
                    low_part(i + 1)
                if p3:
                    scatter_rows(k)

            def split_q(j, r):
                for c in range(H):
                    pool.wait_ge(q_hi_done, n(2 * j + c + 1))
                    nc.gpsimd.tensor_tensor(q_lo[:, c, :], q_ring[:, r, c, :], q_hi[:, c, :],
                                            ALU.subtract).then_inc(q_lo_done, 1)

            def batch_end(b):
                if isinstance(b, int) and b == 0:
                    split_q(0, 0)

            def rstd_second(k):
                pool.wait_ge(var2_done, n(k + 1))
                nc.gpsimd.tensor_tensor(rstd2[:, :], var2[:, :], exponent[:, :], ALU.pow).then_inc(rstd2_done, 1)

            def scatter_rows(k):
                pool.wait_ge(slots_done, n(k + 1))
                pool.wait_ge(x1_copied, n(k + 1))
                pool.wait_ge(zeros_out, 16 * E)
                pool.wait_ge(rows_out, 16 * (T * k + 1))
                pool.sem_inc(scatter_turn, 1)
                for t in range(T):
                    nc.gpsimd.indirect_dma_start(
                        dispatched, bass.IndirectOffsetOnAxis(ap=slot_no[:, t:t + 1], axis=0),
                        rows[:, t, :], None, bounds_check=E * CAP - 1, oob_is_err=False).then_inc(rows_out, 16)

            def last(k):
                rstd_second(k)
                scatter_rows(k)

            run_steps(pool, step, batch_end, last)

            def finish(e, pair, y):
                pool.wait_ge(scaled_done, n(e + 1))
                pool.wait_ge(x1_in[y], 16 * (pair + 1))
                nc.gpsimd.tensor_tensor(res[y][:, :, :], res[y][:, :, :], got_x1[y][:, :, 0:D],
                                        ALU.add).then_inc(res_done, 1)
                pool.wait_ge(token_done, n(e + 1))
                pool.wait_ge(res_done, n(e + 1))
                pool.wait_ge(x1_out, 16 * NBLK)
                pool.wait_ge(res_out, 16 * (T * e + 1))
                pool.sem_inc(scatter_turn, 1)
                for t in range(T):
                    nc.gpsimd.indirect_dma_start(
                        out, bass.IndirectOffsetOnAxis(ap=token_at[y][:, t:t + 1], axis=0),
                        res[y][:, t, :], None, bounds_check=NBLK * BLK - 1, oob_is_err=False).then_inc(res_out, 16)

            def body(e, pair, y, prev, nxt):
                if prev:
                    finish(e - 1, pair if y else pair - 1, 1 - y)

            run_experts(pool, body, finish)

        @block.scalar
        def _(act):
            start_counts(act, xn_done, q_hi_done, h_scaled, kv_hi_out, u_out, q_out, sq_out, rms_out, gt_hi_out, x1_copied,
                         h2t_out, prob_out, e_hi_out, f_hi_out, w_hi_out, factor0_out)
            act.wait_ge(res_out, 16)
            nc.scalar.activation(c_silu[:, :, :], c_raw[:, :, :], ACT.Silu).then_inc(c_ready, 1)
            act.wait_ge(w4_in, 16)
            for c in range(H):
                nc.scalar.activation(w4_hi[:, c, :], q_ring[:, c, :, :].rearrange("p h w -> p (h w)"),
                                     ACT.Copy).then_inc(w4_hi_done, 1)

            def normalise_first(i):
                act.wait_ge(rstd1_done, n(i + 1))
                act.wait_ge(h_turned, n(2 * i))
                for t in range(T):
                    ins = nc.scalar.activation(xn[:, t, :], xa[:, t, :], ACT.Identity, bias=bias1[:, t:t + 1],
                                               scale=rstd1[:, t:t + 1])
                ins.then_inc(xn_done, 1)

            def scale_h(i):
                act.wait_ge(q_done, n(2 * i))
                act.wait_ge(h_lo_done, n(2 * i))
                act.wait_ge(mod_t_read, 2)
                for c in range(H):
                    act.wait_ge(h_turned, n(2 * i + c + 1))
                    for h in (h32, h_hi):
                        ins = nc.scalar.activation(h[:, c, :], X[c][:, :], ACT.Identity,
                                                   bias=shift1[:, c, bass.ds(i, 1)], scale=scale1[:, c, bass.ds(i, 1)])
                    ins.then_inc(h_scaled, 1)

            def q_high(j, r):
                act.wait_ge(att_done, n(2 * j))
                act.wait_ge(q_out, n(2 * j + 2))
                for c in range(H):
                    nc.scalar.activation(q_hi[:, c, :], q_ring[:, r, c, :], ACT.Copy).then_inc(q_hi_done, 1)

            def kv_high(i, t):
                act.wait_ge(kv_done, n(4 * i + t + 1))
                act.wait_ge(kv_summed, n(4 * i + t - 1))
                nc.scalar.activation(k_hi[t % 2][:, :], KV[t % 2][:, 0:D], ACT.Relu)
                nc.scalar.activation(v2[t % 2][:, :, 0:P], KV[t % 2][:, D:2 * D].rearrange("p (c w) -> p c w", c=H),
                                     ACT.Copy).then_inc(kv_hi_out, 1)

            def silu_u(i, r, pr):
                act.wait_ge(u_done, n(2 * i + pr + 1))
                nc.scalar.activation(u_ring[:, r, 2 * pr:2 * pr + 2, :].rearrange("p t d -> p (t d)"),
                                     UB[:, :], ACT.Silu).then_inc(u_out, 1)

            def copy_x1(k):
                act.wait_ge(x1_done, n(2 * k + 2))
                act.wait_ge(rows_out, 16 * (T * k + 1))
                act.wait_ge(zeros_out, 16 * E)
                nc.scalar.activation(rows[:, :, D:2 * D], x1[:, :, :], ACT.Copy).then_inc(x1_copied, 1)

            def keep_h2t(k):
                for c in range(H):
                    act.wait_ge(h2_turned, n(2 * k + c + 1))
                    act.wait_ge(logits_done, n(k))
                    nc.scalar.activation(h2t[:, c, :], X[c][:, :], ACT.Copy).then_inc(h2t_out, 1)

            def exp_logits(k):
                act.wait_ge(shifted_done, n(k + 1))
                act.wait_ge(slots_done, n(k))
                nc.scalar.activation(prob[:, :, :], below_top[:, :, :], ACT.Exp).then_inc(prob_out, 1)

            normalise_first(0)
            scale_h(0)

            def step(i, b, r, p1, p2, p3, ahead):
                j, k = i - PER, i - PER - 1
                if p1:
                    kv_high(i, 0)
                if ahead:
                    normalise_first(i + 1)
                if p2:
                    for pr in range(2):
                        act.wait_ge(att_done, n(2 * j + pr + 1))
                        act.wait_ge(ssq_sum, n(j))
                        nc.scalar.activation(sq[:, 2 * pr:2 * pr + 2, :].rearrange("p t d -> p (t d)"),
                                             O[pr][:, :], ACT.Square).then_inc(sq_out, 1)
                    if has_next(j):
                        q_high(j + 1, (r + 1) % PER)
                if p1:
                    kv_high(i, 1)
                    if p2:
                        act.wait_ge(gated, n(2 * j + 2))
                    silu_u(i, r, 0)
                if p2:
                    act.wait_ge(ssq_done, n(j + 1))
                    nc.scalar.activation(rms[:, :], ssq[:, :], ACT.Sqrt, scale=1.0 / HEAD).then_inc(rms_out, 1)
                if p1:
                    kv_high(i, 2)
                if p3:
                    copy_x1(k)
                if p1:
                    kv_high(i, 3)
                if p3:
                    keep_h2t(k)
                    if not p1:
                        exp_logits(k)
                if p1:
                    keep_q(i, j, r, 0, p2)
                if p2:
                    for c in range(H):
                        act.wait_ge(g_turned, n(2 * j + c + 1))
                        act.wait_ge(wo_done, n(2 * j))
                        nc.scalar.activation(gt_hi[:, c, :], X[c][:, :], ACT.Copy).then_inc(gt_hi_out, 1)
                if p3 and p1:
                    exp_logits(k)
                if p1:
                    silu_u(i, r, 1)
                    keep_q(i, j, r, 1, p2)
                if ahead:
                    scale_h(i + 1)

            def keep_q(i, j, r, c, p2):
                act.wait_ge(q_done, n(2 * i + c + 1))
                if p2:
                    act.wait_ge(q_lo_done, n(2 * j + 2))
                else:
                    act.wait_ge(w4_lo_done, 2)
                nc.scalar.activation(q_ring[:, r, c, :], KV[c][:, :], ACT.Relu).then_inc(q_out, 1)

            def batch_end(b):
                if isinstance(b, int) and b == 0:
                    q_high(0, 0)

            def last(k):
                copy_x1(k)
                keep_h2t(k)
                exp_logits(k)

            run_steps(act, step, batch_end, last)

            def split_w(e, pair, y, piece):
                act.wait_ge(w_in[y], 16 * (pair + 1))
                act.wait_ge(hid_done if piece < 2 else y_part, n(NF * (e - 1)))
                part = slice(piece * EW // 4, (piece + 1) * EW // 4)
                nc.scalar.activation(w_hi[y][:, part], w_raw[y][:, part], ACT.Copy).then_inc(w_hi_out, 1)

            def rows_high(e, y, c):
                act.wait_ge(e_turned, n(2 * e + c + 1))
                act.wait_ge(hid_done, n(NF * (e - 1)))
                nc.scalar.activation(e_hi[y][:, c, :], X[1][:, :], ACT.Copy).then_inc(e_hi_out, 1)

            act.wait_ge(mods_in, 32 * NB)
            act.wait_ge(w_in[0], 16)
            for piece in range(4):
                part = slice(piece * EW // 4, (piece + 1) * EW // 4)
                nc.scalar.activation(w_hi[0][:, part], w_raw[0][:, part], ACT.Copy).then_inc(w_hi_out, 1)
            for c in range(H):
                act.wait_ge(e_turned, n(c + 1))
                nc.scalar.activation(e_hi[0][:, c, :], X[1][:, :], ACT.Copy).then_inc(e_hi_out, 1)

            def body(e, pair, y, prev, nxt):
                next_pair = pair + 1 if y else pair
                for f in range(NF):
                    act.wait_ge(hid_done, n(NF * e + f + 1))
                    act.wait_ge(y_part, n(chunk_freed(e, f)))
                    nc.scalar.activation(f_hi[f % 3][:, :], HID[f % 3][:, :], ACT.Relu).then_inc(f_hi_out, 1)
                    if nxt and f < 4:
                        split_w(e + 1, next_pair, 1 - y, f)
                    if f == 3:
                        act.wait_ge(scaled_done, n(e))
                        act.wait_ge(x1_in[y], 16 * (pair + 1))
                        for t in range(T):
                            ins = nc.scalar.activation(factor[:, t, :], gb_all[:, 0, :], ACT.Copy,
                                                       scale=got_x1[y][:, t, GATE1:GATE1 + 1])
                        ins.then_inc(factor0_out, 1)
                    if nxt and f in (4, 6):
                        rows_high(e + 1, 1 - y, (f - 4) // 2)

            run_experts(act, body, lambda e, pair, y: None)

        @block.vector
        def _(dve):
            start_counts(dve, stats1_done, mv1_done, var1_done, kv_lo_done, places_read,
                         att_kv, att_kv_step, wog_step, wog_done, gated, ssq_sum, ssq_done, rrms_done, g_done,
                         gt_lo_done, x1_done, stats2_done, mv2_done, var2_done, xc_done, h2_done,
                         route_step, shifted_done, chosen_done, slot_step, slots_done,
                         e_lo_done, f_lo_done, w_lo_done, factor_step, scaled_done, token_done)
            nc.vector.memset(exponent[:, :], -0.5).then_inc(consts_dve, 1)
            nc.vector.memset(ones[:, :], 1.0).then_inc(consts_dve, 1)
            nc.vector.memset(seen[:, :], 0.0).then_inc(consts_dve, 1)

            def norm_stats_first(i):
                dve.wait_ge(x_in, 16 * (i + 1))
                for t in range(T):
                    ins = nc.vector.bn_stats(stats1[:, t, :], xa[:, t, :])
                ins.then_inc(stats1_done, 1)
                dve.wait_ge(stats1_done, n(i + 1))
                dve.sem_inc(stats1_seen, 1)
                for t in range(T):
                    ins = nc.vector.bn_aggr(mv1[:, t, :], stats1[:, t, :])
                ins.then_inc(mv1_done, 1)
                dve.wait_ge(mv1_done, n(i + 1))
                nc.vector.tensor_scalar(neg_mean1[:, :], mv1[:, :, 0], -1.0, None, ALU.mult)
                nc.vector.tensor_scalar(var1[:, :], mv1[:, :, 1], LN_EPS, None, ALU.add).then_inc(var1_done, 1)

            norm_stats_first(0)
            for c in range(H):
                dve.wait_ge(w4_hi_done, c + 1)
                nc.vector.tensor_tensor(w4_lo[:, c, :], q_ring[:, c, :, :].rearrange("p h w -> p (h w)"),
                                        w4_hi[:, c, :], ALU.subtract).then_inc(w4_lo_done, 1)
            dve.wait_ge(mod_t_done, 1)
            by_row = UB[:, 0:2 * H * NB].rearrange("p (a c b) -> p a c b", a=2, c=H)
            nc.vector.tensor_copy(shift1[:, :, :].rearrange("p c (b r) -> p c b r", r=PER),
                                  by_row[:, 0, :, :].unsqueeze(3).to_broadcast([P, H, NB, PER])).then_inc(mod_t_read, 1)
            nc.vector.tensor_scalar(scale1[:, :, :].rearrange("p c (b r) -> p c b r", r=PER),
                                    by_row[:, 1, :, :].unsqueeze(3).to_broadcast([P, H, NB, PER]),
                                    1.0, None, ALU.add).then_inc(mod_t_read, 1)
            norm_stats_first(1)
            def kv_low(i, t):
                dve.wait_ge(kv_hi_out, n(4 * i + t + 1))
                nc.vector.scalar_tensor_tensor(out=k_lo[t % 2][:, :], in0=KV[t % 2][:, 0:D], scalar=0.0,
                                               in1=k_hi[t % 2][:, :], op0=ALU.max, op1=ALU.subtract)
                nc.vector.tensor_tensor(v2[t % 2][:, :, P:2 * P],
                                        KV[t % 2][:, D:2 * D].rearrange("p (c w) -> p c w", c=H),
                                        v2[t % 2][:, :, 0:P], ALU.subtract).then_inc(kv_lo_done, 1)

            def batch_end(b):
                dve.wait_ge(kv_summed, n(4 * PER * (b + 1)))
                dve.wait_ge(consts_pool, 7)
                both = KVSUM[:, :].rearrange("p (c a w) -> p c a w", c=H, a=2)
                mask = head_mask[:, :].unsqueeze(1).to_broadcast([P, H, P])
                dve.wait_ge(att_done, n(2 * PER * b))
                nc.vector.tensor_tensor(kv_a[:, :, :], both[:, :, 0, :], mask, ALU.mult)
                nc.vector.tensor_tensor(kv_b[:, :, :], both[:, :, 1, :], mask, ALU.mult).then_inc(att_kv_step, 1)
                dve.wait_ge(att_kv_step, n(3 * b + 1))
                nc.vector.tensor_tensor(kv_a[:, :, :], kv_a[:, :, :], kv_b[:, :, :], ALU.add).then_inc(att_kv_step, 1)
                dve.wait_ge(att_kv_step, n(3 * b + 2))
                nc.vector.tensor_copy(kv_hi[:, :, :], kv_a[:, :, :]).then_inc(att_kv_step, 1)
                dve.wait_ge(att_kv_step, n(3 * b + 3))
                nc.vector.tensor_tensor(kv_lo[:, :, :], kv_a[:, :, :], kv_hi[:, :, :],
                                        ALU.subtract).then_inc(att_kv, 1)
                dve.wait_ge(wo_done, n(2 * PER * b))
                dve.wait_ge(mods_in, 32 * NB)
                ga = mods[:, b, GA, :].unsqueeze(1).to_broadcast([P, H, D])
                nc.vector.tensor_tensor(wog, wo[:, :, :], ga, ALU.mult).then_inc(wog_step, 1)
                dve.wait_ge(wog_step, n(2 * b + 1))
                nc.vector.tensor_copy(wog_hi[:, :, :], wog).then_inc(wog_step, 1)
                dve.wait_ge(wog_step, n(2 * b + 2))
                nc.vector.tensor_tensor(wog_lo[:, :, :], wog, wog_hi[:, :, :],
                                        ALU.subtract).then_inc(wog_done, 1)

            def make_mods():
                for half in range(2):
                    dve.wait_ge(mod_done, half + 1)
                    halves = O[half][0:NB, 0:D], O[half][0:NB, D:2 * D]
                    g_psum, s_psum = halves[half], halves[1 - half]
                    nc.vector.tensor_scalar(g_size, g_psum, 0.25, None, ALU.max)
                    nc.vector.tensor_scalar(g_sign, g_psum, 0.0, 2.0, ALU.is_ge, ALU.mult).then_inc(g_guard, 1)
                    nc.vector.tensor_scalar(mod_rows[:, 1 + half, :], s_psum, 1.0 if half else 0.0, None, ALU.add)
                    dve.wait_ge(g_guard, 3 * half + 1)
                    nc.vector.scalar_tensor_tensor(out=g_size, in0=g_psum, scalar=-1.0, in1=g_size,
                                                   op0=ALU.mult, op1=ALU.max).then_inc(g_guard, 1)
                    dve.wait_ge(g_guard, 3 * half + 2)
                    nc.vector.scalar_tensor_tensor(out=mod_rows[:, 3 * half, :], in0=g_sign, scalar=-1.0, in1=g_size,
                                                   op0=ALU.add, op1=ALU.mult).then_inc(g_guard, 1)
                    dve.wait_ge(g_guard, 3 * half + 3)

            def stats_second(k):
                dve.wait_ge(x1_done, n(2 * k + 2))
                for t in range(T):
                    ins = nc.vector.bn_stats(stats2[:, t, :], x1[:, t, :])
                ins.then_inc(stats2_done, 1)
                dve.wait_ge(stats2_done, n(k + 1))
                dve.sem_inc(stats2_seen, 1)
                for t in range(T):
                    ins = nc.vector.bn_aggr(mv2[:, t, :], stats2[:, t, :])
                ins.then_inc(mv2_done, 1)
                dve.wait_ge(mv2_done, n(k + 1))
                nc.vector.tensor_scalar(var2[:, :], mv2[:, :, 1], LN_EPS, None, ALU.add).then_inc(var2_done, 1)

            def centre(k):
                for t in range(T):
                    ins = nc.vector.scalar_tensor_tensor(out=xc[:, t, :], in0=x1[:, t, :], scalar=mv2[:, t, 0:1],
                                                         in1=mods[:, row_of(k), CB, :], op0=ALU.subtract, op1=ALU.mult)
                ins.then_inc(xc_done, 1)

            def row_of(k):
                return k // PER

            def modulate(k):
                dve.wait_ge(rstd2_done, n(k + 1))
                dve.wait_ge(xc_done, n(k + 1))
                dve.wait_ge(rows_out, 16 * (T * k + 1))
                dve.wait_ge(zeros_out, 16 * E)
                for t in range(T):
                    ins = nc.vector.scalar_tensor_tensor(out=rows[:, t, 0:D], in0=xc[:, t, :], scalar=rstd2[:, t:t + 1],
                                                         in1=mods[:, row_of(k), SB, :], op0=ALU.mult, op1=ALU.add)
                ins.then_inc(h2_done, 1)

            ROUTE = 9

            def wide(ap):
                return ap.unsqueeze(2).to_broadcast([P, T, E])

            def shift_logits(k, bank):
                dve.wait_ge(logits_done, n(k + 1))
                logits = bank[:, 0:T * E].rearrange("p (t e) -> p t e", t=T)
                nc.vector.tensor_reduce(top[:, :], logits, AX.X, ALU.max).then_inc(route_step, 1)
                dve.wait_ge(route_step, n(ROUTE * k + 1))
                nc.vector.tensor_tensor(below_top[:, :, :], logits, wide(top[:, :]), ALU.subtract).then_inc(shifted_done, 1)

            def choose(k):
                dve.wait_ge(prob_out, n(k + 1))
                nc.vector.tensor_reduce(ptop[:, :], prob[:, :, :], AX.X, ALU.max).then_inc(route_step, 1)
                nc.vector.tensor_reduce(psum_[:, :], prob[:, :, :], AX.X, ALU.add).then_inc(route_step, 1)
                dve.wait_ge(route_step, n(ROUTE * k + 2))
                nc.vector.tensor_tensor(is_top[:, :, :], prob[:, :, :], wide(ptop[:, :]),
                                        ALU.is_equal).then_inc(route_step, 1)
                dve.wait_ge(route_step, n(ROUTE * k + 4))
                nc.vector.tensor_tensor(ranked[:, :, :], is_top[:, :, :],
                                        rank[:, :].unsqueeze(1).to_broadcast([P, T, E]), ALU.mult).then_inc(route_step, 1)
                dve.wait_ge(route_step, n(ROUTE * k + 5))
                nc.vector.tensor_reduce(best[:, :], ranked[:, :, :], AX.X, ALU.max).then_inc(route_step, 1)
                nc.vector.reciprocal(rsum[:, :], psum_[:, :])
                dve.wait_ge(route_step, n(ROUTE * k + 6))
                nc.vector.tensor_tensor(chosen[:, :, :], ranked[:, :, :], wide(best[:, :]),
                                        ALU.is_equal).then_inc(chosen_done, 1)
                dve.wait_ge(chosen_done, n(k + 1))
                nc.vector.tensor_tensor(gate[:, :], ptop[:, :], rsum[:, :], ALU.mult).then_inc(route_step, 1)
                nc.vector.tensor_copy(rows[:, :, TOKEN], token_no[:, :])
                dve.wait_ge(route_step, n(ROUTE * k + 7))
                nc.vector.tensor_tensor(rows[:, :, GATE0:GATE0 + NB],
                                        row_onehot[:, row_of(k), :].unsqueeze(1).to_broadcast([P, T, NB]),
                                        gate[:, :].unsqueeze(2).to_broadcast([P, T, NB]), ALU.mult)
                nc.vector.tensor_scalar(first_slot[:, :], best[:, :], -float(CAP), float(E * CAP), ALU.mult, ALU.add)
                nc.vector.tensor_reduce(newly[:, :], chosen[:, :, :].rearrange("p t e -> p e t"),
                                        AX.X, ALU.add).then_inc(route_step, 1)
                nc.vector.tensor_scalar(token_no[:, :], token_no[:, :], float(BLK), None, ALU.add)

            def number_slots(k, bank):
                dve.wait_ge(places_done, n(k + 1))
                places = bank[:, 0:T * E].rearrange("p (t e) -> p t e", t=T)
                nc.vector.tensor_tensor(picked[:, :, :], places, chosen[:, :, :], ALU.mult).then_inc(places_read, 1)
                dve.wait_ge(route_step, n(ROUTE * k + 8))
                nc.vector.tensor_tensor(seen[:, :], seen[:, :], newly[:, :], ALU.add)
                dve.wait_ge(places_read, n(k + 1))
                nc.vector.tensor_reduce(place[:, :], picked[:, :, :], AX.X, ALU.add).then_inc(route_step, 1)
                dve.wait_ge(route_step, n(ROUTE * k + 9))
                nc.vector.tensor_scalar(over[:, :], place[:, :], float(CAP), FAR, ALU.is_ge, ALU.mult)
                nc.vector.tensor_tensor(slot[:, :], place[:, :], first_slot[:, :], ALU.add).then_inc(slot_step, 1)
                dve.wait_ge(slot_step, n(k + 1))
                nc.vector.tensor_tensor(slot_no[:, :], slot[:, :], over[:, :], ALU.add).then_inc(slots_done, 1)

            def gate_attention(j, r):
                for pr in range(2):
                    dve.wait_ge(att_done, n(2 * j + pr + 1))
                    dve.wait_ge(g_turned, n(2 * j))
                    dve.wait_ge(u_out, n(2 * j + pr + 1))
                    dve.wait_ge(sq_out, n(2 * j + pr + 1))
                    nc.vector.tensor_tensor(g[:, 2 * pr:2 * pr + 2, :].rearrange("p t d -> p (t d)"), O[pr][:, :],
                                            u_ring[:, r, 2 * pr:2 * pr + 2, :].rearrange("p t d -> p (t d)"),
                                            ALU.mult).then_inc(gated, 1)
                nc.vector.tensor_reduce(ssq[:, :], sq[:, :, :].rearrange("p t (h w) -> p (t h) w", w=HEAD),
                                        AX.X, ALU.add).then_inc(ssq_sum, 1)
                dve.wait_ge(ssq_sum, n(j + 1))
                nc.vector.tensor_scalar(ssq[:, :], ssq[:, :], HEAD * RMS_FLOOR ** 2, None,
                                        ALU.max).then_inc(ssq_done, 1)

            def norm_heads(j):
                dve.wait_ge(rms_out, n(j + 1))
                nc.vector.reciprocal(rrms[:, :], rms[:, :]).then_inc(rrms_done, 1)
                dve.wait_ge(rrms_done, n(j + 1))
                heads = g[:, :, :].rearrange("p t (h w) -> p (t h) w", w=HEAD)
                nc.vector.tensor_tensor(heads, heads, rrms[:, :].unsqueeze(2).to_broadcast([P, T * NH, HEAD]),
                                        ALU.mult).then_inc(g_done, 1)

            def step(i, b, r, p1, p2, p3, ahead):
                j, k = i - PER, i - PER - 1
                if p3:
                    stats_second(k)
                if p1:
                    kv_low(i, 0)
                if p3 and p1:
                    centre(k)
                if p2:
                    gate_attention(j, r)
                if p3 and not p1:
                    centre(k)
                if p1:
                    kv_low(i, 1)
                if p3:
                    modulate(k)
                if p1:
                    kv_low(i, 2)
                if p2:
                    norm_heads(j)
                if p1:
                    kv_low(i, 3)
                if first_step(i):
                    make_mods()
                if p3 and not p1:
                    shift_logits(k, KV[0])
                    choose(k)
                if p2:
                    for c in range(H):
                        dve.wait_ge(gt_hi_out, n(2 * j + c + 1))
                        nc.vector.tensor_tensor(gt_lo[:, c, :], X[c][:, :], gt_hi[:, c, :],
                                                ALU.subtract).then_inc(gt_lo_done, 1)
                if p3 and p1:
                    shift_logits(k, O[0])
                if ahead == 2:
                    norm_stats_first(i + 2)
                if p3:
                    if p1:
                        choose(k)
                    number_slots(k, O[1] if p1 else KV[1])
                if p2:
                    for pr in range(2):
                        dve.wait_ge(wo_done, n(2 * j + pr + 1))
                        dve.wait_ge(xr_in, 16 * (j + 1))
                        if p3:
                            dve.wait_ge(x1_out, 16 * j)
                            dve.wait_ge(x1_copied, n(j))
                            dve.wait_ge(xc_done, n(j))
                        nc.vector.tensor_tensor(x1[:, 2 * pr:2 * pr + 2, :].rearrange("p t d -> p (t d)"), O[pr][:, :],
                                                xr[:, 2 * pr:2 * pr + 2, :].rearrange("p t d -> p (t d)"),
                                                ALU.add).then_inc(x1_done, 1)

            def last(k):
                stats_second(k)
                centre(k)
                modulate(k)
                shift_logits(k, KV[0])
                choose(k)
                number_slots(k, KV[1])

            run_steps(dve, step, batch_end, last)

            def split_w(e, y, piece):
                dve.wait_ge(w_hi_out, n(4 * e + piece + 1))
                part = slice(piece * EW // 4, (piece + 1) * EW // 4)
                nc.vector.tensor_tensor(w_lo[y][:, part], w_raw[y][:, part], w_hi[y][:, part],
                                        ALU.subtract).then_inc(w_lo_done, 1)

            def rows_low(e, y, c):
                dve.wait_ge(e_hi_out, n(2 * e + c + 1))
                nc.vector.tensor_tensor(e_lo[y][:, c, :], X[1][:, :], e_hi[y][:, c, :],
                                        ALU.subtract).then_inc(e_lo_done, 1)

            def results_landed(e):
                if not (isinstance(e, int) and e < 2):
                    dve.wait_ge(res_out, 16 * (T * (e - 1) + 1))

            def scale_y(e, y):
                dve.wait_ge(y_part, n(NF * (e + 1)))
                dve.wait_ge(factor_step, n((NB - 1) * (e + 1)))
                results_landed(e)
                for pr in range(2):
                    ins = nc.vector.tensor_tensor(res[y][:, 2 * pr:2 * pr + 2, :].rearrange("p t d -> p (t d)"),
                                                  Y[y][pr][:, :],
                                                  factor[:, 2 * pr:2 * pr + 2, :].rearrange("p t d -> p (t d)"), ALU.mult)
                ins.then_inc(scaled_done, 1)

            for piece in range(4):
                split_w(0, 0, piece)
            for c in range(H):
                rows_low(0, 0, c)

            def body(e, pair, y, prev, nxt):
                for f in range(NF):
                    dve.wait_ge(f_hi_out, n(NF * e + f + 1))
                    nc.vector.scalar_tensor_tensor(out=f_lo[f % 3][:, :], in0=HID[f % 3][:, :], scalar=0.0,
                                                   in1=f_hi[f % 3][:, :], op0=ALU.max,
                                                   op1=ALU.subtract).then_inc(f_lo_done, 1)
                    if nxt and f < 4:
                        split_w(e + 1, 1 - y, f)
                    if prev and f == 2:
                        scale_y(e - 1, 1 - y)
                    if f == 3:
                        dve.wait_ge(x1_in[y], 16 * (pair + 1))
                        results_landed(e)
                        nc.vector.tensor_scalar(token_at[y][:, :], got_x1[y][:, :, TOKEN1], FAR, None,
                                                ALU.add).then_inc(token_done, 1)
                    if nxt and f in (4, 6):
                        rows_low(e + 1, 1 - y, (f - 4) // 2)
                    if 4 <= f < 4 + NB - 1:
                        row = f - 3
                        dve.wait_ge(factor0_out, n(e + 1))
                        dve.wait_ge(factor_step, n((NB - 1) * e + row - 1))
                        for t in range(T):
                            ins = nc.vector.scalar_tensor_tensor(
                                out=factor[:, t, :], in0=gb_all[:, row, :],
                                scalar=got_x1[y][:, t, GATE1 + row:GATE1 + row + 1],
                                in1=factor[:, t, :], op0=ALU.mult, op1=ALU.add)
                        ins.then_inc(factor_step, 1)
            run_experts(dve, body, lambda e, pair, y: scale_y(e, y))

        @block.tensor
        def _(pe):
            start_counts(pe, h_turned, kv_done, u_done, q_done, kv_summed, att_done, g_turned, wo_done,
                         h2_turned, logits_done, places_done, e_turned, hid_done, y_part)

            def tile(t):
                return slice(t * P, (t + 1) * P)

            def turn(src, done):
                for c in range(H):
                    for t in range(T):
                        ins = nc.tensor.transpose(X[c][:, tile(t)], src[:, t, c * P:(c + 1) * P], ident[:, :])
                    ins.then_inc(done, 1)

            pe.wait_ge(c_ready, 1)
            pe.wait_ge(mod1_in, 16)
            wm = w_raw[0][:, 0:H * 6 * D].rearrange("p (k w) -> p k w", k=H)
            for a in range(2):
                for c in range(H):
                    at = (a * H + c) * NB
                    for kk in range(H):
                        ins = nc.tensor.matmul(UB[:, at:at + NB], wm[:, kk, a * D + c * P:a * D + (c + 1) * P],
                                               c_silu[:, kk, :], start=(kk == 0), stop=(kk == H - 1))
            ins.then_inc(mod_t_done, 1)

            def mod_by_row():
                pe.wait_ge(weights_in, 32)
                for half in range(2):
                    for kk in range(H):
                        ins = nc.tensor.matmul(O[half][0:NB, :], c_silu[:, kk, :],
                                               wm[:, kk, 2 * D * (half + 1):2 * D * (half + 2)],
                                               start=(kk == 0), stop=(kk == H - 1))
                    ins.then_inc(mod_done, 1)

            def turn_xn(i, j):
                pe.wait_ge(xn_done, n(i + 1))
                if j is None:
                    pe.wait_ge(h_scaled, n(2 * i))
                else:
                    pe.wait_ge(gt_lo_done, n(2 * j + 2))
                turn(xn, h_turned)

            pe.wait_ge(consts_pool, 1)
            turn_xn(0, None)

            def project_tile(i, t):
                if t == 0:
                    pe.wait_ge(h_scaled, n(2 * i + 2))
                    pe.wait_ge(q_out, n(2 * i))
                elif t >= 2:
                    pe.wait_ge(kv_lo_done, n(4 * i + t - 1))
                products = [(KV[t % 2][:, :], 0, 2 * D), (UB[:, (t % 2) * D:(t % 2 + 1) * D], 2 * D, 3 * D)]

                def multiply(which, parts, opens, closes):
                    dst, lo, hi = products[which]
                    for m, (a, w) in enumerate(parts):
                        for c in range(H):
                            ins = nc.tensor.matmul(dst, a[:, c, tile(t)], w[:, c, lo:hi],
                                                   start=opens and m == 0 and c == 0,
                                                   stop=closes and m == len(parts) - 1 and c == H - 1,
                                                   skip_group_check=True)
                    return ins

                def u_bank_free():
                    if t % 2 == 0:
                        pe.wait_ge(u_out, n(2 * i + t // 2))

                high, low = [(h_hi, w4_hi), (h_hi, w4_lo)], [(h_lo, w4_hi)]
                if t == 0:
                    multiply(0, high, True, False)
                    u_bank_free()
                    multiply(1, high, True, False)
                    pe.wait_ge(h_lo_done, n(2 * i + 2))
                    multiply(0, low, False, True).then_inc(kv_done, 1)
                    multiply(1, low, False, True)
                else:
                    multiply(0, high + low, True, True).then_inc(kv_done, 1)
                    u_bank_free()
                    ins = multiply(1, high + low, True, True)
                    if t % 2:
                        ins.then_inc(u_done, 1)

            def sum_kv(i, b, r, t):
                pe.wait_ge(kv_lo_done, n(4 * i + t + 1))
                opens = isinstance(r, int) and r == 0 and t == 0
                if opens:
                    pe.wait_ge(att_kv, n(b))
                ends = False
                for c in range(H):
                    nc.tensor.matmul(KVSUM[:, c * 2 * P:(c + 1) * 2 * P], k_hi[t % 2][:, c * P:(c + 1) * P],
                                     v2[t % 2][:, c, :], start=opens and c == 0, stop=ends, skip_group_check=True)
                    ins = nc.tensor.matmul(KVSUM[:, c * 2 * P:c * 2 * P + P], k_lo[t % 2][:, c * P:(c + 1) * P],
                                           v2[t % 2][:, c, 0:P], start=False, stop=ends, skip_group_check=True)
                ins.then_inc(kv_summed, 1)

            def project_q(i, c):
                pe.wait_ge(kv_lo_done, n(4 * i + 3 + c))
                out_ch = slice(3 * D + c * P, 3 * D + (c + 1) * P)
                m = 0
                for a, w in ((h_hi, w4_hi), (h_hi, w4_lo), (h_lo, w4_hi)):
                    for kk in range(H):
                        ins = nc.tensor.matmul(KV[c][:, :], w[:, kk, out_ch], a[:, kk, :],
                                               start=(m == 0), stop=(m == 3 * H - 1))
                        m += 1
                ins.then_inc(q_done, 1)

            def attend(j, bj):
                pe.wait_ge(att_kv, n(bj + 1))
                pe.wait_ge(q_lo_done, n(2 * j + 2))
                for pr in range(2):
                    pe.wait_ge(x1_done, n(2 * j - 1 + pr))
                    for t in (2 * pr, 2 * pr + 1):
                        for c in range(H):
                            dst = O[pr][:, (t % 2) * D + c * P:(t % 2) * D + (c + 1) * P]
                            nc.tensor.matmul(dst, q_hi[:, c, tile(t)], kv_hi[:, c, :], start=True, stop=False)
                            nc.tensor.matmul(dst, q_hi[:, c, tile(t)], kv_lo[:, c, :], start=False, stop=False)
                            ins = nc.tensor.matmul(dst, q_lo[:, c, tile(t)], kv_hi[:, c, :], start=False, stop=True)
                    ins.then_inc(att_done, 1)

            def project_out(j, bj, k):
                pe.wait_ge(wog_done, n(bj + 1))
                pe.wait_ge(gt_lo_done, n(2 * j + 2))
                for pr in range(2):
                    if k is not None:
                        pe.wait_ge(places_read if pr else shifted_done, n(k + 1))
                    for t in (2 * pr, 2 * pr + 1):
                        m = 0
                        for a, w in ((gt_hi, wog_hi), (gt_hi, wog_lo), (gt_lo, wog_hi)):
                            for c in range(H):
                                ins = nc.tensor.matmul(O[pr][:, (t % 2) * D:(t % 2 + 1) * D], a[:, c, tile(t)],
                                                       w[:, c, :], start=(m == 0), stop=(m == 3 * H - 1))
                                m += 1
                    ins.then_inc(wo_done, 1)

            def turn_h2(k, i):
                pe.wait_ge(h2_done, n(k + 1))
                if i is not None:
                    pe.wait_ge(h_scaled, n(2 * i + 2))
                turn(rows, h2_turned)

            def logits(k, j, bank):
                pe.wait_ge(rows_out, 16)
                pe.wait_ge(h2t_out, n(2 * k + 2))
                if j is not None:
                    pe.wait_ge(gated, n(2 * j + 1))
                else:
                    pe.wait_ge(q_out, n(2 * NBLK))
                for t in range(T):
                    for c in range(H):
                        ins = nc.tensor.matmul(bank[:, t * E:(t + 1) * E], h2t[:, c, tile(t)], wg[:, c, :],
                                               start=(c == 0), stop=(c == H - 1))
                ins.then_inc(logits_done, 1)

            def count_places(k, bank):
                pe.wait_ge(chosen_done, n(k + 1))
                places = bank[:, 0:T * E].rearrange("p (t e) -> p t e", t=T)
                nc.tensor.matmul(places, ones[:, :], seen[:, :].unsqueeze(1).to_broadcast([P, T, E]),
                                 start=True, stop=False, skip_group_check=True)
                for s in range(T):
                    ins = nc.tensor.matmul(places[:, 0:s + 1, :], before[:, :],
                                           chosen[:, s, :].unsqueeze(1).to_broadcast([P, s + 1, E]),
                                           start=False, stop=s == T - 1, skip_group_check=True)
                    if s < T - 1:
                        nc.tensor.matmul(places[:, s + 1:T, :], up_to[:, :],
                                         chosen[:, s, :].unsqueeze(1).to_broadcast([P, T - 1 - s, E]),
                                         start=False, stop=False, skip_group_check=True)
                ins.then_inc(places_done, 1)

            def step(i, b, r, p1, p2, p3, ahead):
                j, k = i - PER, i - PER - 1
                if p1:
                    project_tile(i, 0)
                if p2:
                    attend(j, b - 1)
                if p1:
                    project_tile(i, 1)
                    sum_kv(i, b, r, 0)
                    project_tile(i, 2)
                    sum_kv(i, b, r, 1)
                    project_tile(i, 3)
                    sum_kv(i, b, r, 2)
                if p3:
                    turn_h2(k, i if p1 else None)
                    if not p1:
                        logits(k, None, KV[0])
                if p1:
                    project_q(i, 0)
                if p2:
                    pe.wait_ge(g_done, n(j + 1))
                    if p3:
                        pe.wait_ge(h2t_out, n(2 * k + 2))
                    else:
                        pe.wait_ge(h_scaled, n(2 * i + 2))
                    turn(g, g_turned)
                if p3 and p1:
                    logits(k, j, O[0])
                if p1:
                    sum_kv(i, b, r, 3)
                    project_q(i, 1)
                if ahead:
                    turn_xn(i + 1, j if p2 else None)
                if first_step(i):
                    mod_by_row()
                if p3:
                    count_places(k, O[1] if p1 else KV[1])
                if p2:
                    project_out(j, b - 1, k if p3 and p1 else None)

            def last(k):
                turn_h2(k, None)
                logits(k, None, KV[0])
                count_places(k, KV[1])

            run_steps(pe, step, lambda b: None, last)

            def turn_rows(e, pair, y, c):
                pe.wait_ge(h_in[y], 16 * (pair + 1))
                pe.wait_ge(e_lo_done, n(2 * e + c))
                for t in range(T):
                    ins = nc.tensor.transpose(X[1][:, tile(t)], got_h[y][:, t, c * P:(c + 1) * P], ident[:, :])
                ins.then_inc(e_turned, 1)

            def hidden(e, y, f):
                pe.wait_ge(f_lo_done, n(chunk_freed(e, f)))
                m = 0
                for w, a in ((w_hi, e_hi), (w_lo, e_hi), (w_hi, e_lo)):
                    w1 = w[y][:, 0:H * F].rearrange("p (c f) -> p c f", c=H)
                    for c in range(H):
                        ins = nc.tensor.matmul(HID[f % 3][:, :], w1[:, c, f * P:(f + 1) * P], a[y][:, c, :],
                                               start=(m == 0), stop=(m == 3 * H - 1))
                        m += 1
                ins.then_inc(hid_done, 1)

            def partial_y(e, y, f):
                pe.wait_ge(f_lo_done, n(NF * e + f + 1))
                if f == 0:
                    pe.wait_ge(w_lo_done, n(4 * e + 4))
                    pe.wait_ge(scaled_done, n(e - 1))
                for t in range(T):
                    dst = Y[y][t // 2][:, (t % 2) * D:(t % 2 + 1) * D]
                    m = 0
                    for a, w in ((f_hi, w_hi), (f_hi, w_lo), (f_lo, w_hi)):
                        w2 = w[y][:, H * F:2 * H * F].rearrange("p (f d) -> p f d", f=NF)
                        ins = nc.tensor.matmul(dst, a[f % 3][:, tile(t)], w2[:, f, :],
                                               start=(f == 0 and m == 0 and t % 2 == 0),
                                               stop=(f == NF - 1 and m == 2), skip_group_check=True)
                        m += 1
                ins.then_inc(y_part, 1)

            for c in range(H):
                turn_rows(0, 0, 0, c)

            def body(e, pair, y, prev, nxt):
                pe.wait_ge(e_lo_done, n(2 * e + 2))
                pe.wait_ge(w_lo_done, n(4 * e + 2))
                for f in range(NF):
                    hidden(e, y, f)
                    if f >= 2:
                        partial_y(e, y, f - 2)
                    elif prev:
                        partial_y(e - 1, 1 - y, NF - 2 + f)
                    if nxt and f in (3, 5):
                        turn_rows(e + 1, pair + 1 if y else pair, 1 - y, (f - 3) // 2)

            def last_shares(e, pair, y):
                partial_y(e, y, NF - 2)
                partial_y(e, y, NF - 1)

            run_experts(pe, body, last_shares)


def kernel(L0_attn_x, L0_attn_Wq, L0_attn_Wk, L0_attn_Wv, L0_attn_Wu, L0_attn_Wo, L0_ffn_Wg, L0_ffn_w1,
           L0_ffn_w2, L0_c, L0_wmod):
    import numpy as np
    import concourse.bacc as bacc
    from concourse.bass_utils import run_bass_kernel_spmd

    def halves(w):
        w = np.asarray(w)
        return np.ascontiguousarray(w.reshape(-1, P, w.shape[1]).transpose(1, 0, 2))

    x = np.ascontiguousarray(L0_attn_x)
    b, l, d = x.shape
    experts, _, hidden = L0_ffn_w1.shape
    w4 = np.concatenate([np.asarray(w).T for w in (L0_attn_Wk, L0_attn_Wv, L0_attn_Wu, L0_attn_Wq)], axis=1)
    w1 = np.asarray(L0_ffn_w1).reshape(experts, -1, P, hidden).transpose(0, 2, 1, 3).reshape(experts, P, -1)
    w2 = np.asarray(L0_ffn_w2).reshape(experts, -1, P, d).transpose(0, 2, 1, 3).reshape(experts, P, -1)
    arrays = {
        "x_dram": x.reshape(-1, P, 4 * d),
        "w_kvuq_dram": halves(w4),
        "w_o_dram": halves(np.asarray(L0_attn_Wo).T),
        "w_gate_dram": halves(L0_ffn_Wg),
        "w_experts_dram": np.ascontiguousarray(np.concatenate([w1, w2], axis=2)),
        "c_t_dram": halves(np.asarray(L0_c).T),
        "w_mod_dram": halves(L0_wmod),
    }
    nc = bacc.Bacc("TRN2", target_bir_lowering=False, num_devices=1)
    args = [nc.dram_tensor(name, a.shape, mybir.dt.from_np(a.dtype), kind="ExternalInput").ap()
            for name, a in arrays.items()]
    out = nc.dram_tensor("out_dram", (b * l, d), F32, kind="ExternalOutput").ap()
    adaln_block_kernel(nc, *args, out)
    result = run_bass_kernel_spmd(nc, [arrays], core_ids=[0]).results[0]["out_dram"]
    return result.reshape(b, l, d)
```

```python
from contextlib import ExitStack

import concourse.bass as bass
from concourse import mybir

ALU = mybir.AluOpType
ACT = mybir.ActivationFunctionType
AX = mybir.AxisListType
F32 = mybir.dt.float32
F32R = mybir.dt.float32r
BF16 = mybir.dt.bfloat16
U32 = mybir.dt.uint32

P = 128
START = 2


def n(count):
    return count + START


def adaln_block_kernel(nc, x, w_kvuq, w_o, w_gate, w_experts, c_t, w_mod, out):
    NBLK, _, XW = x.shape
    D = w_o.shape[2]
    H = D // P
    T = XW // D
    BLK = T * P
    NB = c_t.shape[2]
    PER = NBLK // NB
    E = w_gate.shape[2]
    EW = w_experts.shape[2]
    F = EW // (2 * H)
    NF = F // P
    CAP = (NBLK * BLK + E - 1) // E
    HEAD = 16
    NH = D // HEAD
    ROW = 2 * D + 8
    GATE0, TOKEN = 2 * D, 2 * D + NB
    FAR = 65536.0
    LN_EPS, RMS_FLOOR = 1e-5, 1e-12
    assert CAP == BLK and H == 2 and T == 4 and PER == 4 and D % HEAD == 0

    dispatched = nc.dram_tensor("dispatched_dram", [E * CAP, ROW], F32, kind="Internal").ap()
    slots = dispatched.rearrange("(e p t) w -> e p (t w)", p=P, t=T)
    mod_dram = nc.dram_tensor("mod_rows_dram", [NB, 4, D], F32, kind="Internal").ap()
    slots_rows = dispatched.rearrange("(e p t) w -> e p t w", p=P, t=T)
    slots_h, slots_x1 = slots_rows[:, :, :, 0:D], slots_rows[:, :, :, D:ROW]
    out_blocks = out.rearrange("(i p t) d -> i p (t d)", p=P, t=T)

    with ExitStack() as ctx:
        def sem(name):
            return ctx.enter_context(nc.semaphore(name))

        bank = [ctx.enter_context(nc.psum_tensor(f"bank{i}", [P, 512], F32)) for i in range(8)]
        X = bank[0:2]
        KV = bank[2:4]
        UB, KVSUM = bank[4], bank[5]
        O = bank[6:8]
        TAIL = bank[4:6]
        HID = KV + X[0:1]
        Y = [[UB, KVSUM], O]

        def sb(name, shape, dt=F32, stack=ctx):
            return stack.enter_context(nc.sbuf_tensor(name, shape, dt))

        ident = sb("ident", [P, P])
        gb_all = sb("gb_all", [P, NB, D])
        w_raw = [sb("w_raw0", [P, EW]), None]
        w_hi = [sb("w_hi0", [P, EW], F32R), None]
        w_lo = [sb("w_lo0", [P, EW], F32R), None]

        attention = ExitStack()

        def asb(name, shape, dt=F32):
            return sb(name, shape, dt, attention)

        before = asb("before", [P, P], BF16)
        up_to = asb("up_to", [P, P], BF16)
        ones = asb("ones", [P, P], BF16)
        tri = asb("tri", [P, P])
        head_mask = asb("head_mask", [P, P])
        rank = asb("rank", [P, E])
        row_onehot = asb("row_onehot", [P, NB, NB])
        token_no = asb("token_no", [P, T])
        exponent = asb("exponent", [P, T])
        wg = asb("wg", [P, H, E])
        w4_hi = asb("w4_hi", [P, H, 4 * D], F32R)
        w4_lo = asb("w4_lo", [P, H, 4 * D], F32R)
        wo = asb("wo", [P, H, D])
        wog_hi = asb("wog_hi", [P, H, D], F32R)
        wog_lo = asb("wog_lo", [P, H, D], F32R)
        c_raw = asb("c_raw", [P, H, NB])
        c_silu = asb("c_silu", [P, H, NB])
        shift1 = asb("shift1", [P, H, NBLK])
        scale1 = asb("scale1", [P, H, NBLK])
        GA, SB, CB = range(3)
        mods = asb("mods", [P, NB, 3, D])

        x_room = asb("x_room", [P, T * ROW])
        xa = x_room[:, 0:T * D].rearrange("p (t d) -> p t d", t=T)
        xn = x_room[:, T * D:2 * T * D].rearrange("p (t d) -> p t d", t=T)
        rows_b = x_room[:, :].rearrange("p (t w) -> p t w", t=T)
        stats1 = asb("stats1", [P, T, 6])
        mv1 = asb("mv1", [P, T, 2])
        var1 = asb("var1", [P, T])
        neg_mean1 = asb("neg_mean1", [P, T])
        rstd1 = asb("rstd1", [P, T])
        bias1 = asb("bias1", [P, T])
        h32 = asb("h32", [P, H, BLK])
        h_hi = asb("h_hi", [P, H, BLK], F32R)
        h_lo = asb("h_lo", [P, H, BLK], F32R)
        k_hi = [asb(f"k_hi{i}", [P, D], F32R) for i in range(2)]
        k_lo = [asb(f"k_lo{i}", [P, D], F32R) for i in range(2)]
        v2 = [asb(f"v2{i}", [P, H, 2 * P], F32R) for i in range(2)]
        q_ring = asb("q_ring", [P, PER, H, BLK])
        u_ring = asb("u_ring", [P, PER, T, D])
        kv_a = asb("kv_a", [P, H, P])
        kv_b = asb("kv_b", [P, H, P])
        kv_hi = asb("kv_hi", [P, H, P], F32R)
        kv_lo = asb("kv_lo", [P, H, P], F32R)
        q_hi = asb("q_hi", [P, H, BLK], F32R)
        q_lo = asb("q_lo", [P, H, BLK], F32R)
        sq = asb("sq", [P, T, D])
        ssq = asb("ssq", [P, T * NH])
        rms = asb("rms", [P, T * NH])
        rrms = asb("rrms", [P, T * NH])
        g = asb("g", [P, T, D])
        mod_rows = g[0:NB, :, :]
        g_size, g_sign = sq[0:NB, 0, :], sq[0:NB, 1, :]
        gt_hi = asb("gt_hi", [P, H, BLK], F32R)
        gt_lo = asb("gt_lo", [P, H, BLK], F32R)
        xr = asb("xr", [P, T, D])
        x1 = asb("x1", [P, T, D])
        stats2 = asb("stats2", [P, T, 6])
        mv2 = asb("mv2", [P, T, 2])
        var2 = asb("var2", [P, T])
        rstd2 = asb("rstd2", [P, T])
        xc = asb("xc", [P, T, D])
        wog = xc[:, 0:H, :]
        rows = asb("rows", [P, T, ROW])
        h2t = asb("h2t", [P, H, BLK])
        top = asb("top", [P, T])
        below_top = asb("below_top", [P, T, E])
        prob = asb("prob", [P, T, E])
        psum_ = asb("psum_", [P, T])
        ptop = asb("ptop", [P, T])
        is_top = asb("is_top", [P, T, E])
        ranked = asb("ranked", [P, T, E])
        best = asb("best", [P, T])
        chosen = asb("chosen", [P, T, E], BF16)
        seen = asb("seen", [P, E], BF16)
        newly = asb("newly", [P, E])
        rsum = asb("rsum", [P, T])
        gate = asb("gate", [P, T])
        picked = asb("picked", [P, T, E])
        place = asb("place", [P, T])
        over = asb("over", [P, T])
        first_slot = asb("first_slot", [P, T])
        slot = asb("slot", [P, T])
        slot_no = asb("slot_no", [P, T], U32)
        attention.close()

        w_raw[1] = sb("w_raw1", [P, EW])
        w_hi[1] = sb("w_hi1", [P, EW], F32R)
        w_lo[1] = sb("w_lo1", [P, EW], F32R)
        got_h = [sb(f"got_h{i}", [P, T, D]) for i in range(2)]
        got_x1 = [sb(f"got_x1{i}", [P, T, ROW - D]) for i in range(2)]
        GATE1, TOKEN1 = GATE0 - D, TOKEN - D
        e_hi = [sb(f"e_hi{i}", [P, H, BLK], F32R) for i in range(2)]
        e_lo = [sb(f"e_lo{i}", [P, H, BLK], F32R) for i in range(2)]
        f_hi = [sb(f"f_hi{i}", [P, BLK], F32R) for i in range(3)]
        f_lo = [sb(f"f_lo{i}", [P, BLK], F32R) for i in range(3)]
        factor = sb("factor", [P, T, D])
        res = [sb(f"res{i}", [P, T, D]) for i in range(2)]
        token_at = [sb(f"token_at{i}", [P, T], U32) for i in range(2)]

        mod1_in, w4_in, weights_in = sem("mod1_in"), sem("w4_in"), sem("weights_in")
        x_in, xr_in = sem("x_in"), sem("xr_in")
        zeros_out = sem("zeros_out")
        x1_out = sem("x1_out")
        rows_out = sem("rows_out")
        w_in = [sem("w_in0"), sem("w_in1")]
        h_in = [sem("h_in0"), sem("h_in1")]
        x1_in = [sem("x1_in0"), sem("x1_in1")]
        res_out = sem("res_out")
        rows_zero, consts_pool, consts_dve = sem("rows_zero"), sem("consts_pool"), sem("consts_dve")
        tri_made = sem("tri_made")
        c_ready, mod_t_done, mod_t_read, w4_hi_done, w4_lo_done = (
            sem(s) for s in ("c_ready", "mod_t_done", "mod_t_read", "w4_hi_done", "w4_lo_done"))
        mod_done, g_guard, mod_rows_out, mods_in = (
            sem(s) for s in ("mod_done", "g_guard", "mod_rows_out", "mods_in"))
        h_turned, kv_done, u_done, q_done, kv_summed = (
            sem(s) for s in ("h_turned", "kv_done", "u_done", "q_done", "kv_summed"))
        att_done, g_turned, wo_done, h2_turned, logits_done, places_done = (
            sem(s) for s in ("att_done", "g_turned", "wo_done", "h2_turned", "logits_done", "places_done"))
        e_turned, hid_done, y_part = sem("e_turned"), sem("hid_done"), sem("y_part")
        xn_done, h_scaled, h32_made, kv_hi_out, u_out, q_out, sq_out, rms_out = (
            sem(s) for s in ("xn_done", "h_scaled", "h32_made", "kv_hi_out", "u_out", "q_out", "sq_out", "rms_out"))
        q_hi_done, gt_hi_out, x1_copied, h2t_out, prob_out = (
            sem(s) for s in ("q_hi_done", "gt_hi_out", "x1_copied", "h2t_out", "prob_out"))
        e_hi_out, f_hi_out, w_hi_out, factor0_out = (
            sem(s) for s in ("e_hi_out", "f_hi_out", "w_hi_out", "factor0_out"))
        stats1_done, mv1_done, var1_done = (
            sem(s) for s in ("stats1_done", "mv1_done", "var1_done"))
        kv_lo_done, h_lo1_done, att_kv, att_kv_step, wog_step, wog_done = (
            sem(s) for s in ("kv_lo_done", "h_lo1_done", "att_kv", "att_kv_step", "wog_step", "wog_done"))
        gated, ssq_sum, ssq_done, rrms_done, g_done, gt_lo_done, x1_done = (
            sem(s) for s in ("gated", "ssq_sum", "ssq_done", "rrms_done", "g_done", "gt_lo_done", "x1_done"))
        stats2_done, mv2_done, var2_done, xc_done, h2_done = (
            sem(s) for s in ("stats2_done", "mv2_done", "var2_done", "xc_done", "h2_done"))
        route_step, shifted_done, chosen_done, places_read, slot_step, slots_done = (
            sem(s) for s in ("route_step", "shifted_done", "chosen_done", "places_read", "slot_step", "slots_done"))
        e_lo_done, f_lo_done, w_lo_done, factor_step, scaled_done, token_done = (
            sem(s) for s in ("e_lo_done", "f_lo_done", "w_lo_done", "factor_step", "scaled_done", "token_done"))
        stats1_seen, stats2_seen, scatter_turn = (
            sem(s) for s in ("stats1_seen", "stats2_seen", "scatter_turn"))
        rstd1_step, rstd1_done, h_lo0_done, q_lo_done, rstd2_done, res_done = (
            sem(s) for s in ("rstd1_step", "rstd1_done", "h_lo0_done", "q_lo_done", "rstd2_done", "res_done"))

        block = ctx.enter_context(nc.Block())

        def run_steps(eng, step, tail_start, tail, last):
            step(0, 0, 0, p2=False, p3=False, ahead=2)
            with eng.Fori(1, PER - 1) as r:
                step(r, 0, r, p2=False, p3=False, ahead=2)
            step(PER - 1, 0, PER - 1, p2=False, p3=False, ahead=2)
            step(PER, 1, 0, p2=True, p3=False, ahead=2)
            with eng.Fori(1, NB - 1) as b:
                with eng.Fori(1, PER - 1) as r:
                    step(b * PER + r, b, r, p2=True, p3=True, ahead=2)
                step(b * PER + PER - 1, b, PER - 1, p2=True, p3=True, ahead=2)
                step(b * PER + PER, b + 1, 0, p2=True, p3=True, ahead=2)
            with eng.Fori(1, PER - 2) as r:
                step(r + (NB - 1) * PER, NB - 1, r, p2=True, p3=True, ahead=2)
            step(NBLK - 2, NB - 1, PER - 2, p2=True, p3=True, ahead=1)
            step(NBLK - 1, NB - 1, PER - 1, p2=True, p3=True, ahead=0)
            tail_start(NBLK - PER)
            for r in range(PER):
                tail(NBLK - PER + r, r, rows if r % 2 else rows_b, attends=r < PER - 1, splits=r < PER - 2)
            last(NBLK - 1, rows_b)

        def opens_row(r):
            return isinstance(r, int) and r == 0

        def closes_row(r):
            return isinstance(r, int) and r == PER - 1

        def first_step(i):
            return isinstance(i, int) and i == 0

        def run_experts(eng, body, last):
            body(0, 0, 0, False, True)
            body(1, 0, 1, True, True)
            with eng.Fori(1, E // 2 - 1) as pair:
                body(2 * pair, pair, 0, True, True)
                body(2 * pair + 1, pair, 1, True, True)
            body(E - 2, E // 2 - 1, 0, True, True)
            body(E - 1, E // 2 - 1, 1, True, False)
            last(E - 1, E // 2 - 1, 1)

        def chunk_freed(e, f):
            return NF * e + (f - 2 if f >= 3 else (-1, 0, 0)[f])

        def rows_landed(k, two):
            return 16 * (T * (k - 1 if two else k) + 1)

        def start_counts(eng, *sems):
            for s in sems:
                eng.sem_inc(s, START)

        @block.sync
        def _(sp):
            sp.dma_start(xa[:, :, :], x[0]).then_inc(x_in, 16)
            wm = w_raw[0][:, 0:H * 6 * D].rearrange("p (k w) -> p k w", k=H)
            sp.dma_start(wm[:, :, 0:2 * D], w_mod[:, :, 0:2 * D]).then_inc(mod1_in, 16)
            sp.dma_start(q_ring[:, 0:2, :, :], w_kvuq).then_inc(w4_in, 16)
            sp.dma_start(wm[:, :, 2 * D:6 * D], w_mod[:, :, 2 * D:6 * D]).then_inc(weights_in, 16)
            sp.dma_start(wo[:, :, :], w_o).then_inc(weights_in, 16)

            sp.wait_ge(rows_zero, 1)

            def zero_slots(s):
                for e in range(E // NB):
                    sp.dma_start(slots[s * (E // NB) + e], rows[:, :, :]).then_inc(zeros_out, 16)

            def load_x(i):
                sp.wait_ge(xn_done, n(i))
                sp.dma_start(xa[:, :, :], x[i]).then_inc(x_in, 16)

            def swap_x1(j, rows_first):
                sp.wait_ge(x1_done, n(2 * j + 2))
                if rows_first:
                    sp.wait_ge(rows_out, 16 * (T * j + 1))
                sp.dma_start(out_blocks[j], x1[:, :, :]).then_inc(x1_out, 16)
                if not (isinstance(j, int) and j == NBLK - 1):
                    sp.dma_start(xr[:, :, :], x[j + 1]).then_inc(xr_in, 16)

            load_x(1)
            load_x(2)
            sp.wait_ge(g_guard, 6)
            sp.dma_start(mod_dram, mod_rows).then_inc(mod_rows_out, 16)
            sp.wait_ge(mod_rows_out, 16)

            def spread_mods(b):
                row = mod_dram[bass.ds(b, 1)]
                sp.dma_start(mods[:, bass.ds(b, 1), :, :],
                             row[:, 0:3, :].unsqueeze(0).to_broadcast([P, 1, 3, D])).then_inc(mods_in, 16)
                sp.dma_start(gb_all[:, bass.ds(b, 1), :],
                             row[:, 3, :].unsqueeze(0).to_broadcast([P, 1, D])).then_inc(mods_in, 16)

            with sp.Fori(0, NB) as s:
                spread_mods(s)
                load_x(s + 3)
                zero_slots(s)
            sp.dma_start(xr[:, :, :], x[0]).then_inc(xr_in, 16)
            sp.wait_ge(mod_done, 2)
            sp.dma_start(w_raw[0][:, :], w_experts[0]).then_inc(w_in[0], 16)
            swap_x1(0, False)
            with sp.Fori(PER + 1, NBLK - 2) as s:
                load_x(s + 2)
                swap_x1(s - PER, True)
            for j in range(NBLK - 2 - PER, NBLK - PER):
                swap_x1(j, True)
            with sp.Fori(NBLK - PER, NBLK - 1) as j:
                swap_x1(j, False)
            swap_x1(NBLK - 1, False)

            sp.wait_ge(x1_out, 16 * NBLK)
            sp.wait_ge(rows_out, 16 * (NBLK * T + 1))

            def load_h(e, y):
                if not (isinstance(e, int) and e < 2):
                    sp.wait_ge(e_turned, n(2 * (e - 1)))
                sp.dma_start(got_h[y][:, :, :], slots_h[e]).then_inc(h_in[y], 16)

            def load_x1(e, y):
                if not (isinstance(e, int) and e < 2):
                    sp.wait_ge(res_done, n(e - 1))
                sp.dma_start(got_x1[y][:, :, :], slots_x1[e]).then_inc(x1_in[y], 16)

            def load_w(e, y):
                if not (isinstance(e, int) and e < 2):
                    sp.wait_ge(w_hi_out, n(4 * (e - 1)))
                    sp.wait_ge(w_lo_done, n(4 * (e - 1)))
                sp.dma_start(w_raw[y][:, :], w_experts[e]).then_inc(w_in[y], 16)

            load_h(0, 0)
            load_w(1, 1)
            load_h(1, 1)
            load_x1(0, 0)
            load_x1(1, 1)
            load_h(2, 0)
            load_w(2, 0)
            with sp.Fori(1, E // 2 - 1) as pair:
                load_x1(2 * pair, 0)
                load_h(2 * pair + 1, 1)
                load_w(2 * pair + 1, 1)
                load_x1(2 * pair + 1, 1)
                load_h(2 * pair + 2, 0)
                load_w(2 * pair + 2, 0)
            load_x1(E - 2, 0)
            load_h(E - 1, 1)
            load_w(E - 1, 1)
            load_x1(E - 1, 1)
            sp.wait_ge(res_out, 16 * (E * T + 1))

        @block.gpsimd
        def _(pool):
            start_counts(pool, rstd1_step, rstd1_done, h_lo0_done, q_lo_done, rstd2_done, res_done)
            def rstd_first(i):
                pool.wait_ge(var1_done, n(i + 1))
                nc.gpsimd.tensor_tensor(rstd1[:, :], var1[:, :], exponent[:, :], ALU.pow).then_inc(rstd1_step, 1)
                pool.wait_ge(rstd1_step, n(i + 1))
                nc.gpsimd.tensor_tensor(bias1[:, :], neg_mean1[:, :], rstd1[:, :], ALU.mult).then_inc(rstd1_done, 1)

            pool.dma_start(c_raw[:, :, :], c_t).then_inc(res_out, 16)
            pool.dma_start(wg[:, :, :], w_gate).then_inc(rows_out, 16)
            nc.gpsimd.memset(ident[:, :], 0.0).then_inc(tri_made, 1)
            nc.gpsimd.memset(tri[:, :], 1.0).then_inc(tri_made, 1)
            nc.gpsimd.memset(head_mask[:, :], 1.0 / HEAD).then_inc(tri_made, 1)
            nc.gpsimd.memset(row_onehot[:, :, :], 0.0).then_inc(tri_made, 1)
            pool.wait_ge(tri_made, 4)
            nc.gpsimd.affine_select(out=ident[:, :], in_=ident[:, :], compare_op=ALU.not_equal, fill=1.0,
                                    base=0, pattern=[[-1, P]], channel_multiplier=1).then_inc(consts_pool, 1)
            pool.wait_ge(consts_dve, 1)
            rstd_first(0)
            nc.gpsimd.memset(rows[:, :, :], 0.0).then_inc(rows_zero, 1)
            per_half = [[-HEAD, P // HEAD], [0, HEAD]]
            nc.gpsimd.affine_select(out=head_mask[:, :], in_=head_mask[:, :], compare_op=ALU.is_ge, fill=0.0,
                                    base=0, pattern=per_half, channel_multiplier=1).then_inc(tri_made, 1)
            pool.wait_ge(tri_made, 5)
            nc.gpsimd.affine_select(out=head_mask[:, :], in_=head_mask[:, :], compare_op=ALU.is_ge, fill=0.0,
                                    base=HEAD - 1, pattern=[[HEAD, P // HEAD], [0, HEAD]],
                                    channel_multiplier=-1).then_inc(consts_pool, 1)
            nc.gpsimd.affine_select(out=row_onehot[:, :, :], in_=row_onehot[:, :, :], compare_op=ALU.not_equal,
                                    fill=1.0, base=0, pattern=[[1, NB], [-1, NB]],
                                    channel_multiplier=0).then_inc(consts_pool, 1)
            nc.gpsimd.iota(rank[:, :], pattern=[[-1, E]], base=E, channel_multiplier=0,
                           allow_small_or_imprecise_dtypes=True).then_inc(consts_pool, 1)
            nc.gpsimd.iota(token_no[:, :], pattern=[[1, T]], base=-int(FAR), channel_multiplier=T,
                           allow_small_or_imprecise_dtypes=True).then_inc(consts_pool, 1)
            nc.gpsimd.affine_select(out=before[:, :], in_=tri[:, :], compare_op=ALU.is_gt, fill=0.0,
                                    base=0, pattern=[[1, P]], channel_multiplier=-1).then_inc(consts_pool, 1)
            nc.gpsimd.affine_select(out=up_to[:, :], in_=tri[:, :], compare_op=ALU.is_ge, fill=0.0,
                                    base=0, pattern=[[1, P]], channel_multiplier=-1).then_inc(consts_pool, 1)
            nc.gpsimd.memset(x_room[:, 2 * T * D:T * ROW], 0.0).then_inc(consts_pool, 1)

            def low_part(i):
                pool.wait_ge(h32_made, n(2 * i + 1))
                nc.gpsimd.tensor_tensor(h_lo[:, 0, :], h32[:, 0, :], h_hi[:, 0, :],
                                        ALU.subtract).then_inc(h_lo0_done, 1)

            low_part(0)
            rstd_first(1)

            def step(i, b, r, p2, p3, ahead):
                j, k = i - PER, i - PER - 1
                if p3:
                    rstd_second(k)
                if p2:
                    split_q(j + 1, (r + 1) % PER)
                if ahead == 2:
                    rstd_first(i + 2)
                if ahead:
                    low_part(i + 1)
                if p3:
                    scatter_rows(k, rows)
                if not p2 and closes_row(r):
                    split_q(0, 0)

            def split_q(j, r):
                for c in range(H):
                    pool.wait_ge(q_hi_done, n(2 * j + c + 1))
                    nc.gpsimd.tensor_tensor(q_lo[:, c, :], q_ring[:, r, c, :], q_hi[:, c, :],
                                            ALU.subtract).then_inc(q_lo_done, 1)

            def tail_start(j):
                split_q(j + 1, 1)
                rstd_second(j - 1)

            def tail(j, r, rows, attends, splits):
                if splits:
                    split_q(j + 2, r + 2)
                rstd_second(j)
                scatter_rows(j - 1, rows)

            def rstd_second(k):
                pool.wait_ge(var2_done, n(k + 1))
                nc.gpsimd.tensor_tensor(rstd2[:, :], var2[:, :], exponent[:, :], ALU.pow).then_inc(rstd2_done, 1)

            def scatter_rows(k, rows):
                pool.wait_ge(slots_done, n(k + 1))
                pool.wait_ge(x1_copied, n(k + 1))
                pool.wait_ge(zeros_out, 16 * E)
                pool.wait_ge(rows_out, 16 * (T * k + 1))
                pool.sem_inc(scatter_turn, 1)
                for t in range(T):
                    nc.gpsimd.indirect_dma_start(
                        dispatched, bass.IndirectOffsetOnAxis(ap=slot_no[:, t:t + 1], axis=0),
                        rows[:, t, :], None, bounds_check=E * CAP - 1, oob_is_err=False).then_inc(rows_out, 16)

            def last(k, rows):
                scatter_rows(k, rows)

            run_steps(pool, step, tail_start, tail, last)

            def finish(e, pair, y):
                pool.wait_ge(scaled_done, n(e + 1))
                pool.wait_ge(x1_in[y], 16 * (pair + 1))
                nc.gpsimd.tensor_tensor(res[y][:, :, :], res[y][:, :, :], got_x1[y][:, :, 0:D],
                                        ALU.add).then_inc(res_done, 1)
                pool.wait_ge(token_done, n(e + 1))
                pool.wait_ge(res_done, n(e + 1))
                pool.wait_ge(x1_out, 16 * NBLK)
                pool.wait_ge(res_out, 16 * (T * e + 1))
                pool.sem_inc(scatter_turn, 1)
                for t in range(T):
                    nc.gpsimd.indirect_dma_start(
                        out, bass.IndirectOffsetOnAxis(ap=token_at[y][:, t:t + 1], axis=0),
                        res[y][:, t, :], None, bounds_check=NBLK * BLK - 1, oob_is_err=False).then_inc(res_out, 16)

            def body(e, pair, y, prev, nxt):
                if prev:
                    finish(e - 1, pair if y else pair - 1, 1 - y)

            run_experts(pool, body, finish)

        @block.scalar
        def _(act):
            start_counts(act, xn_done, q_hi_done, h_scaled, h32_made, kv_hi_out, u_out, q_out, sq_out, rms_out,
                         gt_hi_out, x1_copied, h2t_out, prob_out, e_hi_out, f_hi_out, w_hi_out, factor0_out)
            act.wait_ge(res_out, 16)
            nc.scalar.activation(c_silu[:, :, :], c_raw[:, :, :], ACT.Silu).then_inc(c_ready, 1)
            act.wait_ge(w4_in, 16)
            for c in range(H):
                nc.scalar.activation(w4_hi[:, c, :], q_ring[:, c, :, :].rearrange("p h w -> p (h w)"),
                                     ACT.Copy).then_inc(w4_hi_done, 1)

            def normalise_first(i):
                act.wait_ge(rstd1_done, n(i + 1))
                act.wait_ge(h_turned, n(2 * i))
                for t in range(T):
                    ins = nc.scalar.activation(xn[:, t, :], xa[:, t, :], ACT.Identity, bias=bias1[:, t:t + 1],
                                               scale=rstd1[:, t:t + 1])
                ins.then_inc(xn_done, 1)

            def scale_half(h, c, i):
                return nc.scalar.activation(h[:, c, :], X[c][:, :], ACT.Identity,
                                            bias=shift1[:, c, bass.ds(i, 1)], scale=scale1[:, c, bass.ds(i, 1)])

            def scale_h(i):
                act.wait_ge(q_done, n(2 * i))
                act.wait_ge(h_lo0_done, n(i))
                act.wait_ge(h_lo1_done, n(i))
                act.wait_ge(mod_t_read, 2)
                for c in range(H):
                    act.wait_ge(h_turned, n(2 * i + c + 1))
                    scale_half(h_hi, c, i).then_inc(h_scaled, 1)
                for c in range(H):
                    scale_half(h32, c, i).then_inc(h32_made, 1)

            def q_high(j, r):
                act.wait_ge(att_done, n(2 * j))
                act.wait_ge(q_out, n(2 * j + 2))
                for c in range(H):
                    nc.scalar.activation(q_hi[:, c, :], q_ring[:, r, c, :], ACT.Copy).then_inc(q_hi_done, 1)

            def kv_high(i, t):
                act.wait_ge(kv_done, n(4 * i + t + 1))
                act.wait_ge(kv_summed, n(4 * i + t - 1))
                nc.scalar.activation(k_hi[t % 2][:, :], KV[t % 2][:, 0:D], ACT.Relu)
                nc.scalar.activation(v2[t % 2][:, :, 0:P], KV[t % 2][:, D:2 * D].rearrange("p (c w) -> p c w", c=H),
                                     ACT.Copy).then_inc(kv_hi_out, 1)

            def silu_u(i, r, pr):
                act.wait_ge(u_done, n(2 * i + pr + 1))
                nc.scalar.activation(u_ring[:, r, 2 * pr:2 * pr + 2, :].rearrange("p t d -> p (t d)"),
                                     UB[:, :], ACT.Silu).then_inc(u_out, 1)

            def copy_x1(k, rows, two):
                act.wait_ge(x1_done, n(2 * k + 2))
                if two:
                    act.wait_ge(h_turned, n(2 * NBLK))
                act.wait_ge(rows_out, rows_landed(k, two))
                act.wait_ge(zeros_out, 16 * E)
                nc.scalar.activation(rows[:, :, D:2 * D], x1[:, :, :], ACT.Copy).then_inc(x1_copied, 1)

            def keep_h2t(k):
                for c in range(H):
                    act.wait_ge(h2_turned, n(2 * k + c + 1))
                    act.wait_ge(logits_done, n(k))
                    nc.scalar.activation(h2t[:, c, :], X[c][:, :], ACT.Copy).then_inc(h2t_out, 1)

            def exp_logits(k):
                act.wait_ge(shifted_done, n(k + 1))
                act.wait_ge(slots_done, n(k))
                nc.scalar.activation(prob[:, :, :], below_top[:, :, :], ACT.Exp).then_inc(prob_out, 1)

            normalise_first(0)
            scale_h(0)

            def square(j, banks):
                for pr in range(2):
                    act.wait_ge(att_done, n(2 * j + pr + 1))
                    act.wait_ge(ssq_sum, n(j))
                    nc.scalar.activation(sq[:, 2 * pr:2 * pr + 2, :].rearrange("p t d -> p (t d)"),
                                         banks[pr][:, :], ACT.Square).then_inc(sq_out, 1)

            def root(j):
                act.wait_ge(ssq_done, n(j + 1))
                nc.scalar.activation(rms[:, :], ssq[:, :], ACT.Sqrt, scale=1.0 / HEAD).then_inc(rms_out, 1)

            def g_high(j):
                for c in range(H):
                    act.wait_ge(g_turned, n(2 * j + c + 1))
                    act.wait_ge(wo_done, n(2 * j))
                    nc.scalar.activation(gt_hi[:, c, :], X[c][:, :], ACT.Copy).then_inc(gt_hi_out, 1)

            def step(i, b, r, p2, p3, ahead):
                j, k = i - PER, i - PER - 1
                kv_high(i, 0)
                if ahead:
                    normalise_first(i + 1)
                if p2:
                    square(j, O)
                    q_high(j + 1, (r + 1) % PER)
                kv_high(i, 1)
                if p2:
                    act.wait_ge(gated, n(2 * j + 2))
                silu_u(i, r, 0)
                if p2:
                    root(j)
                kv_high(i, 2)
                if p3:
                    copy_x1(k, rows, False)
                kv_high(i, 3)
                if p3:
                    keep_h2t(k)
                keep_q(i, j, r, 0, p2)
                if p2:
                    g_high(j)
                if p3:
                    exp_logits(k)
                silu_u(i, r, 1)
                keep_q(i, j, r, 1, p2)
                if ahead:
                    scale_h(i + 1)
                if not p2 and closes_row(r):
                    q_high(0, 0)

            def tail_start(j):
                square(j, TAIL)
                q_high(j + 1, 1)
                root(j)
                g_high(j)

            def tail(j, r, rows, attends, splits):
                if attends:
                    square(j + 1, TAIL)
                copy_x1(j - 1, rows, True)
                if splits:
                    q_high(j + 2, r + 2)
                if attends:
                    root(j + 1)
                keep_h2t(j - 1)
                exp_logits(j - 1)
                if attends:
                    g_high(j + 1)

            def keep_q(i, j, r, c, p2):
                act.wait_ge(q_done, n(2 * i + c + 1))
                if p2:
                    act.wait_ge(q_lo_done, n(2 * j + 2))
                else:
                    act.wait_ge(w4_lo_done, 2)
                nc.scalar.activation(q_ring[:, r, c, :], KV[c][:, :], ACT.Relu).then_inc(q_out, 1)

            def last(k, rows):
                copy_x1(k, rows, True)
                keep_h2t(k)
                exp_logits(k)

            run_steps(act, step, tail_start, tail, last)

            def split_w(e, pair, y, piece):
                act.wait_ge(w_in[y], 16 * (pair + 1))
                act.wait_ge(hid_done if piece < 2 else y_part, n(NF * (e - 1)))
                part = slice(piece * EW // 4, (piece + 1) * EW // 4)
                nc.scalar.activation(w_hi[y][:, part], w_raw[y][:, part], ACT.Copy).then_inc(w_hi_out, 1)

            def rows_high(e, y, c):
                act.wait_ge(e_turned, n(2 * e + c + 1))
                act.wait_ge(hid_done, n(NF * (e - 1)))
                nc.scalar.activation(e_hi[y][:, c, :], X[1][:, :], ACT.Copy).then_inc(e_hi_out, 1)

            act.wait_ge(mods_in, 32 * NB)
            act.wait_ge(w_in[0], 16)
            for piece in range(4):
                part = slice(piece * EW // 4, (piece + 1) * EW // 4)
                nc.scalar.activation(w_hi[0][:, part], w_raw[0][:, part], ACT.Copy).then_inc(w_hi_out, 1)
            for c in range(H):
                act.wait_ge(e_turned, n(c + 1))
                nc.scalar.activation(e_hi[0][:, c, :], X[c][:, :], ACT.Copy).then_inc(e_hi_out, 1)

            def body(e, pair, y, prev, nxt):
                next_pair = pair + 1 if y else pair
                for f in range(NF):
                    act.wait_ge(hid_done, n(NF * e + f + 1))
                    act.wait_ge(y_part, n(chunk_freed(e, f)))
                    nc.scalar.activation(f_hi[f % 3][:, :], HID[f % 3][:, :], ACT.Relu).then_inc(f_hi_out, 1)
                    if nxt and f < 4:
                        split_w(e + 1, next_pair, 1 - y, f)
                    if f == 3:
                        act.wait_ge(scaled_done, n(e))
                        act.wait_ge(x1_in[y], 16 * (pair + 1))
                        for t in range(T):
                            ins = nc.scalar.activation(factor[:, t, :], gb_all[:, 0, :], ACT.Copy,
                                                       scale=got_x1[y][:, t, GATE1:GATE1 + 1])
                        ins.then_inc(factor0_out, 1)
                    if nxt and f in (4, 6):
                        rows_high(e + 1, 1 - y, (f - 4) // 2)

            run_experts(act, body, lambda e, pair, y: None)

        @block.vector
        def _(dve):
            start_counts(dve, stats1_done, mv1_done, var1_done, kv_lo_done, h_lo1_done, places_read,
                         att_kv, att_kv_step, wog_step, wog_done, gated, ssq_sum, ssq_done, rrms_done, g_done,
                         gt_lo_done, x1_done, stats2_done, mv2_done, var2_done, xc_done, h2_done,
                         route_step, shifted_done, chosen_done, slot_step, slots_done,
                         e_lo_done, f_lo_done, w_lo_done, factor_step, scaled_done, token_done)
            nc.vector.memset(exponent[:, :], -0.5).then_inc(consts_dve, 1)
            nc.vector.memset(ones[:, :], 1.0).then_inc(consts_dve, 1)
            nc.vector.memset(seen[:, :], 0.0).then_inc(consts_dve, 1)

            def norm_stats_first(i):
                dve.wait_ge(x_in, 16 * (i + 1))
                for t in range(T):
                    ins = nc.vector.bn_stats(stats1[:, t, :], xa[:, t, :])
                ins.then_inc(stats1_done, 1)
                dve.wait_ge(stats1_done, n(i + 1))
                dve.sem_inc(stats1_seen, 1)
                for t in range(T):
                    ins = nc.vector.bn_aggr(mv1[:, t, :], stats1[:, t, :])
                ins.then_inc(mv1_done, 1)
                dve.wait_ge(mv1_done, n(i + 1))
                nc.vector.tensor_scalar(neg_mean1[:, :], mv1[:, :, 0], -1.0, None, ALU.mult)
                nc.vector.tensor_scalar(var1[:, :], mv1[:, :, 1], LN_EPS, None, ALU.add).then_inc(var1_done, 1)

            norm_stats_first(0)
            for c in range(H):
                dve.wait_ge(w4_hi_done, c + 1)
                nc.vector.tensor_tensor(w4_lo[:, c, :], q_ring[:, c, :, :].rearrange("p h w -> p (h w)"),
                                        w4_hi[:, c, :], ALU.subtract).then_inc(w4_lo_done, 1)
            dve.wait_ge(mod_t_done, 1)
            by_row = UB[:, 0:2 * H * NB].rearrange("p (a c b) -> p a c b", a=2, c=H)
            nc.vector.tensor_copy(shift1[:, :, :].rearrange("p c (b r) -> p c b r", r=PER),
                                  by_row[:, 0, :, :].unsqueeze(3).to_broadcast([P, H, NB, PER])).then_inc(mod_t_read, 1)
            nc.vector.tensor_scalar(scale1[:, :, :].rearrange("p c (b r) -> p c b r", r=PER),
                                    by_row[:, 1, :, :].unsqueeze(3).to_broadcast([P, H, NB, PER]),
                                    1.0, None, ALU.add).then_inc(mod_t_read, 1)
            norm_stats_first(1)
            def kv_low(i, t):
                dve.wait_ge(kv_hi_out, n(4 * i + t + 1))
                nc.vector.scalar_tensor_tensor(out=k_lo[t % 2][:, :], in0=KV[t % 2][:, 0:D], scalar=0.0,
                                               in1=k_hi[t % 2][:, :], op0=ALU.max, op1=ALU.subtract)
                nc.vector.tensor_tensor(v2[t % 2][:, :, P:2 * P],
                                        KV[t % 2][:, D:2 * D].rearrange("p (c w) -> p c w", c=H),
                                        v2[t % 2][:, :, 0:P], ALU.subtract).then_inc(kv_lo_done, 1)

            def finish_kv(b):
                dve.wait_ge(kv_summed, n(4 * PER * (b + 1)))
                dve.wait_ge(consts_pool, 8)
                both = KVSUM[:, :].rearrange("p (c a w) -> p c a w", c=H, a=2)
                mask = head_mask[:, :].unsqueeze(1).to_broadcast([P, H, P])
                dve.wait_ge(att_done, n(2 * PER * b))
                nc.vector.tensor_tensor(kv_a[:, :, :], both[:, :, 0, :], mask, ALU.mult)
                nc.vector.tensor_tensor(kv_b[:, :, :], both[:, :, 1, :], mask, ALU.mult).then_inc(att_kv_step, 1)
                dve.wait_ge(att_kv_step, n(3 * b + 1))
                nc.vector.tensor_tensor(kv_a[:, :, :], kv_a[:, :, :], kv_b[:, :, :], ALU.add).then_inc(att_kv_step, 1)
                dve.wait_ge(att_kv_step, n(3 * b + 2))
                nc.vector.tensor_copy(kv_hi[:, :, :], kv_a[:, :, :]).then_inc(att_kv_step, 1)
                dve.wait_ge(att_kv_step, n(3 * b + 3))
                nc.vector.tensor_tensor(kv_lo[:, :, :], kv_a[:, :, :], kv_hi[:, :, :],
                                        ALU.subtract).then_inc(att_kv, 1)

            def output_weights(b):
                dve.wait_ge(wo_done, n(2 * PER * b))
                dve.wait_ge(mods_in, 32 * NB)
                ga = mods[:, b, GA, :].unsqueeze(1).to_broadcast([P, H, D])
                nc.vector.tensor_tensor(wog, wo[:, :, :], ga, ALU.mult).then_inc(wog_step, 1)
                dve.wait_ge(wog_step, n(2 * b + 1))
                nc.vector.tensor_copy(wog_hi[:, :, :], wog).then_inc(wog_step, 1)
                dve.wait_ge(wog_step, n(2 * b + 2))
                nc.vector.tensor_tensor(wog_lo[:, :, :], wog, wog_hi[:, :, :],
                                        ALU.subtract).then_inc(wog_done, 1)

            def make_mods():
                for half in range(2):
                    dve.wait_ge(mod_done, half + 1)
                    halves = O[half][0:NB, 0:D], O[half][0:NB, D:2 * D]
                    g_psum, s_psum = halves[half], halves[1 - half]
                    nc.vector.tensor_scalar(g_size, g_psum, 0.25, None, ALU.max)
                    nc.vector.tensor_scalar(g_sign, g_psum, 0.0, 2.0, ALU.is_ge, ALU.mult).then_inc(g_guard, 1)
                    nc.vector.tensor_scalar(mod_rows[:, 1 + half, :], s_psum, 1.0 if half else 0.0, None, ALU.add)
                    dve.wait_ge(g_guard, 3 * half + 1)
                    nc.vector.scalar_tensor_tensor(out=g_size, in0=g_psum, scalar=-1.0, in1=g_size,
                                                   op0=ALU.mult, op1=ALU.max).then_inc(g_guard, 1)
                    dve.wait_ge(g_guard, 3 * half + 2)
                    nc.vector.scalar_tensor_tensor(out=mod_rows[:, 3 * half, :], in0=g_sign, scalar=-1.0, in1=g_size,
                                                   op0=ALU.add, op1=ALU.mult).then_inc(g_guard, 1)
                    dve.wait_ge(g_guard, 3 * half + 3)

            def stats_second(k):
                dve.wait_ge(x1_done, n(2 * k + 2))
                for t in range(T):
                    ins = nc.vector.bn_stats(stats2[:, t, :], x1[:, t, :])
                ins.then_inc(stats2_done, 1)
                dve.wait_ge(stats2_done, n(k + 1))
                dve.sem_inc(stats2_seen, 1)
                for t in range(T):
                    ins = nc.vector.bn_aggr(mv2[:, t, :], stats2[:, t, :])
                ins.then_inc(mv2_done, 1)
                dve.wait_ge(mv2_done, n(k + 1))
                nc.vector.tensor_scalar(var2[:, :], mv2[:, :, 1], LN_EPS, None, ALU.add).then_inc(var2_done, 1)

            def centre(k):
                for t in range(T):
                    ins = nc.vector.scalar_tensor_tensor(out=xc[:, t, :], in0=x1[:, t, :], scalar=mv2[:, t, 0:1],
                                                         in1=mods[:, row_of(k), CB, :], op0=ALU.subtract, op1=ALU.mult)
                ins.then_inc(xc_done, 1)

            def row_of(k):
                return k // PER

            def modulate(k, rows, two):
                dve.wait_ge(rstd2_done, n(k + 1))
                dve.wait_ge(xc_done, n(k + 1))
                if two:
                    dve.wait_ge(h_turned, n(2 * NBLK))
                dve.wait_ge(rows_out, rows_landed(k, two))
                dve.wait_ge(zeros_out, 16 * E)
                for t in range(T):
                    ins = nc.vector.scalar_tensor_tensor(out=rows[:, t, 0:D], in0=xc[:, t, :], scalar=rstd2[:, t:t + 1],
                                                         in1=mods[:, row_of(k), SB, :], op0=ALU.mult, op1=ALU.add)
                ins.then_inc(h2_done, 1)

            ROUTE = 9

            def wide(ap):
                return ap.unsqueeze(2).to_broadcast([P, T, E])

            def shift_logits(k, bank):
                dve.wait_ge(logits_done, n(k + 1))
                logits = bank[:, 0:T * E].rearrange("p (t e) -> p t e", t=T)
                nc.vector.tensor_reduce(top[:, :], logits, AX.X, ALU.max).then_inc(route_step, 1)
                dve.wait_ge(route_step, n(ROUTE * k + 1))
                nc.vector.tensor_tensor(below_top[:, :, :], logits, wide(top[:, :]), ALU.subtract).then_inc(shifted_done, 1)

            def choose(k, rows):
                dve.wait_ge(prob_out, n(k + 1))
                nc.vector.tensor_reduce(ptop[:, :], prob[:, :, :], AX.X, ALU.max).then_inc(route_step, 1)
                nc.vector.tensor_reduce(psum_[:, :], prob[:, :, :], AX.X, ALU.add).then_inc(route_step, 1)
                dve.wait_ge(route_step, n(ROUTE * k + 2))
                nc.vector.tensor_tensor(is_top[:, :, :], prob[:, :, :], wide(ptop[:, :]),
                                        ALU.is_equal).then_inc(route_step, 1)
                dve.wait_ge(route_step, n(ROUTE * k + 4))
                nc.vector.tensor_tensor(ranked[:, :, :], is_top[:, :, :],
                                        rank[:, :].unsqueeze(1).to_broadcast([P, T, E]), ALU.mult).then_inc(route_step, 1)
                dve.wait_ge(route_step, n(ROUTE * k + 5))
                nc.vector.tensor_reduce(best[:, :], ranked[:, :, :], AX.X, ALU.max).then_inc(route_step, 1)
                nc.vector.reciprocal(rsum[:, :], psum_[:, :])
                dve.wait_ge(route_step, n(ROUTE * k + 6))
                nc.vector.tensor_tensor(chosen[:, :, :], ranked[:, :, :], wide(best[:, :]),
                                        ALU.is_equal).then_inc(chosen_done, 1)
                dve.wait_ge(chosen_done, n(k + 1))
                nc.vector.tensor_tensor(gate[:, :], ptop[:, :], rsum[:, :], ALU.mult).then_inc(route_step, 1)
                nc.vector.tensor_copy(rows[:, :, TOKEN], token_no[:, :])
                dve.wait_ge(route_step, n(ROUTE * k + 7))
                nc.vector.tensor_tensor(rows[:, :, GATE0:GATE0 + NB],
                                        row_onehot[:, row_of(k), :].unsqueeze(1).to_broadcast([P, T, NB]),
                                        gate[:, :].unsqueeze(2).to_broadcast([P, T, NB]), ALU.mult)
                nc.vector.tensor_scalar(first_slot[:, :], best[:, :], -float(CAP), float(E * CAP), ALU.mult, ALU.add)
                nc.vector.tensor_reduce(newly[:, :], chosen[:, :, :].rearrange("p t e -> p e t"),
                                        AX.X, ALU.add).then_inc(route_step, 1)
                nc.vector.tensor_scalar(token_no[:, :], token_no[:, :], float(BLK), None, ALU.add)

            def number_slots(k, bank):
                dve.wait_ge(places_done, n(k + 1))
                places = bank[:, 0:T * E].rearrange("p (t e) -> p t e", t=T)
                nc.vector.tensor_tensor(picked[:, :, :], places, chosen[:, :, :], ALU.mult).then_inc(places_read, 1)
                dve.wait_ge(route_step, n(ROUTE * k + 8))
                nc.vector.tensor_tensor(seen[:, :], seen[:, :], newly[:, :], ALU.add)
                dve.wait_ge(places_read, n(k + 1))
                nc.vector.tensor_reduce(place[:, :], picked[:, :, :], AX.X, ALU.add).then_inc(route_step, 1)
                dve.wait_ge(route_step, n(ROUTE * k + 9))
                nc.vector.tensor_scalar(over[:, :], place[:, :], float(CAP), FAR, ALU.is_ge, ALU.mult)
                nc.vector.tensor_tensor(slot[:, :], place[:, :], first_slot[:, :], ALU.add).then_inc(slot_step, 1)
                dve.wait_ge(slot_step, n(k + 1))
                nc.vector.tensor_tensor(slot_no[:, :], slot[:, :], over[:, :], ALU.add).then_inc(slots_done, 1)

            def gate_attention(j, r, banks):
                for pr in range(2):
                    dve.wait_ge(att_done, n(2 * j + pr + 1))
                    dve.wait_ge(g_turned, n(2 * j))
                    dve.wait_ge(u_out, n(2 * j + pr + 1))
                    dve.wait_ge(sq_out, n(2 * j + pr + 1))
                    nc.vector.tensor_tensor(g[:, 2 * pr:2 * pr + 2, :].rearrange("p t d -> p (t d)"), banks[pr][:, :],
                                            u_ring[:, r, 2 * pr:2 * pr + 2, :].rearrange("p t d -> p (t d)"),
                                            ALU.mult).then_inc(gated, 1)
                nc.vector.tensor_reduce(ssq[:, :], sq[:, :, :].rearrange("p t (h w) -> p (t h) w", w=HEAD),
                                        AX.X, ALU.add).then_inc(ssq_sum, 1)
                dve.wait_ge(ssq_sum, n(j + 1))
                nc.vector.tensor_scalar(ssq[:, :], ssq[:, :], HEAD * RMS_FLOOR ** 2, None,
                                        ALU.max).then_inc(ssq_done, 1)

            def norm_heads(j):
                dve.wait_ge(rms_out, n(j + 1))
                nc.vector.reciprocal(rrms[:, :], rms[:, :]).then_inc(rrms_done, 1)
                dve.wait_ge(rrms_done, n(j + 1))
                heads = g[:, :, :].rearrange("p t (h w) -> p (t h) w", w=HEAD)
                nc.vector.tensor_tensor(heads, heads, rrms[:, :].unsqueeze(2).to_broadcast([P, T * NH, HEAD]),
                                        ALU.mult).then_inc(g_done, 1)

            def g_low(j):
                for c in range(H):
                    dve.wait_ge(gt_hi_out, n(2 * j + c + 1))
                    nc.vector.tensor_tensor(gt_lo[:, c, :], X[c][:, :], gt_hi[:, c, :],
                                            ALU.subtract).then_inc(gt_lo_done, 1)

            def low_part(i):
                dve.wait_ge(h32_made, n(2 * i + 2))
                nc.vector.tensor_tensor(h_lo[:, 1, :], h32[:, 1, :], h_hi[:, 1, :],
                                        ALU.subtract).then_inc(h_lo1_done, 1)

            def residual(j, pr, earlier):
                dve.wait_ge(wo_done, n(2 * j + pr + 1))
                dve.wait_ge(xr_in, 16 * (j + 1))
                if earlier:
                    dve.wait_ge(x1_out, 16 * j)
                    dve.wait_ge(x1_copied, n(j))
                    dve.wait_ge(xc_done, n(j))
                nc.vector.tensor_tensor(x1[:, 2 * pr:2 * pr + 2, :].rearrange("p t d -> p (t d)"), O[pr][:, :],
                                        xr[:, 2 * pr:2 * pr + 2, :].rearrange("p t d -> p (t d)"),
                                        ALU.add).then_inc(x1_done, 1)

            low_part(0)

            def step(i, b, r, p2, p3, ahead):
                j, k = i - PER, i - PER - 1
                if p3:
                    stats_second(k)
                kv_low(i, 0)
                if p3:
                    centre(k)
                if p2:
                    gate_attention(j, r, O)
                kv_low(i, 1)
                if p3:
                    modulate(k, rows, False)
                kv_low(i, 2)
                if p2:
                    norm_heads(j)
                kv_low(i, 3)
                if p2 and opens_row(r):
                    output_weights(b - 1)
                if ahead == 2:
                    norm_stats_first(i + 2)
                if p2:
                    g_low(j)
                if p3:
                    shift_logits(k, O[0])
                if first_step(i):
                    make_mods()
                if p3:
                    choose(k, rows)
                if closes_row(r):
                    finish_kv(b)
                if p3:
                    number_slots(k, O[1])
                if p2:
                    residual(j, 0, p3)
                if ahead:
                    low_part(i + 1)
                if p2:
                    residual(j, 1, p3)

            def tail_start(j):
                gate_attention(j, 0, TAIL)
                norm_heads(j)
                stats_second(j - 1)
                output_weights(NB - 1)
                g_low(j)

            def tail(j, r, rows, attends, splits):
                k = j - 1
                dve.wait_ge(wog_done, n(NB))
                centre(k)
                if attends:
                    gate_attention(j + 1, r + 1, TAIL)
                modulate(k, rows, True)
                residual(j, 0, True)
                residual(j, 1, True)
                if attends:
                    norm_heads(j + 1)
                stats_second(j)
                if not attends:
                    centre(j)
                    modulate(j, rows_b, True)
                shift_logits(k, KV[0])
                choose(k, rows)
                if attends:
                    g_low(j + 1)
                dve.wait_ge(rows_out, rows_landed(k, False))
                number_slots(k, KV[1])

            def last(k, rows):
                shift_logits(k, KV[0])
                choose(k, rows)
                dve.wait_ge(rows_out, rows_landed(k, False))
                number_slots(k, KV[1])

            run_steps(dve, step, tail_start, tail, last)

            def split_w(e, y, piece):
                dve.wait_ge(w_hi_out, n(4 * e + piece + 1))
                part = slice(piece * EW // 4, (piece + 1) * EW // 4)
                nc.vector.tensor_tensor(w_lo[y][:, part], w_raw[y][:, part], w_hi[y][:, part],
                                        ALU.subtract).then_inc(w_lo_done, 1)

            def rows_low(e, y, c, bank):
                dve.wait_ge(e_hi_out, n(2 * e + c + 1))
                nc.vector.tensor_tensor(e_lo[y][:, c, :], bank[:, :], e_hi[y][:, c, :],
                                        ALU.subtract).then_inc(e_lo_done, 1)

            def results_landed(e):
                if not (isinstance(e, int) and e < 2):
                    dve.wait_ge(res_out, 16 * (T * (e - 1) + 1))

            def scale_y(e, y):
                dve.wait_ge(y_part, n(NF * (e + 1)))
                dve.wait_ge(factor_step, n((NB - 1) * (e + 1)))
                results_landed(e)
                for pr in range(2):
                    ins = nc.vector.tensor_tensor(res[y][:, 2 * pr:2 * pr + 2, :].rearrange("p t d -> p (t d)"),
                                                  Y[y][pr][:, :],
                                                  factor[:, 2 * pr:2 * pr + 2, :].rearrange("p t d -> p (t d)"), ALU.mult)
                ins.then_inc(scaled_done, 1)

            for piece in range(4):
                split_w(0, 0, piece)
            for c in range(H):
                rows_low(0, 0, c, X[c])

            def body(e, pair, y, prev, nxt):
                for f in range(NF):
                    dve.wait_ge(f_hi_out, n(NF * e + f + 1))
                    nc.vector.scalar_tensor_tensor(out=f_lo[f % 3][:, :], in0=HID[f % 3][:, :], scalar=0.0,
                                                   in1=f_hi[f % 3][:, :], op0=ALU.max,
                                                   op1=ALU.subtract).then_inc(f_lo_done, 1)
                    if nxt and f < 4:
                        split_w(e + 1, 1 - y, f)
                    if prev and f == 2:
                        scale_y(e - 1, 1 - y)
                    if f == 3:
                        dve.wait_ge(x1_in[y], 16 * (pair + 1))
                        results_landed(e)
                        nc.vector.tensor_scalar(token_at[y][:, :], got_x1[y][:, :, TOKEN1], FAR, None,
                                                ALU.add).then_inc(token_done, 1)
                    if nxt and f in (4, 6):
                        rows_low(e + 1, 1 - y, (f - 4) // 2, X[1])
                    if 4 <= f < 4 + NB - 1:
                        row = f - 3
                        dve.wait_ge(factor0_out, n(e + 1))
                        dve.wait_ge(factor_step, n((NB - 1) * e + row - 1))
                        for t in range(T):
                            ins = nc.vector.scalar_tensor_tensor(
                                out=factor[:, t, :], in0=gb_all[:, row, :],
                                scalar=got_x1[y][:, t, GATE1 + row:GATE1 + row + 1],
                                in1=factor[:, t, :], op0=ALU.mult, op1=ALU.add)
                        ins.then_inc(factor_step, 1)
            run_experts(dve, body, lambda e, pair, y: scale_y(e, y))

        @block.tensor
        def _(pe):
            start_counts(pe, h_turned, kv_done, u_done, q_done, kv_summed, att_done, g_turned, wo_done,
                         h2_turned, logits_done, places_done, e_turned, hid_done, y_part)

            def tile(t):
                return slice(t * P, (t + 1) * P)

            def turn(src, done):
                for c in range(H):
                    for t in range(T):
                        ins = nc.tensor.transpose(X[c][:, tile(t)], src[:, t, c * P:(c + 1) * P], ident[:, :])
                    ins.then_inc(done, 1)

            pe.wait_ge(c_ready, 1)
            pe.wait_ge(mod1_in, 16)
            wm = w_raw[0][:, 0:H * 6 * D].rearrange("p (k w) -> p k w", k=H)
            for a in range(2):
                for c in range(H):
                    at = (a * H + c) * NB
                    for kk in range(H):
                        ins = nc.tensor.matmul(UB[:, at:at + NB], wm[:, kk, a * D + c * P:a * D + (c + 1) * P],
                                               c_silu[:, kk, :], start=(kk == 0), stop=(kk == H - 1))
            ins.then_inc(mod_t_done, 1)

            def mod_by_row():
                pe.wait_ge(weights_in, 32)
                for half in range(2):
                    for kk in range(H):
                        ins = nc.tensor.matmul(O[half][0:NB, :], c_silu[:, kk, :],
                                               wm[:, kk, 2 * D * (half + 1):2 * D * (half + 2)],
                                               start=(kk == 0), stop=(kk == H - 1))
                    ins.then_inc(mod_done, 1)

            def turn_xn(i, j):
                pe.wait_ge(xn_done, n(i + 1))
                if j is None:
                    pe.wait_ge(h32_made, n(2 * i))
                else:
                    pe.wait_ge(gt_lo_done, n(2 * j + 2))
                turn(xn, h_turned)

            pe.wait_ge(consts_pool, 1)
            turn_xn(0, None)
            mod_by_row()

            def project_tile(i, t):
                if t == 0:
                    pe.wait_ge(q_out, n(2 * i))
                elif t >= 2:
                    pe.wait_ge(kv_lo_done, n(4 * i + t - 1))
                products = [(KV[t % 2][:, :], 0, 2 * D), (UB[:, (t % 2) * D:(t % 2 + 1) * D], 2 * D, 3 * D)]

                def multiply(which, parts, halves, opens, closes):
                    dst, lo, hi = products[which]
                    steps = [(a, w, c) for a, w in parts for c in halves]
                    for m, (a, w, c) in enumerate(steps):
                        ins = nc.tensor.matmul(dst, a[:, c, tile(t)], w[:, c, lo:hi], start=opens and m == 0,
                                               stop=closes and m == len(steps) - 1, skip_group_check=True)
                    return ins

                def u_bank_free():
                    if t % 2 == 0:
                        pe.wait_ge(u_out, n(2 * i + t // 2))

                high, low = [(h_hi, w4_hi), (h_hi, w4_lo)], [(h_lo, w4_hi)]
                if t == 0:
                    for c in range(H):
                        pe.wait_ge(h_scaled, n(2 * i + c + 1))
                        multiply(0, high, [c], c == 0, False)
                        if c == 0:
                            u_bank_free()
                        multiply(1, high, [c], c == 0, False)
                    pe.wait_ge(h_lo0_done, n(i + 1))
                    pe.wait_ge(h_lo1_done, n(i + 1))
                    multiply(0, low, range(H), False, True).then_inc(kv_done, 1)
                    multiply(1, low, range(H), False, True)
                else:
                    multiply(0, high + low, range(H), True, True).then_inc(kv_done, 1)
                    u_bank_free()
                    ins = multiply(1, high + low, range(H), True, True)
                    if t % 2:
                        ins.then_inc(u_done, 1)

            def sum_kv(i, b, r, t):
                pe.wait_ge(kv_lo_done, n(4 * i + t + 1))
                opens = opens_row(r) and t == 0
                if opens:
                    pe.wait_ge(att_kv, n(b))
                ends = False
                for c in range(H):
                    nc.tensor.matmul(KVSUM[:, c * 2 * P:(c + 1) * 2 * P], k_hi[t % 2][:, c * P:(c + 1) * P],
                                     v2[t % 2][:, c, :], start=opens and c == 0, stop=ends, skip_group_check=True)
                    ins = nc.tensor.matmul(KVSUM[:, c * 2 * P:c * 2 * P + P], k_lo[t % 2][:, c * P:(c + 1) * P],
                                           v2[t % 2][:, c, 0:P], start=False, stop=ends, skip_group_check=True)
                ins.then_inc(kv_summed, 1)

            def project_q(i, c):
                pe.wait_ge(kv_lo_done, n(4 * i + 3 + c))
                out_ch = slice(3 * D + c * P, 3 * D + (c + 1) * P)
                m = 0
                for a, w in ((h_hi, w4_hi), (h_hi, w4_lo), (h_lo, w4_hi)):
                    for kk in range(H):
                        ins = nc.tensor.matmul(KV[c][:, :], w[:, kk, out_ch], a[:, kk, :],
                                               start=(m == 0), stop=(m == 3 * H - 1))
                        m += 1
                ins.then_inc(q_done, 1)

            def attend(j, bj, banks):
                pe.wait_ge(att_kv, n(bj + 1))
                pe.wait_ge(q_lo_done, n(2 * j + 2))
                for pr in range(2):
                    if banks is O:
                        pe.wait_ge(x1_done, n(2 * j - 1 + pr))
                    else:
                        pe.wait_ge(u_out, n(2 * NBLK))
                        pe.wait_ge(gated, n(2 * j))
                    for t in (2 * pr, 2 * pr + 1):
                        for c in range(H):
                            dst = banks[pr][:, (t % 2) * D + c * P:(t % 2) * D + (c + 1) * P]
                            nc.tensor.matmul(dst, q_hi[:, c, tile(t)], kv_hi[:, c, :], start=True, stop=False)
                            nc.tensor.matmul(dst, q_hi[:, c, tile(t)], kv_lo[:, c, :], start=False, stop=False)
                            ins = nc.tensor.matmul(dst, q_lo[:, c, tile(t)], kv_hi[:, c, :], start=False, stop=True)
                    ins.then_inc(att_done, 1)

            def project_out(j, bj, pr):
                pe.wait_ge(wog_done, n(bj + 1))
                pe.wait_ge(gt_lo_done, n(2 * j + 2))
                for t in (2 * pr, 2 * pr + 1):
                    m = 0
                    for a, w in ((gt_hi, wog_hi), (gt_hi, wog_lo), (gt_lo, wog_hi)):
                        for c in range(H):
                            ins = nc.tensor.matmul(O[pr][:, (t % 2) * D:(t % 2 + 1) * D], a[:, c, tile(t)],
                                                   w[:, c, :], start=(m == 0), stop=(m == 3 * H - 1))
                            m += 1
                ins.then_inc(wo_done, 1)

            def turn_h2(k, rows):
                pe.wait_ge(h2_done, n(k + 1))
                turn(rows, h2_turned)

            def logits(k, j, bank):
                pe.wait_ge(rows_out, 16)
                pe.wait_ge(h2t_out, n(2 * k + 2))
                if j is not None:
                    pe.wait_ge(gated, n(2 * j + 1))
                else:
                    pe.wait_ge(q_out, n(2 * NBLK))
                for t in range(T):
                    for c in range(H):
                        ins = nc.tensor.matmul(bank[:, t * E:(t + 1) * E], h2t[:, c, tile(t)], wg[:, c, :],
                                               start=(c == 0), stop=(c == H - 1))
                ins.then_inc(logits_done, 1)

            def count_places(k, bank):
                pe.wait_ge(chosen_done, n(k + 1))
                places = bank[:, 0:T * E].rearrange("p (t e) -> p t e", t=T)
                nc.tensor.matmul(places, ones[:, :], seen[:, :].unsqueeze(1).to_broadcast([P, T, E]),
                                 start=True, stop=False, skip_group_check=True)
                for s in range(T):
                    ins = nc.tensor.matmul(places[:, 0:s + 1, :], before[:, :],
                                           chosen[:, s, :].unsqueeze(1).to_broadcast([P, s + 1, E]),
                                           start=False, stop=s == T - 1, skip_group_check=True)
                    if s < T - 1:
                        nc.tensor.matmul(places[:, s + 1:T, :], up_to[:, :],
                                         chosen[:, s, :].unsqueeze(1).to_broadcast([P, T - 1 - s, E]),
                                         start=False, stop=False, skip_group_check=True)
                ins.then_inc(places_done, 1)

            def step(i, b, r, p2, p3, ahead):
                j, k = i - PER, i - PER - 1
                project_tile(i, 0)
                if p2:
                    attend(j, b - 1, O)
                project_tile(i, 1)
                sum_kv(i, b, r, 0)
                project_tile(i, 2)
                sum_kv(i, b, r, 1)
                project_tile(i, 3)
                sum_kv(i, b, r, 2)
                if p3:
                    pe.wait_ge(h32_made, n(2 * i + 2))
                    turn_h2(k, rows)
                project_q(i, 0)
                if p2:
                    pe.wait_ge(g_done, n(j + 1))
                    if p3:
                        pe.wait_ge(h2t_out, n(2 * k + 2))
                    else:
                        pe.wait_ge(h32_made, n(2 * i + 2))
                    turn(g, g_turned)
                if p3:
                    logits(k, j, O[0])
                sum_kv(i, b, r, 3)
                project_q(i, 1)
                if ahead:
                    turn_xn(i + 1, j if p2 else None)
                if p3:
                    count_places(k, O[1])
                    pe.wait_ge(shifted_done, n(k + 1))
                if p2:
                    project_out(j, b - 1, 0)
                if p3:
                    pe.wait_ge(places_read, n(k + 1))
                if p2:
                    project_out(j, b - 1, 1)

            def turn_g(j):
                pe.wait_ge(g_done, n(j + 1))
                pe.wait_ge(gt_lo_done, n(2 * j))
                pe.wait_ge(h2t_out, n(2 * (j - 1)))
                turn(g, g_turned)

            def tail_start(j):
                attend(j, NB - 1, TAIL)
                turn_g(j)

            def tail(j, r, rows, attends, splits):
                k = j - 1
                if attends:
                    attend(j + 1, NB - 1, TAIL)
                for pr in range(2):
                    pe.wait_ge(x1_done, n(2 * j - 1 + pr))
                    project_out(j, NB - 1, pr)
                pe.wait_ge(gt_lo_done, n(2 * j + 2))
                turn_h2(k, rows)
                logits(k, None, KV[0])
                if attends:
                    turn_g(j + 1)
                else:
                    pe.wait_ge(h2t_out, n(2 * k + 2))
                    turn_h2(j, rows_b)
                count_places(k, KV[1])

            def last(k, rows):
                logits(k, None, KV[0])
                count_places(k, KV[1])

            run_steps(pe, step, tail_start, tail, last)

            def turn_rows(e, pair, y, c, bank):
                pe.wait_ge(h_in[y], 16 * (pair + 1))
                if not (isinstance(e, int) and e == 0):
                    pe.wait_ge(e_lo_done, n(2 * e + c))
                for t in range(T):
                    ins = nc.tensor.transpose(bank[:, tile(t)], got_h[y][:, t, c * P:(c + 1) * P], ident[:, :])
                ins.then_inc(e_turned, 1)

            def hidden(e, y, f):
                pe.wait_ge(f_lo_done, n(chunk_freed(e, f)))
                m = 0
                for w, a in ((w_hi, e_hi), (w_lo, e_hi), (w_hi, e_lo)):
                    w1 = w[y][:, 0:H * F].rearrange("p (c f) -> p c f", c=H)
                    for c in range(H):
                        ins = nc.tensor.matmul(HID[f % 3][:, :], w1[:, c, f * P:(f + 1) * P], a[y][:, c, :],
                                               start=(m == 0), stop=(m == 3 * H - 1))
                        m += 1
                ins.then_inc(hid_done, 1)

            def partial_y(e, y, f):
                pe.wait_ge(f_lo_done, n(NF * e + f + 1))
                if f == 0:
                    pe.wait_ge(w_lo_done, n(4 * e + 4))
                    pe.wait_ge(scaled_done, n(e - 1))
                for t in range(T):
                    dst = Y[y][t // 2][:, (t % 2) * D:(t % 2 + 1) * D]
                    m = 0
                    for a, w in ((f_hi, w_hi), (f_hi, w_lo), (f_lo, w_hi)):
                        w2 = w[y][:, H * F:2 * H * F].rearrange("p (f d) -> p f d", f=NF)
                        ins = nc.tensor.matmul(dst, a[f % 3][:, tile(t)], w2[:, f, :],
                                               start=(f == 0 and m == 0 and t % 2 == 0),
                                               stop=(f == NF - 1 and m == 2), skip_group_check=True)
                        m += 1
                ins.then_inc(y_part, 1)

            for c in range(H):
                turn_rows(0, 0, 0, c, X[c])

            def body(e, pair, y, prev, nxt):
                pe.wait_ge(e_lo_done, n(2 * e + 2))
                pe.wait_ge(w_lo_done, n(4 * e + 2))
                for f in range(NF):
                    hidden(e, y, f)
                    if f >= 2:
                        partial_y(e, y, f - 2)
                    elif prev:
                        partial_y(e - 1, 1 - y, NF - 2 + f)
                    if nxt and f in (3, 5):
                        turn_rows(e + 1, pair + 1 if y else pair, 1 - y, (f - 3) // 2, X[1])

            def last_shares(e, pair, y):
                partial_y(e, y, NF - 2)
                partial_y(e, y, NF - 1)

            run_experts(pe, body, last_shares)


def kernel(L0_attn_x, L0_attn_Wq, L0_attn_Wk, L0_attn_Wv, L0_attn_Wu, L0_attn_Wo, L0_ffn_Wg, L0_ffn_w1,
           L0_ffn_w2, L0_c, L0_wmod):
    import numpy as np
    import concourse.bacc as bacc
    from concourse.bass_utils import run_bass_kernel_spmd

    def halves(w):
        w = np.asarray(w)
        return np.ascontiguousarray(w.reshape(-1, P, w.shape[1]).transpose(1, 0, 2))

    x = np.ascontiguousarray(L0_attn_x)
    b, l, d = x.shape
    experts, _, hidden = L0_ffn_w1.shape
    w4 = np.concatenate([np.asarray(w).T for w in (L0_attn_Wk, L0_attn_Wv, L0_attn_Wu, L0_attn_Wq)], axis=1)
    w1 = np.asarray(L0_ffn_w1).reshape(experts, -1, P, hidden).transpose(0, 2, 1, 3).reshape(experts, P, -1)
    w2 = np.asarray(L0_ffn_w2).reshape(experts, -1, P, d).transpose(0, 2, 1, 3).reshape(experts, P, -1)
    arrays = {
        "x_dram": x.reshape(-1, P, 4 * d),
        "w_kvuq_dram": halves(w4),
        "w_o_dram": halves(np.asarray(L0_attn_Wo).T),
        "w_gate_dram": halves(L0_ffn_Wg),
        "w_experts_dram": np.ascontiguousarray(np.concatenate([w1, w2], axis=2)),
        "c_t_dram": halves(np.asarray(L0_c).T),
        "w_mod_dram": halves(L0_wmod),
    }
    nc = bacc.Bacc("TRN2", target_bir_lowering=False, num_devices=1)
    args = [nc.dram_tensor(name, a.shape, mybir.dt.from_np(a.dtype), kind="ExternalInput").ap()
            for name, a in arrays.items()]
    out = nc.dram_tensor("out_dram", (b * l, d), F32, kind="ExternalOutput").ap()
    adaln_block_kernel(nc, *args, out)
    result = run_bass_kernel_spmd(nc, [arrays], core_ids=[0]).results[0]["out_dram"]
    return result.reshape(b, l, d)
```
